# Optimizing a Trainium2 kernel written in Bass

```python
import numpy as np
import jax
import jax.numpy as jnp

def _softmax(x, axis=-1):
    return jax.nn.softmax(x, axis=axis)

def _gelu(x):
    return jax.nn.gelu(x, approximate=True)

def _silu(x):
    return jax.nn.silu(x)

def _sigmoid(x):
    return jax.nn.sigmoid(x)

def _layernorm(x, axis=-1, eps=1e-05):
    m = jnp.mean(x, axis=axis, keepdims=True)
    v = jnp.var(x, axis=axis, keepdims=True)
    return (x - m) / jnp.sqrt(v + eps)

def _scatter_add(tgt, idx, src, axis=0):
    return tgt.at[idx].add(src)

def _segment_sum(src, seg, n):
    return jax.ops.segment_sum(src, seg, n)
kernel_name = 'mk_perceiver_d1_seqx_r8_75bda9'

def setup_inputs(seed: int=0):
    np.random.seed(seed)
    _w = jnp.asarray

    def _rec_inputs():
        import jax
        import jax.numpy as jnp
        _rk = jax.random.key(seed)
        x = -0.0005146 + 1 * jax.random.normal(jax.random.fold_in(_rk, 1), (16, 64, 128), jnp.float32)
        _lenS = 64 - jax.random.randint(jax.random.fold_in(_rk, 7), (16,), 0, max(1, 64 // 4) + 1, jnp.int32)
        _lenS2 = 1601 - jax.random.randint(jax.random.fold_in(_rk, 8), (16,), 0, max(1, 1601 // 4) + 1, jnp.int32)
        _ctx_1024P = jax.random.normal(jax.random.fold_in(_rk, 11), (16, 16, 128), jnp.float32)
        _ctx_1024c = jax.random.dirichlet(jax.random.fold_in(_rk, 511), 0.3 * jnp.ones((16,), jnp.float32), (16, 1601))
        _ctx_1024t = jnp.einsum('bsk,bkd->bsd', _ctx_1024c, _ctx_1024P)
        _ctx_1024t = _ctx_1024t * jax.lax.rsqrt(jnp.mean(jnp.square(_ctx_1024t)) + 1e-12) * 0.953939
        ctx_1024 = -0.000392918 + 0.999932 * (_ctx_1024t + 0.3 * jax.random.normal(jax.random.fold_in(_rk, 611), (16, 1601, 128), jnp.float32))
        return (x, ctx_1024)
    x, ctx_1024 = _rec_inputs()

    def _L0_xattn_setup():
        import jax, jax.numpy as jnp
        import numpy as np
        DIM = 128
        DIM_HEAD = 64
        HEADS = 16
        INNER = DIM_HEAD * HEADS
        EPS = 1e-05

        def layer_norm(x, g, b):
            m = jnp.mean(x, axis=-1, keepdims=True)
            v = jnp.mean(jnp.square(x - m), axis=-1, keepdims=True)
            return (x - m) * jax.lax.rsqrt(v + EPS) * g + b
        key = jax.random.key(seed)
        ks = jax.random.split(key, 8)
        B, N_IMG, N_LAT = (4, 512, 64)
        std = 1.0 / np.sqrt(DIM)
        return {'image_embeds': jax.random.normal(ks[0], (B, N_IMG, DIM), dtype=jnp.float32), 'latents': jax.random.normal(ks[1], (B, N_LAT, DIM), dtype=jnp.float32), 'ln1_g': jnp.ones((DIM,), jnp.float32), 'ln1_b': jnp.zeros((DIM,), jnp.float32), 'ln2_g': jnp.ones((DIM,), jnp.float32), 'ln2_b': jnp.zeros((DIM,), jnp.float32), 'Wq': jax.random.normal(ks[2], (DIM, INNER), dtype=jnp.float32) * std, 'Wkv': jax.random.normal(ks[3], (DIM, 2 * INNER), dtype=jnp.float32) * std, 'Wo': jax.random.normal(ks[4], (INNER, DIM), dtype=jnp.float32) * std}
    _L0_xattn_all = _L0_xattn_setup()
    _L0_xattn_in = {k: v for k, v in _L0_xattn_all.items() if k in ('ln1_g', 'ln1_b', 'ln2_g', 'ln2_b', 'Wq', 'Wkv', 'Wo')}
    del _L0_xattn_all

    def _L0_attn_setup():
        import jax, jax.numpy as jnp
        import numpy as np
        D_MODEL = 128
        NUM_HEADS = 16
        D_HEAD = D_MODEL // NUM_HEADS
        LAMBDA_INIT = 0.8
        EPS = 1e-05
        B, N = (4, 128)
        key = jax.random.key(seed)
        ks = jax.random.split(key, 10)
        w_scale = 1.0 / np.sqrt(D_MODEL)
        d2 = 2 * D_HEAD * NUM_HEADS
        return {'X': jax.random.normal(ks[0], (B, N, D_MODEL), jnp.float32), 'Wq': jax.random.normal(ks[1], (d2, D_MODEL), jnp.float32) * w_scale, 'Wk': jax.random.normal(ks[2], (d2, D_MODEL), jnp.float32) * w_scale, 'Wv': jax.random.normal(ks[3], (d2, D_MODEL), jnp.float32) * w_scale, 'Wo': jax.random.normal(ks[4], (D_MODEL, d2), jnp.float32) * w_scale, 'lq1': jax.random.normal(ks[5], (NUM_HEADS, D_HEAD), jnp.float32), 'lk1': jax.random.normal(ks[6], (NUM_HEADS, D_HEAD), jnp.float32), 'lq2': jax.random.normal(ks[7], (NUM_HEADS, D_HEAD), jnp.float32), 'lk2': jax.random.normal(ks[8], (NUM_HEADS, D_HEAD), jnp.float32), 'rms_scale': jnp.ones((2 * D_HEAD,), jnp.float32)}
    _L0_attn_all = _L0_attn_setup()
    _L0_attn_in = {k: v for k, v in _L0_attn_all.items() if k in ('Wq', 'Wk', 'Wv', 'Wo', 'lq1', 'lk1', 'lq2', 'lk2', 'rms_scale')}
    del _L0_attn_all

    def _L0_ffn_setup():
        import jax, jax.numpy as jnp
        import numpy as np
        B, S, D, O, E, K = (4, 256, 128, 128, 8, 2)
        key = jax.random.key(seed)
        ks = jax.random.split(key, 5)
        scale_in = 1.0 / np.sqrt(D)
        x = jax.random.normal(ks[0], (B, S, D), dtype=jnp.float32)
        gate_w = jax.random.uniform(ks[1], (E, D), jnp.float32, -scale_in, scale_in)
        gate_b = jax.random.uniform(ks[2], (E,), jnp.float32, -scale_in, scale_in)
        expert_w = jax.random.uniform(ks[3], (E, D, O), jnp.float32, -scale_in, scale_in)
        expert_b = jax.random.uniform(ks[4], (E, O), jnp.float32, -scale_in, scale_in)
        return {'x': x, 'gate_w': gate_w, 'gate_b': gate_b, 'expert_w': expert_w, 'expert_b': expert_b}
    _L0_ffn_all = _L0_ffn_setup()
    _L0_ffn_in = {k: v for k, v in _L0_ffn_all.items() if k in ('gate_w', 'gate_b', 'expert_w', 'expert_b')}
    del _L0_ffn_all
    return {'x': x, 'ctx_1024': ctx_1024, 'L0_xattn_ln1_g': _L0_xattn_in['ln1_g'], 'L0_xattn_ln1_b': _L0_xattn_in['ln1_b'], 'L0_xattn_ln2_g': _L0_xattn_in['ln2_g'], 'L0_xattn_ln2_b': _L0_xattn_in['ln2_b'], 'L0_xattn_Wq': _L0_xattn_in['Wq'], 'L0_xattn_Wkv': _L0_xattn_in['Wkv'], 'L0_xattn_Wo': _L0_xattn_in['Wo'], 'L0_attn_Wq': _L0_attn_in['Wq'], 'L0_attn_Wk': _L0_attn_in['Wk'], 'L0_attn_Wv': _L0_attn_in['Wv'], 'L0_attn_Wo': _L0_attn_in['Wo'], 'L0_attn_lq1': _L0_attn_in['lq1'], 'L0_attn_lk1': _L0_attn_in['lk1'], 'L0_attn_lq2': _L0_attn_in['lq2'], 'L0_attn_lk2': _L0_attn_in['lk2'], 'L0_attn_rms_scale': _L0_attn_in['rms_scale'], 'L0_ffn_gate_w': _L0_ffn_in['gate_w'], 'L0_ffn_gate_b': _L0_ffn_in['gate_b'], 'L0_ffn_expert_w': _L0_ffn_in['expert_w'], 'L0_ffn_expert_b': _L0_ffn_in['expert_b']}

def reference(x, ctx_1024, L0_xattn_ln1_g, L0_xattn_ln1_b, L0_xattn_ln2_g, L0_xattn_ln2_b, L0_xattn_Wq, L0_xattn_Wkv, L0_xattn_Wo, L0_attn_Wq, L0_attn_Wk, L0_attn_Wv, L0_attn_Wo, L0_attn_lq1, L0_attn_lk1, L0_attn_lq2, L0_attn_lk2, L0_attn_rms_scale, L0_ffn_gate_w, L0_ffn_gate_b, L0_ffn_expert_w, L0_ffn_expert_b):
    import jax
    import jax.numpy as jnp

    def _L0_xattn_ref(image_embeds, latents, ln1_g, ln1_b, ln2_g, ln2_b, Wq, Wkv, Wo):
        import jax, jax.numpy as jnp
        import numpy as np
        DIM = 128
        DIM_HEAD = 64
        HEADS = 16
        INNER = DIM_HEAD * HEADS
        EPS = 1e-05

        def layer_norm(x, g, b):
            m = jnp.mean(x, axis=-1, keepdims=True)
            v = jnp.mean(jnp.square(x - m), axis=-1, keepdims=True)
            return (x - m) * jax.lax.rsqrt(v + EPS) * g + b
        B, S_lat, _ = latents.shape
        x = layer_norm(image_embeds, ln1_g, ln1_b)
        l = layer_norm(latents, ln2_g, ln2_b)
        q = l @ Wq
        kv_in = jnp.concatenate([x, l], axis=1)
        kv = kv_in @ Wkv
        k, v = jnp.split(kv, 2, axis=-1)

        def to_heads(t):
            return t.reshape(t.shape[0], t.shape[1], HEADS, DIM_HEAD).transpose(0, 2, 1, 3)
        q, k, v = (to_heads(q), to_heads(k), to_heads(v))
        scale = 1.0 / np.sqrt(np.sqrt(DIM_HEAD))
        w = jnp.einsum('bhqd,bhkd->bhqk', q * scale, k * scale)
        w = jax.nn.softmax(w.astype(jnp.float32), axis=-1).astype(q.dtype)
        out = jnp.einsum('bhqk,bhkd->bhqd', w, v)
        out = out.transpose(0, 2, 1, 3).reshape(B, S_lat, INNER)
        return out @ Wo

    def _L0_attn_ref(X, Wq, Wk, Wv, Wo, lq1, lk1, lq2, lk2, rms_scale):
        import jax, jax.numpy as jnp
        import numpy as np
        D_MODEL = 128
        NUM_HEADS = 16
        D_HEAD = D_MODEL // NUM_HEADS
        LAMBDA_INIT = 0.8
        EPS = 1e-05
        B, N = (4, 128)
        b, n, _ = X.shape
        H, dh = (NUM_HEADS, D_HEAD)

        def proj(W):
            return (X @ W.T).reshape(b, n, H, 2 * dh).transpose(0, 2, 1, 3)
        Q, K, V = (proj(Wq), proj(Wk), proj(Wv))
        Q1, Q2 = jnp.split(Q, 2, axis=-1)
        K1, K2 = jnp.split(K, 2, axis=-1)
        lam = jnp.exp(jnp.sum(lq1 * lk1, axis=-1)) - jnp.exp(jnp.sum(lq2 * lk2, axis=-1)) + LAMBDA_INIT
        lam = lam[None, :, None, None]
        scaling = 1.0 / np.sqrt(dh)
        causal = jnp.tril(jnp.ones((n, n), bool))
        A1 = jnp.where(causal, jnp.einsum('bhnd,bhmd->bhnm', Q1, K1) * scaling, -jnp.inf)
        A2 = jnp.where(causal, jnp.einsum('bhnd,bhmd->bhnm', Q2, K2) * scaling, -jnp.inf)
        attn = jax.nn.softmax(A1, axis=-1) - lam * jax.nn.softmax(A2, axis=-1)
        O = jnp.einsum('bhnm,bhmd->bhnd', attn, V)
        rms = jnp.sqrt(jnp.mean(O * O, axis=-1, keepdims=True) + EPS)
        O = O / rms * rms_scale * (1.0 - LAMBDA_INIT)
        Oc = O.transpose(0, 2, 1, 3).reshape(b, n, H * 2 * dh)
        return Oc @ Wo.T

    def _L0_ffn_ref(x, gate_w, gate_b, expert_w, expert_b):
        import jax, jax.numpy as jnp
        import numpy as np
        B, S, D, O, E, K = (4, 256, 128, 128, 8, 2)
        logits = jnp.einsum('bsd,ed->bse', x, gate_w) + gate_b
        if K < E:
            topv, topi = jax.lax.top_k(logits, K)
            keep = jax.nn.one_hot(topi, E, dtype=jnp.float32).sum(axis=-2)
            logits = jnp.where(keep > 0, logits, -jnp.inf)
        gate_score = jax.nn.softmax(logits, axis=-1)
        expert_out = jnp.einsum('bsd,edo->bseo', x, expert_w) + expert_b
        out = jnp.einsum('bseo,bse->bso', expert_out, gate_score)
        return out
    x = x + _L0_xattn_ref(ctx_1024, _layernorm(x, axis=-1), L0_xattn_ln1_g, L0_xattn_ln1_b, L0_xattn_ln2_g, L0_xattn_ln2_b, L0_xattn_Wq, L0_xattn_Wkv, L0_xattn_Wo)
    x = x + _L0_attn_ref(_layernorm(x, axis=-1), L0_attn_Wq, L0_attn_Wk, L0_attn_Wv, L0_attn_Wo, L0_attn_lq1, L0_attn_lk1, L0_attn_lq2, L0_attn_lk2, L0_attn_rms_scale)
    x = x + _L0_ffn_ref(_layernorm(x, axis=-1), L0_ffn_gate_w, L0_ffn_gate_b, L0_ffn_expert_w, L0_ffn_expert_b)
    return x

_drawn_inputs = setup_inputs


def setup_inputs(seed=0):
    import zlib

    import numpy as np

    out = dict(_drawn_inputs(seed))
    spreads = {'L0_xattn_ln1_g': (1.0, 0.2),
     'L0_xattn_ln1_b': (0.0, 0.1),
     'L0_xattn_ln2_g': (1.0, 0.2),
     'L0_xattn_ln2_b': (0.0, 0.1),
     'L0_attn_rms_scale': (1.0, 0.2)}
    factors = {'L0_ffn_expert_b': 2.87}
    for name, (base, spread) in spreads.items():
        noise = np.random.default_rng([zlib.crc32(name.encode()), seed]).standard_normal(out[name].shape)
        drawn = base * np.exp(spread * noise) if base else spread * noise
        out[name] = jnp.asarray(drawn.astype(out[name].dtype))
    for name, factor in factors.items():
        out[name] = (out[name] * factor).astype(out[name].dtype)
    return out
```

```python
import concourse.bass as bass
from concourse import mybir
from contextlib import ExitStack

F32 = mybir.dt.float32
F16 = mybir.dt.float16
ALU = mybir.AluOpType
ACT = mybir.ActivationFunctionType
AX = mybir.AxisListType

B, NQ, D = 16, 64, 128
NCTX = 1601
H, DH = 16, 64
COLS = H * NQ
FULL = NCTX // 128
REST = NCTX - FULL * 128
TILES = FULL + 1
UNITS = TILES + 1
LAT = TILES
HALF = COLS // 2
GROUPS = 4
EPS = 1e-5
QMAX = 64.0
NPB = 4
TB = 8
SH, SD = 16, 8
NE = 8


class Turn:

    def __init__(self, off, i=None, step=2):
        self.off, self.i, self.step = off, i, step

    def plus(self, d):
        return Turn(self.off + d, self.i, self.step)

    def times(self, per, add=0):
        if self.i is None:
            return per * self.off + add
        return self.i * (self.step * per) + (per * self.off + add)


class Signal:

    def __init__(self, sem, per=1):
        self.sem, self.per = sem, per

    def upto(self, turn, k=0):
        return turn.times(self.per, k + 1)


def side_plan():
    m_counts = {3: 3, 4: 3, 5: 3, 6: 3, 7: 3, 8: 3, 9: 4, 10: 3, 11: 3, 12: 4}
    plan, m = [], 0
    for u in range(UNITS):
        row = []
        if u == 0:
            row += [("q", 0), ("q", 1)]
        if u == 1:
            row += [("ol", 0), ("ol", 1), ("q", 2), ("q", 3)]
        if 2 <= u < 2 + GROUPS:
            row += [("t", u - 2)]
        if u == 6:
            row += [("bc", 0), ("bc", 1)]
        for _ in range(m_counts.get(u, 0)):
            row += [("m", m)]
            m += 1
        if u == 11:
            row += [("pj", 0)]
        if u == UNITS - 1:
            row += [("mt", 0), ("mt", 1)]
        plan.append(row)
    assert m == 32
    return plan


PLAN = side_plan()
BANK = {item: n % 2 for n, item in enumerate([it for row in PLAN for it in row])}
assert BANK[("ol", 0)] != BANK[("ol", 1)]
STATS_AT = {0: range(0, 3), 1: range(3, 6), 2: range(6, 11), 3: range(11, 13)}
PREP = ("q", "t", "m", "mt")


def rows_of(u):
    return 128 if u < FULL else (REST if u == FULL else NQ)


def perceiver(nc, x, ctx_in, ln1_g, ln1_b, ln2_g, ln2_b, Wq, Wkv, Wo, aWq, aWk, aWv, aWo,
              lq1, lk1, lq2, lk2, rms_scale, gate_w, gate_b, expert_w, expert_b, out):
    es = ExitStack()
    with es:
        def sb(name, shape, dt=F32):
            return es.enter_context(nc.sbuf_tensor(name, shape, dt))

        def sem(name, per=1):
            return Signal(es.enter_context(nc.semaphore(name)), per)

        ident = sb("ident", [128, 128])
        ident16 = sb("ident16", [128, 128], F16)
        ones = sb("ones", [1, 128])
        ones16 = sb("ones16", [1, 64], F16)
        region = sb("region", [128, 10 * 1024])

        def part(start, size, dt=F32):
            v = region[:, start:start + size]
            return v if dt == F32 else v.bitcast(dt)

        wq_sb = part(0, 1024)
        wkv_sb = part(1024, 2048)
        wo_sb = part(3072, 1024).rearrange("p (n d) -> p n d", d=128)
        wqT = part(4096, 1024).rearrange("p (n d) -> p n d", d=128)
        wkT = part(5120, 2048).rearrange("p (n d) -> p n d", d=256)
        wvT = part(7168, 2048).rearrange("p (n d) -> p n d", d=256)
        q_hi = [part(2048 * p, 1024, F16) for p in range(2)]
        q_lo = [part(2048 * p + 1024, 1024, F16) for p in range(2)]
        p_hi = [part(4096 + 1024 * k, 512, F16) for k in range(NPB)]
        p_lo = [part(4608 + 1024 * k, 512, F16) for k in range(NPB)]
        o_sb = part(8192, 2048).rearrange("p (k n) -> p k n", k=2)
        A = part(0, 2048).rearrange("p (g c a m) -> p g c a m", g=4, c=4, a=2)
        E = part(2048, 2048).rearrange("p (g c a m) -> p g c a m", g=4, c=4, a=2)
        t1 = part(4096, 1024).rearrange("p (g c m) -> p g c m", g=4, c=4)
        t2 = part(5120, 1024).rearrange("p (g c m) -> p g c m", g=4, c=4)
        At = part(6144, 1024).rearrange("p (h m) -> p h m", m=64)
        AT = part(7168, 1024).rearrange("p (h n) -> p h n", n=128)
        prod = [part(8192 + 1024 * p, 1024).rearrange("p (e o) -> p e o", o=D) for p in range(2)]
        gb = sb("gb", [128, 4])
        g0row = sb("g0row", [1, 2, 1])
        fold = sb("fold", [128, 2, 128])
        G = sb("G", [128, H, 256])
        WO = sb("WO", [128, H, 256])
        amax = sb("amax", [128, 2])
        sigma = sb("sigma", [128, 2])
        lx = sb("lx", [NQ, B, D])
        lk_hi = sb("lk_hi", [NQ, B, D], F16)
        lk_lo = sb("lk_lo", [NQ, B, D], F16)
        lT = sb("lT", [128, B * NQ])
        lT_hi = sb("lT_hi", [128, B * NQ], F16)
        lT_lo = sb("lT_lo", [128, B * NQ], F16)
        cT = sb("cT", [128, NQ])
        cT_hi = [sb(f"cT_hi{p}", [128, NQ], F16) for p in range(2)]
        cT_lo = [sb(f"cT_lo{p}", [128, NQ], F16) for p in range(2)]
        ck_hi = [sb(f"ck_hi{p}", [NQ, D], F16) for p in range(2)]
        ck_lo = [sb(f"ck_lo{p}", [NQ, D], F16) for p in range(2)]
        raw = [sb(f"raw{p}", [128, TILES, D]) for p in range(2)]
        xk_hi = [sb(f"xk_hi{p}", [128, TILES, D], F16) for p in range(2)]
        xk_lo = [sb(f"xk_lo{p}", [128, TILES, D], F16) for p in range(2)]
        xT_hi = [sb(f"xT_hi{p}", [128, TILES * 128], F16) for p in range(2)]
        xT_lo = [sb(f"xT_lo{p}", [128, TILES * 128], F16) for p in range(2)]
        srow = sb("srow", [1, COLS])
        rb = sb("rb", [128, COLS])
        attnT = sb("attnT", [128, B * NQ])
        st = sb("st", [128, 16, 6])
        sm = sb("sm", [128, 8, 16])
        carrier = sb("carrier", [1, 16])
        mhalf = sb("mhalf", [128, 16])
        mx = sb("mx", [128, 8, 4])
        m16 = sb("m16", [128, 8], F16)
        xres = sb("xres", [128, TB, D])
        hn = sb("hn", [128, TB, D])
        hT = lT
        wpad = sb("wpad", [128, 3, 4, 128])
        wpadT = sb("wpadT", [128, 3, 4, 128])
        wv_sb = sb("wv_sb", [128, 2, 128])
        wvaT = sb("wvaT", [128, 256])
        woa_sb = sb("woa_sb", [128, 256])
        woaT = sb("woaT", [128, 2, 128])
        rmsc = sb("rmsc", [128, 1])
        lv = sb("lv", [128, 4, 128])
        lp = sb("lp", [128, 2, 128])
        lsum = sb("lsum", [128, 2, SH])
        lexp = sb("lexp", [128, 2, SH])
        nlam = sb("nlam", [128, SH])
        mask = sb("mask", [128, NQ])
        gw_sb = sb("gw_sb", [NE, 128])
        gwT = sb("gwT", [128, NE])
        gbias = sb("gbias", [128, NE])
        ew = sb("ew", [128, NE, 128])
        eb = sb("eb", [NE, 128])

        S = es.enter_context(nc.psum_tensor("S", [128, 4, 512], F32))
        OA = es.enter_context(nc.psum_tensor("OA", [128, 2, 512], F32))
        W = [es.enter_context(nc.psum_tensor(f"W{k}", [128, 512], F32)) for k in range(2)]

        ld_w = sem("ld_w")
        ld_gb = sem("ld_gb")
        ld_x = sem("ld_x")
        ld_res = sem("ld_res")
        ld_raw = [sem(f"ld_raw{p}") for p in range(2)]
        ld_a = sem("ld_a")
        consts = sem("consts")
        padded = sem("padded")
        pool_link = sem("pool_link")
        dve_link = sem("dve_link")
        folded = sem("folded")
        pe_w = sem("pe_w")
        ev_w = sem("ev_w")
        amax_rdy = sem("amax_rdy")
        amax_all = sem("amax_all")
        g_rdy = sem("g_rdy")
        var_rdy = sem("var_rdy")
        rstd_rdy = sem("rstd_rdy")
        rstd_ctx = sem("rstd_ctx")
        lat_rdy = sem("lat_rdy")
        lat_t = sem("lat_t")
        lat_cp = sem("lat_cp")
        lat_hi = sem("lat_hi")
        lat_lo = sem("lat_lo")
        s_done = sem("s_done", UNITS)
        e_done = sem("e_done", UNITS)
        lo_done = sem("lo_done", UNITS)
        pv_done = sem("pv_done", UNITS)
        oa_free = sem("oa_free")
        pe_item = {k: sem("pe_" + k, n) for k, n in
                   (("q", 4), ("t", 4), ("m", 32), ("mt", 2), ("bc", 2), ("pj", 1))}
        q_hi_done = sem("q_hi_done", 4)
        free = {"q": sem("q_lo_done", 4), "t": sem("t_copied", 4), "m": sem("m_reduced", 32),
                "mt": sem("m_row", 2), "ol": sem("ol_copied", 2), "bc": sem("recip_done", 2),
                "pj": sem("pj_copied", 1)}
        stats_ok = sem("stats_ok")
        normed = sem("normed")
        split_hi = sem("split_hi", GROUPS)
        split = sem("split", GROUPS)
        cur32 = sem("cur32")
        curT = sem("curT")
        curk = sem("curk")
        m16_done = sem("m16_done")
        srow_done = sem("srow_done")
        o_normed = sem("o_normed", 2)
        dve_step = sem("dve_step", 4)

        def pbuf(turn, u):
            return (2 * (turn.off % 2) + u) % NPB

        def score_bank(u, half):
            return S[:, 2 * (u % 2) + half, :]

        def load_raw(sp, turn):
            p = turn.off % 2
            b = turn.times(1)
            first = ctx_in[bass.ds(b, 1), 0:FULL * 128, :] if turn.i is not None else ctx_in[b:b + 1, 0:FULL * 128, :]
            last = ctx_in[bass.ds(b, 1), FULL * 128:NCTX, :] if turn.i is not None else ctx_in[b:b + 1, FULL * 128:NCTX, :]
            sp.dma_start(raw[p][:, 0:FULL, :],
                         first.rearrange("o (p t) d -> p (o t) d", t=FULL)).then_inc(ld_raw[p].sem, 16)
            sp.dma_start(raw[p][0:REST, FULL, :],
                         last.rearrange("o p d -> p (o d)")).then_inc(ld_raw[p].sem, 16)

        LD_A = 16 * (12 + 2 + 4 + 8 + 4)

        def stats_combine(P, n, link):
            mean_e, var_e, mean_o, var_o = (st[0:P, 0:n, k] for k in (1, 2, 4, 5))
            c = lambda k: sm[0:P, k, 0:n]
            nc.vector.tensor_tensor(c(2), mean_e, mean_o, ALU.subtract)
            nc.vector.tensor_tensor(c(3), var_e, var_o, ALU.add)
            link(nc.vector.tensor_tensor(c(4), mean_e, mean_o, ALU.add))
            nc.vector.tensor_scalar(c(0), c(4), 0.5, None, ALU.mult)
            link(nc.vector.tensor_tensor(c(5), c(2), c(2), ALU.mult))
            link(nc.vector.scalar_tensor_tensor(c(6), c(5), 32.0, c(3), ALU.mult, ALU.add))
            return nc.vector.tensor_scalar(c(7), c(6), 1.0 / D, EPS, ALU.mult, ALU.add)

        def bn(turn, t):
            r = rows_of(t)
            return nc.vector.bn_stats(st[0:r, t, :], raw[turn.off % 2][0:r, t, :])

        def raw_loaded(turn):
            return (turn.i * 32 if turn.i is not None else 0) + 32 * (turn.off // 2) + 32

        hTd = sb("hTd", [128, 2, 2, 64])
        Qs = sb("Qs", [128, 4, 128])
        Ks = sb("Ks", [128, 4, 2, 2, 64])
        Vb = sb("Vb", [128, 2, 8, 32])
        amx = sb("amx", [128, 4, 4, 2])
        asum = sb("asum", [128, 4, 4, 2])
        arc = sb("arc", [128, 4, 4, 2])
        Ob = sb("Ob", [128, 256])
        Osq = sb("Osq", [128, 256])
        Oc = sb("Oc", [128, 256])
        oms = sb("oms", [128, 3, SH])
        OcT = sb("OcT", [128, 2, 128])
        lg = sb("lg", [128, 10, TB, NE])
        g1 = sb("g1", [128, 4, TB])
        rank = sb("rank", [128, NE])
        gT = rb[0:NE, :]
        xb = attnT[:].rearrange("p (t d) -> p t d", d=D)
        ta = {n: sem("ta_" + n) for n in (
            "x1t", "x1", "h", "ht", "hcopy",
            "hd", "projqk", "projv", "qk1", "k2", "vb", "scores", "masked", "max", "shifted", "exp", "r", "r2",
            "t1", "t2", "sums", "attn", "at_t", "at", "pv", "ob", "sq", "ms", "ms2", "ms3", "oc", "oct_t", "oct", "proj_o",
            "x2", "h2", "h2t", "h2copy", "logits", "gexp_in", "gexp", "gates", "gates_t", "gt")}
        ex_mm, ex_prod, ex_b, ex_add, ex_out = (sem("ex_" + n) for n in ("mm", "prod", "xb", "add", "out"))
        tail_dve = sem("tail_dve")
        tail_pool = sem("tail_pool")
        wt_t, wt_c = sem("wt_t"), sem("wt_c")
        lam_in, lam_exp = sem("lam_in"), sem("lam_exp")
        rms_rdy = sem("rms_rdy")
        LAST = Turn(B - 1)

        def carry(pool, turn, site):
            if turn.i is not None:
                nc.gpsimd.tensor_tensor(carrier[:, site:site + 1], carrier[:, 14:15], carrier[:, 15:16], ALU.mult)

        def inverse_deviation(pool, n):
            pool.wait_ge(var_rdy.sem, n + 1)
            nc.gpsimd.tensor_tensor(sm[:, 1, :], sm[:, 7, :], mhalf[:], ALU.pow).then_inc(rstd_rdy.sem, 1)

        def layer_norm(dve, link, n, turn_no):
            for t in range(n):
                ins = nc.vector.bn_stats(st[:, t, :], xres[:, t, :])
            link(ins)
            stats_combine(128, n, link).then_inc(var_rdy.sem, 1)
            dve.wait_ge(rstd_rdy.sem, turn_no)
            for t in range(n):
                ins = nc.vector.tensor_scalar(hn[:, t, :], xres[:, t, :], sm[:, 0, t:t + 1], sm[:, 1, t:t + 1],
                                              ALU.subtract, ALU.mult)
            return ins

        def small_weights_vector(dve, link):
            dve.wait_ge(ld_a.sem, LD_A)
            for k in range(2):
                ins = nc.vector.tensor_tensor(lp[:, k, :], lv[:, 2 * k, :], lv[:, 2 * k + 1, :], ALU.mult)
            link(ins)
            nc.vector.tensor_reduce(lsum[:], lp[:].rearrange("p k (h d) -> p k h d", d=SD), AX.X, ALU.add)\
              .then_inc(lam_in.sem, 1)
            nc.vector.tensor_scalar(rmsc[:], rmsc[:], 1.0 - 0.8, None, ALU.mult).then_inc(rms_rdy.sem, 1)
            dve.wait_ge(lam_exp.sem, 1)
            link(nc.vector.tensor_tensor(nlam[:], lexp[:, 1, :], lexp[:, 0, :], ALU.subtract))
            link(nc.vector.tensor_scalar(nlam[:], nlam[:], -0.8, None, ALU.add))
            nc.vector.memset(Vb[:].rearrange("p a b c -> p (a b c)"), 0.0)
            for e in range(NE):
                ins = nc.vector.memset(rank[:, e:e + 1], float(NE - e))
            link(ins)

        def small_weights_tensor(pe):
            pe.wait_ge(ld_a.sem, LD_A)
            for g in range(5):
                if g >= 2:
                    pe.wait_ge(wt_c.sem, g - 1)
                w = W[g % 2]
                if g < 3:
                    for c in range(4):
                        ins = nc.tensor.transpose(w[:, 128 * c:128 * c + 128], wpad[:, g, c, :], ident[:])
                if g == 3:
                    for c in range(2):
                        nc.tensor.transpose(w[:, 128 * c:128 * c + 128], wv_sb[:, c, :], ident[:])
                        ins = nc.tensor.transpose(w[:, 256 + 128 * c:384 + 128 * c], woa_sb[:, 128 * c:128 * c + 128],
                                                  ident[:])
                if g == 4:
                    ins = nc.tensor.transpose(w[:, 0:NE], gw_sb[:], ident[0:NE, 0:NE])
                ins.then_inc(wt_t.sem, 1)
            pe.wait_ge(wt_c.sem, 5)

        def small_weights_scalar(act):
            act.wait_ge(lam_in.sem, 1)
            nc.scalar.activation(lexp[:], lsum[:], ACT.Exp).then_inc(lam_exp.sem, 1)
            for g in range(5):
                act.wait_ge(wt_t.sem, g + 1)
                w = W[g % 2]
                if g < 3:
                    ins = nc.scalar.copy(wpadT[:, g, :, :].rearrange("p c n -> p (c n)"), w[:])
                if g == 3:
                    act.wait_ge(rms_rdy.sem, 1)
                    nc.scalar.copy(wvaT[:], w[:, 0:256])
                    ins = nc.scalar.activation(woaT[:].rearrange("p c n -> p (c n)"), w[:, 256:512], ACT.Copy,
                                               scale=rmsc[:])
                if g == 4:
                    ins = nc.scalar.copy(gwT[:], w[:, 0:NE])
                ins.then_inc(wt_c.sem, 1)

        def tile_cols(t, turn):
            if turn.i is None:
                return t[:, 128 * turn.off:128 * turn.off + 128]
            return t[:, bass.ds(turn.times(128), 128)]

        def tile_of(t, turn):
            if turn.i is None:
                return t[:, turn.off, :]
            return t[:, bass.ds(turn.times(1), 1), :].rearrange("p o d -> p (o d)")

        def wait(eng, name, turn):
            eng.wait_ge(ta[name].sem, ta[name].upto(turn))

        def first(turn):
            return turn.i is None and turn.off == 0

        def more(turn):
            return turn.i is not None or turn.off < TB - 1

        def bc(ap, n):
            return ap.unsqueeze(len(ap.shape)).to_broadcast(list(ap.shape) + [n])

        def tail_vector(dve):
            chain = [0]

            def link(ins):
                chain[0] += 1
                ins.then_inc(tail_dve.sem, 1)
                dve.wait_ge(tail_dve.sem, chain[0])

            wait(dve, "x1t", Turn(0))
            dve.wait_ge(ld_res.sem, 16)
            xf = xres[:].rearrange("p t d -> p (t d)")
            dve.wait_ge(normed.sem, normed.upto(LAST))
            link(nc.vector.tensor_tensor(xf, S[:, 0:2, :].rearrange("p a n -> p (a n)"), xf, ALU.add))
            layer_norm(dve, link, TB, 3).then_inc(ta["h"].sem, 1)

            def keys2(t):
                wait(dve, "projqk", t)
                nc.vector.tensor_copy(Ks[:, :, :, 1, :], W[0][:].rearrange("p (c j m) -> p c j m", c=4, j=2))\
                  .then_inc(ta["k2"].sem, 1)

            def masked_scores(t):
                wait(dve, "scores", t)
                nc.vector.scalar_tensor_tensor(
                    A[:].rearrange("p g c a m -> p (g c a) m"),
                    S[:].rearrange("p g (k m) -> p (g k) m", m=64), SD ** -0.5,
                    mask[:].unsqueeze(1).to_broadcast([128, 32, 64]), ALU.mult, ALU.add).then_inc(ta["masked"].sem, 1)
                wait(dve, "masked", t)
                if not first(t):
                    wait(dve, "shifted", t.plus(-1))
                nc.vector.tensor_reduce(amx[:].rearrange("p g c a -> p (g c a)"),
                                        A[:].rearrange("p g c a m -> p (g c a) m"), AX.X, ALU.max)\
                  .then_inc(ta["max"].sem, 1)

            def attention(t):
                wait(dve, "exp", t)
                nc.vector.tensor_reduce(asum[:].rearrange("p g c a -> p (g c a)"),
                                        E[:].rearrange("p g c a m -> p (g c a) m"), AX.X, ALU.add)\
                  .then_inc(ta["sums"].sem, 1)
                wait(dve, "sums", t)
                if not first(t):
                    wait(dve, "t2", t.plus(-1))
                nc.vector.reciprocal(arc[:], asum[:]).then_inc(ta["r"].sem, 1)
                wait(dve, "r", t)
                nc.vector.tensor_tensor(arc[:, :, :, 1], arc[:, :, :, 1], nlam[:].rearrange("p (c g) -> p g c", c=4),
                                        ALU.mult).then_inc(ta["r2"].sem, 1)
                nc.vector.tensor_tensor(t1[:], E[:, :, :, 0, :], bc(arc[:, :, :, 0], 64), ALU.mult)\
                  .then_inc(ta["t1"].sem, 1)
                wait(dve, "t1", t)
                wait(dve, "t2", t)
                if not first(t):
                    wait(dve, "at_t", t.plus(-1))
                nc.vector.tensor_tensor(At[:].rearrange("p (c g) m -> p g c m", c=4), t1[:], t2[:], ALU.add)\
                  .then_inc(ta["attn"].sem, 1)

            def group_norm(t):
                wait(dve, "ob", t)
                nc.vector.tensor_tensor(Osq[:], Ob[:], Ob[:], ALU.mult).then_inc(ta["sq"].sem, 1)
                wait(dve, "sq", t)
                nc.vector.tensor_reduce(oms[:, 0, :], Osq[:].rearrange("p (h d) -> p h d", h=SH), AX.X, ALU.add)\
                  .then_inc(ta["ms"].sem, 1)
                wait(dve, "ms", t)
                nc.vector.tensor_scalar(oms[:, 1, :], oms[:, 0, :], 1.0 / (2 * SD), EPS, ALU.mult, ALU.add)\
                  .then_inc(ta["ms2"].sem, 1)
                wait(dve, "ms3", t)
                if not first(t):
                    wait(dve, "oct_t", t.plus(-1))
                nc.vector.tensor_tensor(Oc[:].rearrange("p (h d) -> p h d", h=SH),
                                        Ob[:].rearrange("p (h d) -> p h d", h=SH), bc(oms[:, 2, :], 2 * SD),
                                        ALU.mult).then_inc(ta["oc"].sem, 1)

            def residual(t):
                wait(dve, "proj_o", t)
                nc.vector.tensor_tensor(tile_of(xres, t), W[0][:, 0:128], tile_of(xres, t), ALU.add)\
                  .then_inc(ta["x2"].sem, 1)

            keys2(Turn(0))
            masked_scores(Turn(0))
            def middle(t):
                keys2(t.plus(1))
                attention(t)
                masked_scores(t.plus(1))
                group_norm(t)
                residual(t)
            middle(Turn(0))
            with dve.Fori(0, TB - 2) as i:
                middle(Turn(1, i, 1))
            t = Turn(TB - 1)
            attention(t)
            group_norm(t)
            residual(t)
            wait(dve, "x2", t)
            layer_norm(dve, link, TB, 4).then_inc(ta["h2"].sem, 1)

            L = lambda k: lg[:, k, :, :]
            rk = rank[:].unsqueeze(1).to_broadcast([128, TB, NE])
            wait(dve, "logits", Turn(0))
            link(nc.vector.tensor_tensor(L(0), W[0][:, 0:64].rearrange("p (t e) -> p t e", t=TB),
                                         gbias[:].unsqueeze(1).to_broadcast([128, TB, NE]), ALU.add))

            def largest(src, dst, tmp, mxi, m2i):
                link(nc.vector.tensor_reduce(g1[:, mxi, :], src, AX.X, ALU.max))
                link(nc.vector.tensor_tensor(tmp, src, bc(g1[:, mxi, :], NE), ALU.is_equal))
                link(nc.vector.tensor_tensor(tmp, tmp, rk, ALU.mult))
                link(nc.vector.tensor_reduce(g1[:, m2i, :], tmp, AX.X, ALU.max))
                link(nc.vector.tensor_tensor(dst, tmp, bc(g1[:, m2i, :], NE), ALU.is_equal))

            largest(L(0), L(1), L(2), 0, 1)
            nc.vector.tensor_tensor(L(8), L(0), bc(g1[:, 0, :], NE), ALU.subtract).then_inc(ta["gexp_in"].sem, 1)
            link(nc.vector.scalar_tensor_tensor(L(3), L(1), -3e38, L(0), ALU.mult, ALU.add))
            largest(L(3), L(4), L(2), 2, 1)
            link(nc.vector.tensor_tensor(L(5), L(1), L(4), ALU.add))
            wait(dve, "gexp", Turn(0))
            link(nc.vector.tensor_tensor(L(6), L(9), L(5), ALU.mult))
            link(nc.vector.tensor_reduce(g1[:, 3, :], L(6), AX.X, ALU.add))
            link(nc.vector.reciprocal(g1[:, 2, :], g1[:, 3, :]))
            link(nc.vector.tensor_tensor(L(7), L(6), bc(g1[:, 2, :], NE), ALU.mult))
            nc.vector.tensor_copy(L(8), L(7)).then_inc(ta["gates"].sem, 1)
            for t in range(TB):
                dve.wait_ge(ex_mm.sem, t + 1)
                if t >= 2:
                    dve.wait_ge(ex_add.sem, t - 1)
                nc.vector.tensor_tensor(prod[t % 2][:], S[:, 2 * (t % 2):2 * (t % 2) + 2, :].rearrange(
                    "p a (e o) -> p (a e) o", o=D), bc(lg[:, 7, t, :], D), ALU.mult).then_inc(ex_prod.sem, 1)
                nc.vector.tensor_tensor(xb[:, t, :], W[t % 2][:, 0:128], xres[:, t, :], ALU.add).then_inc(ex_b.sem, 1)

        def tail_gpsimd(pool):
            def columns(t):
                wait(pool, "hcopy", Turn(0))
                if not first(t):
                    wait(pool, "projv", t.plus(-1))
                src = tile_cols(hT, t).rearrange("p (j n) -> p j n", j=2)
                carry(pool, t, 0 + 0)
                nc.gpsimd.tensor_copy(hTd[:, :, 0, :], src)
                nc.gpsimd.tensor_copy(hTd[:, :, 1, :], src).then_inc(ta["hd"].sem, 1)

            def shift(t):
                wait(pool, "max", t)
                nc.gpsimd.tensor_tensor(A[:], A[:], bc(amx[:], 64), ALU.subtract).then_inc(ta["shifted"].sem, 1)

            def second_map(t):
                wait(pool, "r2", t)
                nc.gpsimd.tensor_tensor(t2[:], E[:, :, :, 1, :], bc(arc[:, :, :, 1], 64), ALU.mult)\
                  .then_inc(ta["t2"].sem, 1)

            def inverse_rms(t):
                wait(pool, "ms2", t)
                nc.gpsimd.tensor_tensor(oms[:, 2, :], oms[:, 1, :], mhalf[:], ALU.pow).then_inc(ta["ms3"].sem, 1)

            inverse_deviation(pool, 2)
            columns(Turn(0))
            shift(Turn(0))
            def middle(t):
                columns(t.plus(1))
                second_map(t)
                shift(t.plus(1))
                inverse_rms(t)
            middle(Turn(0))
            with pool.Fori(0, TB - 2) as i:
                middle(Turn(1, i, 1))
            second_map(Turn(TB - 1))
            inverse_rms(Turn(TB - 1))
            inverse_deviation(pool, 3)
            n = 0
            for t in range(TB):
                pool.wait_ge(ex_prod.sem, t + 1)
                pr = prod[t % 2]
                for m in (4, 2, 1):
                    nc.gpsimd.tensor_tensor(pr[:, 0:m, :], pr[:, 0:m, :], pr[:, m:2 * m, :], ALU.add)\
                      .then_inc(tail_pool.sem, 1)
                    n += 1
                    pool.wait_ge(tail_pool.sem, n)
                pool.wait_ge(ex_b.sem, t + 1)
                nc.gpsimd.tensor_tensor(xb[:, t, :], xb[:, t, :], pr[:, 0, :], ALU.add).then_inc(ex_add.sem, 1)

        def tail_scalar(act):
            act.wait_ge(ta["ht"].sem, 1)
            nc.scalar.copy(hT[:], S[:, 2:4, :].rearrange("p a n -> p (a n)")).then_inc(ta["hcopy"].sem, 1)

            def queries_keys(t):
                wait(act, "projqk", t)
                nc.scalar.copy(Qs[:].rearrange("p c n -> p (c n)"), OA[:, 0, :])
                nc.scalar.copy(Ks[:, :, :, 0, :], OA[:, 1, :].rearrange("p (c j m) -> p c j m", c=4, j=2))\
                  .then_inc(ta["qk1"].sem, 1)

            def values(t):
                wait(act, "projv", t)
                if first(t):
                    act.wait_ge(ld_a.sem, LD_A)
                v = W[1][:].rearrange("p (j h d) -> p j h d", j=2, h=8)
                nc.scalar.copy(Vb[0:64, :, :, 0:16], v[0:64, :, :, 0:16])
                nc.scalar.copy(Vb[64:128, :, :, 16:32], v[64:128, :, :, 16:32]).then_inc(ta["vb"].sem, 1)

            def exp(t):
                wait(act, "shifted", t)
                if not first(t):
                    wait(act, "attn", t.plus(-1))
                nc.scalar.activation(E[:].rearrange("p g c a m -> p (g c a m)"),
                                     A[:].rearrange("p g c a m -> p (g c a m)"), ACT.Exp).then_inc(ta["exp"].sem, 1)

            def weights(t):
                wait(act, "at_t", t)
                nc.scalar.copy(AT[:].rearrange("p h n -> p (h n)"), OA[:].rearrange("p a n -> p (a n)"))\
                  .then_inc(ta["at"].sem, 1)
                wait(act, "pv", t)
                nc.scalar.copy(Ob[:], W[0][:, 0:256]).then_inc(ta["ob"].sem, 1)

            def columns_out(t):
                wait(act, "oct_t", t)
                nc.scalar.copy(OcT[:].rearrange("p c n -> p (c n)"), W[1][:, 0:256]).then_inc(ta["oct"].sem, 1)

            queries_keys(Turn(0))
            values(Turn(0))
            exp(Turn(0))
            def middle(t):
                queries_keys(t.plus(1))
                weights(t)
                values(t.plus(1))
                columns_out(t)
                exp(t.plus(1))
            middle(Turn(0))
            with act.Fori(0, TB - 2) as i:
                middle(Turn(1, i, 1))
            weights(Turn(TB - 1))
            columns_out(Turn(TB - 1))
            wait(act, "h2t", Turn(0))
            nc.scalar.copy(hT[:], S[:, 0:2, :].rearrange("p a n -> p (a n)")).then_inc(ta["h2copy"].sem, 1)
            wait(act, "gexp_in", Turn(0))
            nc.scalar.activation(lg[:, 9, :, :], lg[:, 8, :, :], ACT.Exp).then_inc(ta["gexp"].sem, 1)
            wait(act, "gates_t", Turn(0))
            nc.scalar.copy(gT[:], OA[0:NE, :, :].rearrange("p a n -> p (a n)")).then_inc(ta["gt"].sem, 1)

        def tail_tensor(pe):
            mm = nc.tensor.matmul
            pe.wait_ge(free["pj"].sem, free["pj"].upto(LAST))
            pe.wait_ge(lo_done.sem, lo_done.upto(LAST, LAT))
            for t in range(TB):
                ins = nc.tensor.transpose(S[:, t // 4, 128 * (t % 4):128 * (t % 4) + 128],
                                          attnT[:, 128 * t:128 * t + 128], ident[:])
            ins.then_inc(ta["x1t"].sem, 1)
            wait(pe, "h", Turn(0))
            for t in range(TB):
                ins = nc.tensor.transpose(S[:, 2 + t // 4, 128 * (t % 4):128 * (t % 4) + 128], hn[:, t, :], ident[:])
            ins.then_inc(ta["ht"].sem, 1)

            def project(t):
                wait(pe, "hd", t)
                if t.i is not None or t.off >= 2:
                    wait(pe, "at", t.plus(-2))
                    wait(pe, "x2", t.plus(-2))
                if first(t):
                    pe.wait_ge(free["bc"].sem, free["bc"].upto(LAST, 1))
                for kind, dst in enumerate((OA[:, 0, :], OA[:, 1, :], W[0][:])):
                    for c in range(4):
                        ins = mm(dst[:, 128 * c:128 * c + 128], wpadT[:, kind, c, :], hTd[:, :, 0, :],
                                 start=True, stop=True)
                ins.then_inc(ta["projqk"].sem, 1)

            def project_values(t):
                if t.i is not None or t.off >= 2:
                    wait(pe, "oct", t.plus(-2))
                for j in range(2):
                    ins = mm(W[1][:, 256 * j:256 * j + 256], hTd[:, j, :, :].rearrange("p a n -> p (a n)"), wvaT[:],
                             start=True, stop=True)
                ins.then_inc(ta["projv"].sem, 1)

            def self_scores(t):
                wait(pe, "qk1", t)
                wait(pe, "k2", t)
                if not first(t):
                    wait(pe, "masked", t.plus(-1))
                else:
                    wait(pe, "hcopy", t)
                for c in range(4):
                    for j in range(2):
                        for g in range(4):
                            r = slice(32 * g, 32 * g + 32)
                            ins = mm(S[64 * j:64 * j + 64, g, 128 * c:128 * c + 128], Qs[r, c, 64 * j:64 * j + 64],
                                     Ks[r, c, j, :, :].rearrange("p a m -> p (a m)"), start=True, stop=True,
                                     tile_position=(32 * g, 64 * j))
                ins.then_inc(ta["scores"].sem, 1)

            def transpose_attention(t):
                wait(pe, "attn", t)
                if more(t):
                    wait(pe, "qk1", t.plus(1))
                for h in range(8):
                    ins = nc.tensor.transpose(OA[:, h // 4, 128 * (h % 4):128 * (h % 4) + 128],
                                              At[:, 2 * h:2 * h + 2, :].rearrange("p a m -> p (a m)"), ident[:])
                ins.then_inc(ta["at_t"].sem, 1)

            def weigh_values(t):
                wait(pe, "at", t)
                wait(pe, "vb", t)
                if more(t):
                    wait(pe, "k2", t.plus(1))
                else:
                    wait(pe, "x2", t.plus(-1))
                for j in range(2):
                    for h in range(8):
                        ins = mm(W[0][64 * j:64 * j + 64, 32 * h:32 * h + 32], AT[:, h, 64 * j:64 * j + 64],
                                 Vb[:, j, h, :], start=True, stop=True)
                ins.then_inc(ta["pv"].sem, 1)

            def project_out(t):
                wait(pe, "oc", t)
                if more(t):
                    wait(pe, "vb", t.plus(1))
                for c in range(2):
                    ins = nc.tensor.transpose(W[1][:, 128 * c:128 * c + 128], Oc[:, 128 * c:128 * c + 128], ident[:])
                ins.then_inc(ta["oct_t"].sem, 1)
                wait(pe, "oct", t)
                wait(pe, "ob", t)
                for c in range(2):
                    ins = mm(W[0][:, 0:128], OcT[:, c, :], woaT[:, c, :], start=(c == 0), stop=(c == 1))
                ins.then_inc(ta["proj_o"].sem, 1)

            project(Turn(0))
            self_scores(Turn(0))
            project_values(Turn(0))
            def middle(t):
                project(t.plus(1))
                self_scores(t.plus(1))
                transpose_attention(t)
                weigh_values(t)
                project_values(t.plus(1))
                project_out(t)
            middle(Turn(0))
            with pe.Fori(0, TB - 2) as i:
                middle(Turn(1, i, 1))
            t = Turn(TB - 1)
            transpose_attention(t)
            weigh_values(t)
            project_out(t)

            wait(pe, "h2", Turn(0))
            wait(pe, "masked", Turn(TB - 1))
            for t in range(TB):
                ins = nc.tensor.transpose(S[:, t // 4, 128 * (t % 4):128 * (t % 4) + 128], hn[:, t, :], ident[:])
            ins.then_inc(ta["h2t"].sem, 1)
            wait(pe, "h2copy", Turn(0))
            wait(pe, "x2", Turn(TB - 1))
            for t in range(TB):
                ins = mm(W[0][:, NE * t:NE * t + NE], hT[:, 128 * t:128 * t + 128], gwT[:], start=True, stop=True)
            ins.then_inc(ta["logits"].sem, 1)

            def experts(t):
                if t >= 2:
                    pe.wait_ge(ex_prod.sem, t - 1)
                for c in range(2):
                    mm(S[:, 2 * (t % 2) + c, :], hT[:, 128 * t:128 * t + 128],
                       ew[:, 4 * c:4 * c + 4, :].rearrange("p e o -> p (e o)"), start=True, stop=True)

            def expert_bias(t):
                if t >= 2:
                    pe.wait_ge(ex_b.sem, t - 1)
                mm(W[t % 2][:, 0:128], gT[:, 128 * t:128 * t + 128], eb[:], start=True, stop=True)\
                    .then_inc(ex_mm.sem, 1)

            experts(0)
            experts(1)
            wait(pe, "gates", Turn(0))
            for t in range(TB):
                ins = nc.tensor.transpose(OA[0:NE, t // 4, 128 * (t % 4):128 * (t % 4) + 128], lg[:, 8, t, :], ident[:])
            ins.then_inc(ta["gates_t"].sem, 1)
            wait(pe, "gt", Turn(0))
            expert_bias(0)
            expert_bias(1)
            for t in range(2, TB):
                experts(t)
                expert_bias(t)


        block = es.enter_context(nc.Block())

        @block.sync
        def _(sp):
            with nc.allow_non_contiguous_dma(reason="columns of gains and biases"):
                for k, v in enumerate((ln1_g, ln1_b, ln2_g, ln2_b)):
                    sp.dma_start(gb[:, k:k + 1], v.rearrange("(p o) -> p o", o=1)).then_inc(ld_gb.sem, 16)
                for k, v in enumerate((ln1_g, ln2_g)):
                    sp.dma_start(g0row[0:1, k, :], v[0:1].rearrange("(o n) -> o n", o=1)).then_inc(ld_gb.sem, 16)
            sp.dma_start(lx[:], x.rearrange("b q d -> q b d")).then_inc(ld_x.sem, 16)
            sp.dma_start(wq_sb[:], Wq).then_inc(ld_w.sem, 16)
            sp.dma_start(wkv_sb[:], Wkv).then_inc(ld_w.sem, 16)
            sp.dma_start(wo_sb[:], Wo.rearrange("(n p) d -> p n d", p=128)).then_inc(ld_w.sem, 16)
            load_raw(sp, Turn(0))
            load_raw(sp, Turn(1))
            sp.dma_start(xres[:], x.rearrange("(t j) q d -> (j q) t d", j=2)).then_inc(ld_res.sem, 16)
            sp.wait_ge(padded.sem, 1)
            for j in range(4):
                for kind, wt, r0, r1 in ((0, aWq, 0, 16), (1, aWk, 0, 8), (2, aWk, 8, 16)):
                    src = wt.rearrange("(c j k) d -> j k c d", c=4, j=4)[j, r0:r1]
                    sp.dma_start(wpad[32 * j + r0:32 * j + r1, kind, :, :], src).then_inc(ld_a.sem, 16)
            sp.dma_start(wv_sb[:], aWv.rearrange("(c p) d -> p c d", p=128)).then_inc(ld_a.sem, 16)
            sp.dma_start(woa_sb[:], aWo).then_inc(ld_a.sem, 16)
            for k, v in enumerate((lq1, lk1, lq2, lk2)):
                sp.dma_start(lv[:, k, :], v.rearrange("h (o d) -> o (h d)", o=1).to_broadcast([128, 128]))\
                  .then_inc(ld_a.sem, 16)
            with nc.allow_non_contiguous_dma(reason="one scale per row"):
                for h in range(8):
                    sp.dma_start(rmsc[16 * h:16 * h + 16, :], rms_scale.rearrange("(p o) -> p o", o=1))\
                      .then_inc(ld_a.sem, 16)
            sp.dma_start(gw_sb[:], gate_w).then_inc(ld_a.sem, 16)
            sp.dma_start(gbias[:], gate_b.rearrange("(o e) -> o e", o=1).to_broadcast([128, NE])).then_inc(ld_a.sem, 16)
            sp.dma_start(ew[:], expert_w.rearrange("e d o -> d e o")).then_inc(ld_a.sem, 16)
            sp.dma_start(eb[:], expert_b).then_inc(ld_a.sem, 16)

            with sp.Fori(0, B // 2 - 1) as i:
                for off in (2, 3):
                    n = Turn(off, i)
                    sp.wait_ge(split.sem, split.upto(n.plus(-2), GROUPS - 1))
                    load_raw(sp, n)

            for t in range(TB):
                sp.wait_ge(ex_add.sem, t + 1)
                sp.dma_start(out[2 * t:2 * t + 2].rearrange("j q d -> (j q) d"), xb[:, t, :]).then_inc(ex_out.sem, 16)
            sp.wait_ge(ex_out.sem, 16 * TB)
        @block.vector
        def _(dve):
            chain = [0]

            def link(ins):
                chain[0] += 1
                ins.then_inc(dve_link.sem, 1)
                dve.wait_ge(dve_link.sem, chain[0])

            nc.vector.memset(st[:], 0.0)
            nc.vector.memset(ones[:], 1.0)
            link(nc.vector.memset(ones16[:], 1.0))
            dve.wait_ge(consts.sem, 1)
            dve.wait_ge(ld_x.sem, 16)
            for rnd in range(2):
                for b in range(B):
                    ins = nc.vector.bn_stats(st[0:NQ, b, :], lx[:, b, :])
                link(ins)
                stats_combine(NQ, B, link).then_inc(var_rdy.sem, 1)
                dve.wait_ge(rstd_rdy.sem, rnd + 1)
                for b in range(B):
                    ins = nc.vector.tensor_scalar(lx[:, b, :], lx[:, b, :], sm[0:NQ, 0, b:b + 1],
                                                  sm[0:NQ, 1, b:b + 1], ALU.subtract, ALU.mult)
                link(ins)
            link(nc.vector.memset(lx[:, :, 0:1], 1.0))
            nc.vector.tensor_copy(lk_hi[:], lx[:]).then_inc(lat_rdy.sem, 1)
            dve.wait_ge(lat_rdy.sem, 1)
            nc.vector.tensor_tensor(lk_lo[:], lx[:], lk_hi[:], ALU.subtract).then_inc(lat_lo.sem, 1)
            dve.wait_ge(ld_gb.sem, 96)
            dve.wait_ge(consts.sem, 2)
            for k in range(2):
                ins = nc.vector.tensor_scalar(fold[:, k, :], ident[:], gb[:, 2 * k:2 * k + 1], None, ALU.mult)
            link(ins)
            for k in range(2):
                ins = nc.vector.tensor_scalar(fold[0:1, k, :], ones[:], g0row[0:1, k, :], -1.0, ALU.mult, ALU.mult)
            link(ins)
            for k in range(2):
                ins = nc.vector.tensor_copy(fold[:, k, 0:1], gb[:, 2 * k + 1:2 * k + 2])
            ins.then_inc(folded.sem, 1)
            for n in range(24):
                dve.wait_ge(pe_w.sem, n + 1)
                hp, kind = n // 3, n % 3
                dst = (wqT[:, hp, :], wkT[:, hp, :], wvT[:, hp, :])[kind]
                src = W[n % 2][:, 128:256] if kind == 0 else W[n % 2][:, 0:256]
                nc.vector.tensor_copy(dst, src).then_inc(ev_w.sem, 1)
            for n in range(24, 24 + 2 * H):
                dve.wait_ge(pe_w.sem, n + 1)
                h, kind = (n - 24) // 2, n % 2
                if kind == 0:
                    ins = nc.vector.tensor_scalar(G[:, h, :], W[n % 2][:, 0:256], DH ** -0.5, None, ALU.mult)
                else:
                    ins = nc.vector.tensor_copy(WO[:, h, :], W[n % 2][:, 0:256])
                ins.then_inc(ev_w.sem, 1)
            dve.wait_ge(ev_w.sem, 24 + 2 * H)
            link(nc.vector.tensor_tensor(G[:, :, 128:129], G[:, :, 128:129], G[:, :, 0:1], ALU.subtract))
            link(nc.vector.memset(G[:, :, 0:1], 0.0))
            nc.vector.tensor_reduce(amax[:, 0:1], G[:].rearrange("p h c -> p (h c)"), AX.X, ALU.max,
                                    apply_absolute_value=True).then_inc(amax_rdy.sem, 1)
            dve.wait_ge(amax_all.sem, 1)
            link(nc.vector.tensor_scalar(sigma[:, 0:1], amax[:, 1:2], 1e-30, 129.0 / QMAX, ALU.max, ALU.mult))
            link(nc.vector.reciprocal(sigma[:, 1:2], sigma[:, 0:1]))
            nc.vector.tensor_scalar(G[:].rearrange("p h c -> p (h c)"), G[:].rearrange("p h c -> p (h c)"),
                                    sigma[:, 1:2], None, ALU.mult).then_inc(g_rdy.sem, 1)
            dve.wait_ge(lat_t.sem, 1)
            nc.vector.tensor_copy(lT[:], S[:, 0:2, :].rearrange("p a n -> p (a n)")).then_inc(lat_cp.sem, 1)
            dve.wait_ge(lat_hi.sem, 1)
            dve.wait_ge(lat_cp.sem, 1)
            nc.vector.tensor_tensor(lT_lo[:], lT[:], lT_hi[:], ALU.subtract).then_inc(lat_lo.sem, 1)

            small_weights_vector(dve, link)

            def statistics(turn, u):
                if u == 0:
                    dve.wait_ge(ld_raw[turn.off % 2].sem, raw_loaded(turn))
                    if not (turn.i is None and turn.off == 0):
                        dve.wait_ge(normed.sem, normed.upto(turn.plus(-1)))
                for t in STATS_AT.get(u, ()):
                    ins = bn(turn, t)
                if u == 3:
                    k = [0]

                    def step(ins):
                        ins.then_inc(dve_step.sem, 1)
                        dve.wait_ge(dve_step.sem, dve_step.upto(turn, k[0]))
                        k[0] += 1
                    step(ins)
                    last = stats_combine(128, TILES, step)
                    last.then_inc(stats_ok.sem, 1)

            def queries_low(turn, c):
                dve.wait_ge(q_hi_done.sem, q_hi_done.upto(turn, c))
                cols = slice(c * HALF, (c + 1) * HALF)
                p = turn.off % 2
                nc.vector.tensor_tensor(q_lo[p][:, cols], W[BANK[("q", c)]][:], q_hi[p][:, cols], ALU.subtract)\
                  .then_inc(free["q"].sem, 1)

            def maxima(turn, n):
                dve.wait_ge(pe_item["m"].sem, pe_item["m"].upto(turn, n))
                c, r = n // 8, n % 8
                if n == 0 and not (turn.i is None and turn.off == 0):
                    dve.wait_ge(m16_done.sem, m16_done.upto(turn.plus(-1)))
                width = 512 if c < 3 else REST + NQ
                nc.vector.tensor_reduce(mx[:, r, c:c + 1], W[BANK[("m", n)]][:, 0:width], AX.X, ALU.max)\
                  .then_inc(free["m"].sem, 1)
                if n == 31:
                    dve.wait_ge(free["m"].sem, free["m"].upto(turn, 31))
                    if not (turn.i is None and turn.off == 0):
                        dve.wait_ge(pe_item["mt"].sem, pe_item["mt"].upto(turn.plus(-1), 1))
                    nc.vector.tensor_reduce(m16[:], mx[:], AX.X, ALU.max, negate=True).then_inc(m16_done.sem, 1)

            def low_part(turn, u):
                r, k = rows_of(u), pbuf(turn, u)
                dve.wait_ge(e_done.sem, e_done.upto(turn, u))
                src = S[0:r, 2 * (u % 2):2 * (u % 2) + 2, :].rearrange("p a n -> p (a n)")
                nc.vector.tensor_tensor(p_lo[k][0:r, :], src, p_hi[k][0:r, :], ALU.subtract)\
                  .then_inc(lo_done.sem, 1)

            def denominators(turn):
                dve.wait_ge(oa_free.sem, oa_free.upto(turn))
                dve.wait_ge(free["ol"].sem, free["ol"].upto(turn, 1))
                if not (turn.i is None and turn.off == 0):
                    dve.wait_ge(pe_item["bc"].sem, pe_item["bc"].upto(turn.plus(-1), 1))
                nc.vector.tensor_tensor(srow[:], o_sb[0:1, 0, :], o_sb[0:1, 1, :], ALU.add).then_inc(srow_done.sem, 1)

            def reciprocals(turn, k):
                dve.wait_ge(pe_item["bc"].sem, pe_item["bc"].upto(turn, k))
                nc.vector.reciprocal(rb[:, k * HALF:(k + 1) * HALF], W[BANK[("bc", k)]][:])\
                  .then_inc(free["bc"].sem, 1)

            def slot(b, prep=True, post=True, stats=True):
                nxt, old = b.plus(1), b.plus(-1)
                for u in range(UNITS):
                    if stats:
                        statistics(b.plus(2), u)
                    for kind, k in PLAN[u]:
                        if kind == "q" and prep:
                            queries_low(nxt, k)
                        if kind == "m" and prep:
                            maxima(nxt, k)
                        if kind == "bc" and post:
                            reciprocals(old, k)
                    low_part(b, u)
                    if u == 2 and post:
                        denominators(old)

            for n in range(2):
                for u in range(4):
                    statistics(Turn(n), u)
            for row in PLAN:
                for kind, k in row:
                    if kind == "q":
                        queries_low(Turn(0), k)
                    if kind == "m":
                        maxima(Turn(0), k)
            slot(Turn(0), post=False)
            with dve.Fori(0, B // 2 - 2) as i:
                slot(Turn(1, i))
                slot(Turn(2, i))
            slot(Turn(B - 3))
            slot(Turn(B - 2), stats=False)
            slot(Turn(B - 1), prep=False, stats=False)
            denominators(Turn(B - 1))
            for k in range(2):
                reciprocals(Turn(B - 1), k)
            tail_vector(dve)

        @block.gpsimd
        def _(pool):
            nc.gpsimd.memset(wpad[:].rearrange("p a b c -> p (a b c)"), 0.0).then_inc(padded.sem, 1)
            nc.gpsimd.memset(sm[:].rearrange("p a b -> p (a b)"), 1.0)
            nc.gpsimd.memset(mhalf[:], -0.5)
            nc.gpsimd.memset(carrier[:], 0.0)
            nc.gpsimd.memset(mask[:], 0.0).then_inc(pool_link.sem, 1)
            nc.gpsimd.memset(ident[:], 0.0).then_inc(pool_link.sem, 1)
            pool.wait_ge(pool_link.sem, 2)
            nc.gpsimd.affine_select(out=ident[:], in_=ident[:], compare_op=ALU.not_equal, fill=1.0, base=0,
                                    pattern=[[-1, 128]], channel_multiplier=1).then_inc(consts.sem, 1)
            pool.wait_ge(consts.sem, 1)
            nc.gpsimd.tensor_copy(ident16[:], ident[:]).then_inc(consts.sem, 1)
            for j in range(2):
                pool.wait_ge(consts.sem, 2 + j)
                nc.gpsimd.affine_select(out=mask[64 * j:64 * j + 64, :], in_=mask[64 * j:64 * j + 64, :],
                                        compare_op=ALU.is_ge, fill=-3e38, base=0,
                                        pattern=[[-1, NQ]], channel_multiplier=1).then_inc(consts.sem, 1)
            pool.wait_ge(consts.sem, 4)
            for p in range(2):
                nc.gpsimd.memset(xk_hi[p][:, :, 0:1], 1.0)
                ins = nc.gpsimd.memset(xk_lo[p][:, :, 0:1], 0.0)
            ins.then_inc(pool_link.sem, 1)
            pool.wait_ge(pool_link.sem, 3)

            for rnd in range(2):
                inverse_deviation(pool, rnd)

            def normalise(turn):
                pool.wait_ge(stats_ok.sem, stats_ok.upto(turn))
                nc.gpsimd.tensor_tensor(sm[:, 1, 0:TILES], sm[:, 7, 0:TILES], mhalf[:, 0:TILES], ALU.pow)\
                  .then_inc(rstd_ctx.sem, 1)
                pool.wait_ge(rstd_ctx.sem, rstd_ctx.upto(turn))
                pool.wait_ge(ld_raw[turn.off % 2].sem, raw_loaded(turn))
                carry(pool, turn, 2 + turn.off % 2)
                x_ = raw[turn.off % 2]
                for t in range(TILES):
                    r = rows_of(t)
                    ins = nc.gpsimd.tensor_scalar(x_[0:r, t, :], x_[0:r, t, :], sm[0:r, 0, t:t + 1],
                                                  sm[0:r, 1, t:t + 1], ALU.subtract, ALU.mult)
                ins.then_inc(normed.sem, 1)

            def split_tokens(turn):
                p = turn.off % 2
                pool.wait_ge(normed.sem, normed.upto(turn))
                if not (turn.i is None and turn.off < 2):
                    pool.wait_ge(pv_done.sem, pv_done.upto(turn.plus(-2), TILES - 1))
                for g in range(GROUPS):
                    r = 128 if g < 3 else REST
                    t = slice(4 * g, 4 * g + 4) if g < 3 else slice(FULL, FULL + 1)
                    hi, lo, f = xk_hi[p][0:r, t, 1:D], xk_lo[p][0:r, t, 1:D], raw[p][0:r, t, 1:D]
                    carry(pool, turn, 4 + turn.off % 2)
                    nc.gpsimd.tensor_copy(hi, f).then_inc(split_hi.sem, 1)
                    pool.wait_ge(split_hi.sem, split_hi.upto(turn, g))
                    nc.gpsimd.tensor_tensor(lo, f, hi, ALU.subtract).then_inc(split.sem, 1)

            def at64(t, turn):
                if turn.i is None:
                    return t[:, 64 * turn.off:64 * turn.off + 64]
                return t[:, bass.ds(turn.times(64), 64)]

            def at_batch(t, turn):
                if turn.i is None:
                    return t[:, turn.off, :]
                return t[:, bass.ds(turn.times(1), 1), :].rearrange("p o d -> p (o d)")

            def current_T(turn):
                p = turn.off % 2
                if not (turn.i is None and turn.off < 2):
                    pool.wait_ge(s_done.sem, s_done.upto(turn.plus(-2), LAT))
                carry(pool, turn, 6 + turn.off % 2)
                nc.gpsimd.tensor_copy(cT_hi[p][:], at64(lT_hi, turn))
                nc.gpsimd.tensor_copy(cT_lo[p][:], at64(lT_lo, turn)).then_inc(curT.sem, 1)

            def current_k(turn):
                p = turn.off % 2
                if not (turn.i is None and turn.off < 2):
                    pool.wait_ge(pv_done.sem, pv_done.upto(turn.plus(-2), LAT))
                carry(pool, turn, 8 + turn.off % 2)
                nc.gpsimd.tensor_copy(ck_hi[p][:], at_batch(lk_hi, turn))
                nc.gpsimd.tensor_copy(ck_lo[p][:], at_batch(lk_lo, turn)).then_inc(curk.sem, 1)

            def current_32(turn):
                if not (turn.i is None and turn.off < 1):
                    pool.wait_ge(pe_item["q"].sem, pe_item["q"].upto(turn.plus(-1), 3))
                carry(pool, turn, 10 + turn.off % 2)
                nc.gpsimd.tensor_copy(cT[:], at64(lT, turn)).then_inc(cur32.sem, 1)

            def scale_outputs(turn):
                for k in range(2):
                    cols = slice(k * HALF, (k + 1) * HALF)
                    pool.wait_ge(free["bc"].sem, free["bc"].upto(turn, k))
                    nc.gpsimd.tensor_tensor(o_sb[:, 0, cols], o_sb[:, 0, cols], rb[:, cols], ALU.mult)
                    nc.gpsimd.tensor_tensor(o_sb[:, 1, cols], o_sb[:, 1, cols], rb[:, cols], ALU.mult)\
                      .then_inc(o_normed.sem, 1)

            def slot(b, prep=True, post=True, stats=True):
                if prep:
                    split_tokens(b.plus(1))
                    current_T(b.plus(1))
                    current_k(b.plus(1))
                if stats:
                    current_32(b.plus(2))
                if stats:
                    normalise(b.plus(2))
                if post:
                    scale_outputs(b.plus(-1))

            pool.wait_ge(amax_rdy.sem, 1)
            nc.gpsimd.partition_all_reduce(amax[:, 1:2], amax[:, 0:1], 128, bass.bass_isa.ReduceOp.max)\
              .then_inc(amax_all.sem, 1)
            pool.wait_ge(lat_lo.sem, 2)
            pool.wait_ge(lat_cp.sem, 1)
            current_32(Turn(0))
            current_T(Turn(0))
            current_k(Turn(0))
            normalise(Turn(0))
            split_tokens(Turn(0))
            current_32(Turn(1))
            normalise(Turn(1))
            slot(Turn(0), post=False)
            with pool.Fori(0, B // 2 - 2) as i:
                slot(Turn(1, i))
                slot(Turn(2, i))
            slot(Turn(B - 3))
            slot(Turn(B - 2), stats=False)
            slot(Turn(B - 1), prep=False, stats=False)
            scale_outputs(Turn(B - 1))
            tail_gpsimd(pool)

        @block.scalar
        def _(act):
            act.wait_ge(lat_cp.sem, 1)
            nc.scalar.copy(lT_hi[:], lT[:]).then_inc(lat_hi.sem, 1)
            act.wait_ge(g_rdy.sem, 1)
            small_weights_scalar(act)

            def queries_high(turn, c):
                act.wait_ge(pe_item["q"].sem, pe_item["q"].upto(turn, c))
                p = turn.off % 2
                nc.scalar.copy(q_hi[p][:, c * HALF:(c + 1) * HALF], W[BANK[("q", c)]][:]).then_inc(q_hi_done.sem, 1)

            def transposed(turn, g):
                act.wait_ge(pe_item["t"].sem, pe_item["t"].upto(turn, g))
                p, w = turn.off % 2, (512 if g < 3 else REST)
                src = W[BANK[("t", g)]][:].bitcast(F16)
                nc.scalar.copy(xT_hi[p][:, 512 * g:512 * g + w], src[:, 0:w])
                nc.scalar.copy(xT_lo[p][:, 512 * g:512 * g + w], src[:, 512:512 + w]).then_inc(free["t"].sem, 1)

            def shift_row(turn, k):
                act.wait_ge(pe_item["mt"].sem, pe_item["mt"].upto(turn, k))
                nc.scalar.copy(q_hi[turn.off % 2][0:1, k * HALF:(k + 1) * HALF], W[BANK[("mt", k)]][0:1, :])\
                  .then_inc(free["mt"].sem, 1)

            def exponentials(turn, u):
                r, k = rows_of(u), pbuf(turn, u)
                act.wait_ge(s_done.sem, s_done.upto(turn, u))
                if not (turn.i is None and turn.off == 0 and u < NPB):
                    act.wait_ge(pv_done.sem, pv_done.upto(turn, u - NPB))
                src = S[0:r, 2 * (u % 2):2 * (u % 2) + 2, :].rearrange("p a n -> p (a n)")
                nc.scalar.activation(p_hi[k][0:r, :], src, ACT.Exp, scale=sigma[0:r, 0:1])
                nc.scalar.activation(src, src, ACT.Exp, scale=sigma[0:r, 0:1]).then_inc(e_done.sem, 1)

            def outputs(turn):
                act.wait_ge(pv_done.sem, pv_done.upto(turn, TILES - 1))
                if not (turn.i is None and turn.off == 0):
                    act.wait_ge(pe_item["pj"].sem, pe_item["pj"].upto(turn.plus(-1)))
                nc.scalar.copy(o_sb[:, 0, :], OA[:].rearrange("p a n -> p (a n)")).then_inc(oa_free.sem, 1)

            def latent_outputs(turn):
                act.wait_ge(pv_done.sem, pv_done.upto(turn, LAT))
                for k in range(2):
                    nc.scalar.copy(o_sb[:, 1, k * HALF:(k + 1) * HALF], W[BANK[("ol", k)]][:])\
                      .then_inc(free["ol"].sem, 1)

            def projected(turn):
                act.wait_ge(pe_item["pj"].sem, pe_item["pj"].upto(turn))
                dst = attnT[:, 64 * turn.off:64 * turn.off + 64] if turn.i is None \
                    else attnT[:, bass.ds(turn.times(64), 64)]
                nc.scalar.copy(dst, W[BANK[("pj", 0)]][:, 0:NQ]).then_inc(free["pj"].sem, 1)

            def slot(b, prep=True, post=True):
                nxt, old = b.plus(1), b.plus(-1)
                for u in range(UNITS):
                    if u == UNITS - 1 and prep:
                        shift_row(nxt, 0)
                        shift_row(nxt, 1)
                    exponentials(b, u)
                    if u == 0 and post:
                        outputs(old)
                    if u == 1 and post:
                        latent_outputs(old)
                    for kind, k in PLAN[u]:
                        if kind == "q" and prep:
                            queries_high(nxt, k)
                        if kind == "t" and prep:
                            transposed(nxt, k)
                        if kind == "pj" and post:
                            projected(old)

            for row in PLAN:
                for kind, k in row:
                    if kind == "q":
                        queries_high(Turn(0), k)
                    if kind == "t":
                        transposed(Turn(0), k)
                    if kind == "mt":
                        shift_row(Turn(0), k)
            slot(Turn(0), post=False)
            with act.Fori(0, B // 2 - 2) as i:
                slot(Turn(1, i))
                slot(Turn(2, i))
            slot(Turn(B - 3))
            slot(Turn(B - 2))
            slot(Turn(B - 1), prep=False)
            outputs(Turn(B - 1))
            latent_outputs(Turn(B - 1))
            projected(Turn(B - 1))
            tail_scalar(act)

        @block.tensor
        def _(pe):
            mm = nc.tensor.matmul
            pe.wait_ge(folded.sem, 1)
            pe.wait_ge(ld_w.sem, 48)
            for n in range(24):
                hp, kind = n // 3, n % 3
                if n >= 2:
                    pe.wait_ge(ev_w.sem, n - 1)
                w = (wq_sb[:, 128 * hp:128 * hp + 128], wkv_sb[:, 128 * hp:128 * hp + 128],
                     wkv_sb[:, H * DH + 128 * hp:H * DH + 128 * hp + 128])[kind]
                mm(W[n % 2][:, 0:256], w, fold[:].rearrange("p k d -> p (k d)"), start=True, stop=True)\
                    .then_inc(pe_w.sem, 1)
            for n in range(24, 24 + 2 * H):
                h, kind = (n - 24) // 2, n % 2
                pe.wait_ge(ev_w.sem, max(n - 1, 24))
                r = slice(64 * (h % 2), 64 * (h % 2) + 64)
                if kind == 0:
                    mm(W[n % 2][:, 0:256], wqT[r, h // 2, :], wkT[r, h // 2, :], start=True, stop=True)\
                        .then_inc(pe_w.sem, 1)
                else:
                    mm(W[n % 2][:, 0:128], wvT[r, h // 2, 0:128], wo_sb[r, h // 2, :], start=True, stop=True)
                    mm(W[n % 2][:, 128:256], wvT[r, h // 2, 128:256], wo_sb[r, h // 2, :], start=True, stop=True)\
                        .then_inc(pe_w.sem, 1)
            pe.wait_ge(lat_rdy.sem, 1)
            for b in range(B):
                ins = nc.tensor.transpose(S[:, b // 8, 64 * (b % 8):64 * (b % 8) + 64], lx[:, b, :], ident[0:NQ, 0:NQ])
            ins.then_inc(lat_t.sem, 1)
            pe.wait_ge(g_rdy.sem, 1)
            pe.wait_ge(consts.sem, 2)
            small_weights_tensor(pe)

            last_user = {}

            def bank_free(item, turn):
                bank = BANK[item]
                if bank in last_user:
                    (kind, k), t = last_user[bank]
                    pe.wait_ge(free[kind].sem, free[kind].upto(t, k))
                last_user[bank] = (item, turn)

            def side_item(item, turn):
                kind, k = item
                w, p = W[BANK[item]], turn.off % 2
                bank_free(item, turn)
                if kind == "q":
                    if k == 0:
                        pe.wait_ge(cur32.sem, cur32.upto(turn))
                    for j in range(8):
                        h, c = 8 * (k % 2) + j, 128 * (k // 2)
                        ins = mm(w[:, 64 * j:64 * j + 64], G[:, h, c:c + 128], cT[:], start=True, stop=True)
                if kind == "t":
                    pe.wait_ge(split.sem, split.upto(turn, k))
                    w16 = w[:].bitcast(F16)
                    for t in (range(4 * k, 4 * k + 4) if k < 3 else [FULL]):
                        r = rows_of(t)
                        for x_, o in ((xk_hi, 0), (xk_lo, 512)):
                            c = o + 128 * (t - 4 * k)
                            ins = nc.tensor.transpose(w16[:, c:c + r], x_[p][0:r, t, :], ident16[0:r, 0:r])
                if kind == "m":
                    c, r = k // 8, k % 8
                    if k == 0:
                        pe.wait_ge(q_hi_done.sem, q_hi_done.upto(turn, 3))
                    if r == 0:
                        pe.wait_ge(free["t"].sem, free["t"].upto(turn, c))
                    if c < 3:
                        ins = mm(w[:], q_hi[p][:, 128 * r:128 * r + 128], xT_hi[p][:, 512 * c:512 * c + 512],
                                 start=True, stop=True)
                    else:
                        if r == 0:
                            pe.wait_ge(curT.sem, curT.upto(turn))
                        mm(w[:, 0:REST], q_hi[p][:, 128 * r:128 * r + 128], xT_hi[p][:, 1536:1536 + REST],
                           start=True, stop=True)
                        ins = mm(w[:, REST:REST + NQ], q_hi[p][:, COLS + 128 * r:COLS + 128 * r + 128], cT_hi[p][:],
                                 start=True, stop=True)
                if kind == "mt":
                    pe.wait_ge(m16_done.sem, m16_done.upto(turn))
                    for j in range(4):
                        ins = mm(w[0:1, 128 * j:128 * j + 128], m16[:, 4 * k + j:4 * k + j + 1], ident16[:],
                                 start=True, stop=True)
                if kind == "bc":
                    pe.wait_ge(srow_done.sem, srow_done.upto(turn))
                    ins = mm(w[:], ones[:], srow[:, HALF * k:HALF * k + HALF], start=True, stop=True)
                if kind == "pj":
                    pe.wait_ge(o_normed.sem, o_normed.upto(turn, 1))
                    for h in range(H):
                        for c in range(2):
                            ins = mm(w[:, 0:NQ], WO[:, h, 128 * c:128 * c + 128], o_sb[:, c, 64 * h:64 * h + 64],
                                     start=(h == 0 and c == 0), stop=(h == H - 1 and c == 1))
                ins.then_inc(pe_item[kind].sem, 1)

            def scores(turn, u):
                p, r = turn.off % 2, rows_of(u)
                if not (turn.i is None and turn.off == 0 and u < 2):
                    pe.wait_ge(lo_done.sem, lo_done.upto(turn, u - 2))
                if u == 0:
                    pe.wait_ge(free["mt"].sem, free["mt"].upto(turn, 1))
                    pe.wait_ge(free["q"].sem, free["q"].upto(turn, 3))
                if u < LAT:
                    hi, lo, qc = xT_hi[p][:, 128 * u:128 * u + r], xT_lo[p][:, 128 * u:128 * u + r], 0
                else:
                    hi, lo, qc = cT_hi[p][:], cT_lo[p][:], COLS
                cols = [slice(qc + HALF * k, qc + HALF * k + HALF) for k in range(2)]
                for k in range(2):
                    mm(score_bank(u, k)[0:r], hi, q_hi[p][:, cols[k]], start=True, stop=False)
                for k in range(2):
                    mm(score_bank(u, k)[0:r], hi, q_lo[p][:, cols[k]], start=False, stop=False)
                if u == LAT:
                    for k in range(2):
                        mm(score_bank(u, k)[0:r], ones16[:], q_hi[p][0:1, HALF * k:HALF * k + HALF],
                           start=False, stop=False)
                for k in range(2):
                    ins = mm(score_bank(u, k)[0:r], lo, q_hi[p][:, cols[k]], start=False, stop=True)
                ins.then_inc(s_done.sem, 1)

            def weigh(turn, u):
                p, r, kb = turn.off % 2, rows_of(u), pbuf(turn, u)
                pe.wait_ge(lo_done.sem, lo_done.upto(turn, u))
                if u == 0 and not (turn.i is None and turn.off == 0):
                    pe.wait_ge(oa_free.sem, oa_free.upto(turn.plus(-1)))
                if u < LAT:
                    hi, lo, first, last = xk_hi[p][0:r, u, :], xk_lo[p][0:r, u, :], u == 0, u == TILES - 1
                    dst = [OA[:, k, :] for k in range(2)]
                else:
                    pe.wait_ge(curk.sem, curk.upto(turn))
                    hi, lo, first, last = ck_hi[p][:], ck_lo[p][:], True, True
                    for k in range(2):
                        bank_free(("ol", k), turn)
                    dst = [W[BANK[("ol", k)]][:] for k in range(2)]
                ph, pl = p_hi[kb], p_lo[kb]
                cols = [slice(HALF * k, HALF * k + HALF) for k in range(2)]
                for k in range(2):
                    mm(dst[k], hi, ph[0:r, cols[k]], start=first, stop=False)
                for k in range(2):
                    mm(dst[k], hi, pl[0:r, cols[k]], start=False, stop=False)
                for k in range(2):
                    ins = mm(dst[k], lo, ph[0:r, cols[k]], start=False, stop=last)
                ins.then_inc(pv_done.sem, 1)

            def slot(b, prep=True, post=True):
                nxt, old = b.plus(1), b.plus(-1)
                last_user.clear()
                for k in range(2):
                    last_user[BANK[("mt", k)]] = (("mt", k), b)
                for u in range(UNITS):
                    scores(b, u)
                    if u == UNITS - 1 and prep:
                        for k in range(2):
                            side_item(("mt", k), nxt)
                    if u >= 2:
                        weigh(b, u - 2)
                    elif post and u == 0:
                        weigh(old, TILES - 1)
                    elif post and u == 1:
                        weigh(old, LAT)
                    for item in PLAN[u]:
                        if item[0] in ("ol", "mt"):
                            continue
                        if item[0] in PREP and prep:
                            side_item(item, nxt)
                        if item[0] not in PREP and post:
                            side_item(item, old)

            for row in PLAN:
                for item in row:
                    if item[0] in PREP:
                        side_item(item, Turn(0))
            slot(Turn(0), post=False)
            with pe.Fori(0, B // 2 - 2) as i:
                slot(Turn(1, i))
                slot(Turn(2, i))
            slot(Turn(B - 3))
            slot(Turn(B - 2))
            slot(Turn(B - 1), prep=False)
            weigh(Turn(B - 1), TILES - 1)
            weigh(Turn(B - 1), LAT)
            for k in range(2):
                side_item(("bc", k), Turn(B - 1))
            side_item(("pj", 0), Turn(B - 1))
            tail_tensor(pe)


_INS = ['x', 'ctx_1024', 'L0_xattn_ln1_g', 'L0_xattn_ln1_b', 'L0_xattn_ln2_g', 'L0_xattn_ln2_b', 'L0_xattn_Wq',
        'L0_xattn_Wkv', 'L0_xattn_Wo', 'L0_attn_Wq', 'L0_attn_Wk', 'L0_attn_Wv', 'L0_attn_Wo', 'L0_attn_lq1',
        'L0_attn_lk1', 'L0_attn_lq2', 'L0_attn_lk2', 'L0_attn_rms_scale', 'L0_ffn_gate_w', 'L0_ffn_gate_b',
        'L0_ffn_expert_w', 'L0_ffn_expert_b']


def kernel(**inputs):
    import numpy as np
    import concourse.bacc as bacc
    from concourse.bass_utils import run_bass_kernel_spmd

    nc = bacc.Bacc("TRN2", target_bir_lowering=False, num_devices=1)
    arrays, args = {}, []
    for name in _INS:
        a = np.ascontiguousarray(inputs[name])
        arrays[name] = a
        args.append(nc.dram_tensor(name, a.shape, mybir.dt.from_np(a.dtype), kind="ExternalInput").ap())
    args.append(nc.dram_tensor("out", (B, NQ, D), F32, kind="ExternalOutput").ap())
    perceiver(nc, *args)
    return run_bass_kernel_spmd(nc, [arrays], core_ids=[0]).results[0]["out"]
```

```python
import concourse.bass as bass
from concourse import mybir
from contextlib import ExitStack

F32 = mybir.dt.float32
F16 = mybir.dt.float16
ALU = mybir.AluOpType
ACT = mybir.ActivationFunctionType
AX = mybir.AxisListType

B, NQ, D = 16, 64, 128
NCTX = 1601
H, DH = 16, 64
COLS = H * NQ
FULL = NCTX // 128
REST = NCTX - FULL * 128
TILES = FULL + 1
UNITS = TILES + 1
LAT = TILES
HALF = COLS // 2
GROUPS = 4
EPS = 1e-5
OSCALE = 1024.0
WMAX = 32768.0
QMAX = 64.0
NPB = 4
TB = 8
SH, SD = 16, 8
NE = 8


class Turn:

    def __init__(self, off, i=None, step=2):
        self.off, self.i, self.step = off, i, step

    def plus(self, d):
        return Turn(self.off + d, self.i, self.step)

    def times(self, per, add=0):
        if self.i is None:
            return per * self.off + add
        return self.i * (self.step * per) + (per * self.off + add)


class Signal:

    def __init__(self, sem, per=1):
        self.sem, self.per = sem, per

    def upto(self, turn, k=0):
        return turn.times(self.per, k + 1)


MAXIMA = 32


LONG = [(r, c) for c in range(3) for r in range(8)]
SHORT = [(r, 3) for r in range(8)]
M_ORDER = LONG[0:3] + SHORT[0:1]
for _k in range(7):
    M_ORDER += LONG[3 * _k + 3:3 * _k + 5] + SHORT[_k + 1:_k + 2] + LONG[3 * _k + 5:3 * _k + 6]
assert sorted(M_ORDER) == sorted(LONG + SHORT)


def two(k):
    return [("m", 2 * k), ("m", 2 * k + 1)]


PLAN = [([], []),
        ([], []),
        ([("q", 0), ("q", 1)], [("t", 0)]),
        ([("q", 2)], [("t", 1)]),
        ([("q", 3), ("sr", 0)], [("t", 2)]),
        ([("t", 3), ("bc", 0)], [("bc", 1)] + two(0))]
PLAN += [(two(2 * u - 11), two(2 * u - 10)) for u in range(6, 13)]
PLAN += [(two(15) + [("pj", 0), ("mt", 0)], [("mt", 1)])]
LATENTS_AT = 1


def bank_of_items():
    order = []
    for u, (early, late) in enumerate(PLAN):
        order += early + ([("ol", 0), ("ol", 1)] if u == LATENTS_AT else []) + late
    return {item: n % 2 for n, item in enumerate(order)}


BANK = bank_of_items()
assert BANK[("ol", 0)] != BANK[("ol", 1)]
STATS_AT = {0: range(0, 3), 1: range(3, 6), 2: range(6, 11), 3: range(11, 13)}
NORMALISE_AT = {6: range(0, 2), 7: range(2, 4), 8: range(4, 6), 9: range(6, 8), 10: range(8, 10), 11: range(10, 12),
                12: range(12, 13)}
OUTPUTS_HIGH_AT = {8: 0, 9: 1}
PREP = ("q", "t", "m", "mt")


def rows_of(u):
    return 128 if u < FULL else (REST if u == FULL else NQ)


def perceiver(nc, x, ctx_in, ln1_g, ln1_b, ln2_g, ln2_b, Wq, Wkv, Wo, aWq, aWk, aWv, aWo,
              lq1, lk1, lq2, lk2, rms_scale, gate_w, gate_b, expert_w, expert_b, out):
    es = ExitStack()
    with es:
        def sb(name, shape, dt=F32):
            return es.enter_context(nc.sbuf_tensor(name, shape, dt))

        def sem(name, per=1):
            return Signal(es.enter_context(nc.semaphore(name)), per)

        ident = sb("ident", [128, 128])
        ident16 = sb("ident16", [128, 128], F16)
        ones = sb("ones", [128, 128])
        ones16 = sb("ones16", [1, 64], F16)
        oscale = sb("oscale", [1, 1])
        rcol = sb("rcol", [128, 8])
        region = sb("region", [128, 10 * 1024])

        def part(start, size, dt=F32):
            v = region[:, start:start + size]
            return v if dt == F32 else v.bitcast(dt)

        wq_sb = part(0, 1024)
        wkv_sb = part(1024, 2048)
        wo_sb = part(9216, 1024).rearrange("p (n d) -> p n d", d=128)
        G = part(0, 4096).rearrange("p (h c) -> p h c", h=H)
        wqT = part(4096, 1024).rearrange("p (n d) -> p n d", d=128)
        wkT = part(5120, 2048).rearrange("p (n d) -> p n d", d=256)
        wvT = part(7168, 2048).rearrange("p (n d) -> p n d", d=256)
        q_hi = [part(2048 * p, 1024, F16) for p in range(2)]
        q_lo = [part(2048 * p + 1024, 1024, F16) for p in range(2)]
        p_hi = [part(4096 + 1024 * k, 512, F16) for k in range(NPB)]
        p_lo = [part(4608 + 1024 * k, 512, F16) for k in range(NPB)]
        o_sb = part(8192, 2048).rearrange("p (k n) -> p k n", k=2)
        A = part(0, 2048).rearrange("p (g c a m) -> p g c a m", g=4, c=4, a=2)
        E = part(2048, 2048).rearrange("p (g c a m) -> p g c a m", g=4, c=4, a=2)
        t1 = part(4096, 1024).rearrange("p (g c m) -> p g c m", g=4, c=4)
        t2 = part(5120, 1024).rearrange("p (g c m) -> p g c m", g=4, c=4)
        At = part(6144, 1024).rearrange("p (h m) -> p h m", m=64)
        AT = part(7168, 1024).rearrange("p (h n) -> p h n", n=128)
        prod = [part(8192 + 1024 * p, 1024).rearrange("p (e o) -> p e o", o=D) for p in range(2)]
        gb = sb("gb", [128, 4])
        g0row = sb("g0row", [1, 2, 1])
        fold = sb("fold", [128, 2, 128])
        G_hi = sb("G_hi", [128, H, 256], F16)
        G_lo = sb("G_lo", [128, H, 256], F16)
        WO_hi = sb("WO_hi", [128, H, 256], F16)
        WO_lo = sb("WO_lo", [128, H, 256], F16)
        amax = sb("amax", [128, 6])
        sigma = sb("sigma", [128, 2])
        wscale = sb("wscale", [128, 2])
        lx = sb("lx", [NQ, B, D])
        lk_hi = sb("lk_hi", [NQ, B, D], F16)
        lk_lo = sb("lk_lo", [NQ, B, D], F16)
        lT = sb("lT", [128, B * NQ])
        lT_hi = sb("lT_hi", [128, B * NQ], F16)
        lT_lo = sb("lT_lo", [128, B * NQ], F16)
        cT_hi = [sb(f"cT_hi{p}", [128, NQ], F16) for p in range(2)]
        cT_lo = [sb(f"cT_lo{p}", [128, NQ], F16) for p in range(2)]
        ck_hi = [sb(f"ck_hi{p}", [NQ, D], F16) for p in range(2)]
        ck_lo = [sb(f"ck_lo{p}", [NQ, D], F16) for p in range(2)]
        raw = [sb(f"raw{p}", [128, TILES, D]) for p in range(2)]
        xk_hi = [sb(f"xk_hi{p}", [128, TILES, D], F16) for p in range(2)]
        xk_lo = [sb(f"xk_lo{p}", [128, TILES, D], F16) for p in range(2)]
        xT_hi = [sb(f"xT_hi{p}", [128, TILES * 128], F16) for p in range(2)]
        xT_lo = [sb(f"xT_lo{p}", [128, TILES * 128], F16) for p in range(2)]
        srow = sb("srow", [1, COLS])
        attnT = sb("attnT", [128, B * NQ])
        st = sb("st", [128, 16, 6])
        sm = sb("sm", [128, 8, 16])
        stc = sb("stc", [128, TILES, 6])
        smc = sb("smc", [128, 8, TILES])
        carrier = sb("carrier", [1, 16])
        mhalf = sb("mhalf", [128, 16])
        mx = sb("mx", [128, 8, 4])
        m16 = sb("m16", [128, 8], F16)
        xres = sb("xres", [128, TB, D])
        hn = sb("hn", [128, TB, D])
        diag = xres[:].rearrange("p (k j) n -> p k j n", k=2)
        rb = hn[:].rearrange("p t d -> p (t d)")
        hT = lT
        wpad = sb("wpad", [128, 3, 4, 128])
        wpadT = sb("wpadT", [128, 3, 4, 128])
        wv_sb = sb("wv_sb", [128, 2, 128])
        wvaT = sb("wvaT", [128, 256])
        woa_sb = sb("woa_sb", [128, 256])
        woaT = sb("woaT", [128, 2, 128])
        rmsc = sb("rmsc", [128, 1])
        lv = sb("lv", [128, 4, 128])
        lp = sb("lp", [128, 2, 128])
        lsum = sb("lsum", [128, 2, SH])
        lexp = sb("lexp", [128, 2, SH])
        nlam = sb("nlam", [128, SH])
        mask = sb("mask", [128, NQ])
        gw_sb = sb("gw_sb", [NE, 128])
        gwT = sb("gwT", [128, NE])
        gbias = sb("gbias", [128, NE])
        ew = sb("ew", [128, NE, 128])
        o_hi = lT[:].bitcast(F16).rearrange("p (c n) -> p c n", c=2)
        o_lo = ew[:].rearrange("p e o -> p (e o)").bitcast(F16).rearrange("p (c n) -> p c n", c=2)
        eb = sb("eb", [NE, 128])

        S = es.enter_context(nc.psum_tensor("S", [128, 4, 512], F32))
        OA = es.enter_context(nc.psum_tensor("OA", [128, 2, 512], F32))
        W = [es.enter_context(nc.psum_tensor(f"W{k}", [128, 512], F32)) for k in range(2)]

        ld_w = sem("ld_w")
        ld_gb = sem("ld_gb")
        ld_x = sem("ld_x")
        ld_res = sem("ld_res")
        ld_raw = [sem(f"ld_raw{p}") for p in range(2)]
        ld_a = sem("ld_a")
        ld_ew = sem("ld_ew")
        consts = sem("consts")
        padded = sem("padded")
        pool_link = sem("pool_link")
        dve_link = sem("dve_link")
        folded = sem("folded")
        pe_w = sem("pe_w")
        ev_w = sem("ev_w")
        amax_rdy = sem("amax_rdy")
        wscale_rdy = sem("wscale_rdy")
        wo_lo_done = sem("wo_lo_done")
        g_hi_rdy = sem("g_hi_rdy")
        sigma_rdy = sem("sigma_rdy")
        amax_all = sem("amax_all")
        g_rdy = sem("g_rdy")
        var_rdy = sem("var_rdy")
        rstd_rdy = sem("rstd_rdy")
        rstd_ctx = sem("rstd_ctx")
        lat_rdy = sem("lat_rdy")
        lat_t = sem("lat_t")
        lat_cp = sem("lat_cp")
        lat_hi = sem("lat_hi")
        lat_lo = sem("lat_lo")
        rstd_step = sem("rstd_step")
        s_done = sem("s_done", UNITS)
        e_done = sem("e_done", UNITS)
        lo_done = sem("lo_done", UNITS)
        pv_done = sem("pv_done", UNITS)
        oa_free = sem("oa_free")
        pe_item = {k: sem("pe_" + k, n) for k, n in
                   (("q", 4), ("t", 4), ("m", MAXIMA), ("mt", 2), ("sr", 1), ("bc", 2), ("pj", 1))}
        q_hi_done = sem("q_hi_done", 4)
        free = {"q": sem("q_lo_done", 4), "t": sem("t_copied", 4), "m": sem("m_reduced", MAXIMA),
                "mt": sem("m_row", 2), "ol": sem("ol_copied", 2), "sr": sem("recip_done"),
                "bc": sem("rb_copied", 2), "pj": sem("pj_copied", 1)}
        diag_done = sem("diag_done", 2)
        o_normed = sem("o_normed", 2)
        o_hi_done = sem("o_hi_done", 2)
        o_split = sem("o_split", 2)
        stats_ok = sem("stats_ok")
        normed = sem("normed")
        split_hi = sem("split_hi", GROUPS)
        split = sem("split", GROUPS)
        curT = sem("curT")
        curk = sem("curk")
        m16_done = sem("m16_done")
        srow_done = sem("srow_done")
        dve_step = sem("dve_step", 4)

        def pbuf(turn, u):
            return (2 * (turn.off % 2) + u) % NPB

        def score_bank(u, half):
            return S[:, 2 * (u % 2) + half, :]

        def load_raw(sp, turn):
            p = turn.off % 2
            b = turn.times(1)
            first = ctx_in[bass.ds(b, 1), 0:FULL * 128, :] if turn.i is not None else ctx_in[b:b + 1, 0:FULL * 128, :]
            last = ctx_in[bass.ds(b, 1), FULL * 128:NCTX, :] if turn.i is not None else ctx_in[b:b + 1, FULL * 128:NCTX, :]
            sp.dma_start(raw[p][:, 0:FULL, :],
                         first.rearrange("o (p t) d -> p (o t) d", t=FULL)).then_inc(ld_raw[p].sem, 16)
            sp.dma_start(raw[p][0:REST, FULL, :],
                         last.rearrange("o p d -> p (o d)")).then_inc(ld_raw[p].sem, 16)

        FOLDS = 3 * H // 2
        fold_banks = [W[0][:, 0:256], W[1][:, 0:256], OA[:, 0, 0:256], OA[:, 1, 0:256]]

        def fold_bank(n):
            return fold_banks[n % 4]

        wo_banks = [OA[:, 0, 0:256], OA[:, 1, 0:256], S[:, 2, 0:256], S[:, 3, 0:256]]
        WO_AFTER = {2 * h + 1: h for h in range(H)}
        SMALL_AFTER = {7 + 6 * g: g for g in range(5)}

        LD_A = 16 * (12 + 2 + 4 + 8 + 3)

        def stats_combine(P, n, link, half=0.5, st=st, sm=sm):
            mean_e, var_e, mean_o, var_o = (st[0:P, 0:n, k] for k in (1, 2, 4, 5))
            c = lambda k: sm[0:P, k, 0:n]
            nc.vector.tensor_tensor(c(2), mean_e, mean_o, ALU.subtract)
            nc.vector.tensor_tensor(c(3), var_e, var_o, ALU.add)
            link(nc.vector.tensor_tensor(c(4), mean_e, mean_o, ALU.add))
            nc.vector.tensor_scalar(c(0), c(4), half, None, ALU.mult)
            link(nc.vector.tensor_tensor(c(5), c(2), c(2), ALU.mult))
            link(nc.vector.scalar_tensor_tensor(c(6), c(5), 32.0, c(3), ALU.mult, ALU.add))
            return nc.vector.tensor_scalar(c(7), c(6), 1.0 / D, EPS, ALU.mult, ALU.add)

        def bn(turn, t):
            r = rows_of(t)
            return nc.vector.bn_stats(stc[0:r, t, :], raw[turn.off % 2][0:r, t, :])

        def token_group(t, turn, g):
            if g < 3:
                return t[turn.off % 2][:, 4 * g:4 * g + 4, 1:D]
            return t[turn.off % 2][0:REST, FULL:TILES, 1:D]

        def raw_loaded(turn):
            return (turn.i * 32 if turn.i is not None else 0) + 32 * (turn.off // 2) + 32

        hTd = sb("hTd", [128, 2, 2, 64])
        Qs = sb("Qs", [128, 4, 128])
        Ks = sb("Ks", [128, 4, 2, 2, 64])
        Vb = sb("Vb", [128, 2, 8, 32])
        amx = sb("amx", [128, 4, 4, 2])
        asum = sb("asum", [128, 4, 4, 2])
        arc = sb("arc", [128, 4, 4, 2])
        Ob = sb("Ob", [128, 256])
        Osq = sb("Osq", [128, 256])
        Oc = sb("Oc", [128, 256])
        oms = sb("oms", [128, 3, SH])
        OcT = sb("OcT", [128, 2, 128])
        lg = sb("lg", [128, 10, TB, NE])
        g1 = sb("g1", [128, 4, TB])
        rank = sb("rank", [128, NE])
        gT = AT[:].rearrange("p h n -> p (h n)")[0:NE, :]
        xb = attnT[:].rearrange("p (t d) -> p t d", d=D)
        ta = {n: sem("ta_" + n) for n in (
            "x1t", "x1", "h", "ht", "hcopy",
            "hd", "projqk", "projv", "qk1", "k2", "vb", "scores", "masked", "max", "shifted", "exp", "r", "r2",
            "t1", "t2", "sums", "attn", "at_t", "at", "pv", "ob", "sq", "ms", "ms2", "ms3", "oc", "oct_t", "oct", "proj_o",
            "x2", "h2", "h2t", "h2copy", "logits", "gexp_in", "gexp", "gates", "gates_t", "gt")}
        ex_mm, ex_prod, ex_b, ex_add, ex_out = (sem("ex_" + n) for n in ("mm", "prod", "xb", "add", "out"))
        tail_dve = sem("tail_dve")
        tail_pool = sem("tail_pool")
        wt_t, wt_c = sem("wt_t"), sem("wt_c")
        lam_in, lam_exp = sem("lam_in"), sem("lam_exp")
        rms_rdy = sem("rms_rdy")
        LAST = Turn(B - 1)

        def carry(pool, turn, site):
            if turn.i is not None:
                nc.gpsimd.tensor_tensor(carrier[:, site:site + 1], carrier[:, 14:15], carrier[:, 15:16], ALU.mult)

        def inverse_deviation(pool, n):
            pool.wait_ge(var_rdy.sem, n + 1)
            nc.gpsimd.tensor_tensor(sm[:, 1, :], sm[:, 7, :], mhalf[:], ALU.pow).then_inc(rstd_rdy.sem, 1)

        def layer_norm(dve, link, n, turn_no):
            for t in range(n):
                ins = nc.vector.bn_stats(st[:, t, :], xres[:, t, :])
            link(ins)
            stats_combine(128, n, link).then_inc(var_rdy.sem, 1)
            dve.wait_ge(rstd_rdy.sem, turn_no)
            for t in range(n):
                ins = nc.vector.tensor_scalar(hn[:, t, :], xres[:, t, :], sm[:, 0, t:t + 1], sm[:, 1, t:t + 1],
                                              ALU.subtract, ALU.mult)
            return ins

        def small_weights_vector(dve, link):
            dve.wait_ge(ld_a.sem, LD_A)
            for k in range(2):
                ins = nc.vector.tensor_tensor(lp[:, k, :], lv[:, 2 * k, :], lv[:, 2 * k + 1, :], ALU.mult)
            link(ins)
            nc.vector.tensor_reduce(lsum[:], lp[:].rearrange("p k (h d) -> p k h d", d=SD), AX.X, ALU.add)\
              .then_inc(lam_in.sem, 1)
            nc.vector.tensor_scalar(rmsc[:], rmsc[:], 1.0 - 0.8, None, ALU.mult).then_inc(rms_rdy.sem, 1)
            nc.vector.memset(Vb[:].rearrange("p a b c -> p (a b c)"), 0.0)
            for e in range(NE):
                ins = nc.vector.memset(rank[:, e:e + 1], float(NE - e))
            link(ins)

        def lambdas_vector(dve, link):
            dve.wait_ge(lam_exp.sem, 1)
            link(nc.vector.tensor_tensor(nlam[:], lexp[:, 1, :], lexp[:, 0, :], ALU.subtract))
            link(nc.vector.tensor_scalar(nlam[:], nlam[:], -0.8, None, ALU.add))

        def small_weights_tensor(pe, g):
            if g == 0:
                pe.wait_ge(ld_a.sem, LD_A)
            if g >= 2:
                pe.wait_ge(wt_c.sem, g - 1)
            w = S[:, g % 2, :]
            if g < 3:
                for c in range(4):
                    ins = nc.tensor.transpose(w[:, 128 * c:128 * c + 128], wpad[:, g, c, :], ident[:])
            if g == 3:
                for c in range(2):
                    nc.tensor.transpose(w[:, 128 * c:128 * c + 128], wv_sb[:, c, :], ident[:])
                    ins = nc.tensor.transpose(w[:, 256 + 128 * c:384 + 128 * c], woa_sb[:, 128 * c:128 * c + 128],
                                              ident[:])
            if g == 4:
                ins = nc.tensor.transpose(w[:, 0:NE], gw_sb[:], ident[0:NE, 0:NE])
            ins.then_inc(wt_t.sem, 1)

        def small_weights_scalar(act, g):
            if g == 0:
                act.wait_ge(lam_in.sem, 1)
                nc.scalar.activation(lexp[:], lsum[:], ACT.Exp).then_inc(lam_exp.sem, 1)
            act.wait_ge(wt_t.sem, g + 1)
            w = S[:, g % 2, :]
            if g < 3:
                ins = nc.scalar.copy(wpadT[:, g, :, :].rearrange("p c n -> p (c n)"), w)
            if g == 3:
                act.wait_ge(rms_rdy.sem, 1)
                nc.scalar.copy(wvaT[:], w[:, 0:256])
                ins = nc.scalar.activation(woaT[:].rearrange("p c n -> p (c n)"), w[:, 256:512], ACT.Copy,
                                           scale=rmsc[:])
            if g == 4:
                ins = nc.scalar.copy(gwT[:], w[:, 0:NE])
            ins.then_inc(wt_c.sem, 1)

        def tile_cols(t, turn):
            if turn.i is None:
                return t[:, 128 * turn.off:128 * turn.off + 128]
            return t[:, bass.ds(turn.times(128), 128)]

        def tile_of(t, turn):
            if turn.i is None:
                return t[:, turn.off, :]
            return t[:, bass.ds(turn.times(1), 1), :].rearrange("p o d -> p (o d)")

        def wait(eng, name, turn):
            eng.wait_ge(ta[name].sem, ta[name].upto(turn))

        def first(turn):
            return turn.i is None and turn.off == 0

        def more(turn):
            return turn.i is not None or turn.off < TB - 1

        def bc(ap, n):
            return ap.unsqueeze(len(ap.shape)).to_broadcast(list(ap.shape) + [n])

        def tail_vector(dve):
            chain = [0]

            def link(ins):
                chain[0] += 1
                ins.then_inc(tail_dve.sem, 1)
                dve.wait_ge(tail_dve.sem, chain[0])

            wait(dve, "x1t", Turn(0))
            dve.wait_ge(ld_res.sem, 16)
            xf = xres[:].rearrange("p t d -> p (t d)")
            link(nc.vector.tensor_tensor(xf, S[:, 0:2, :].rearrange("p a n -> p (a n)"), xf, ALU.add))
            layer_norm(dve, link, TB, 3).then_inc(ta["h"].sem, 1)

            def keys2(t):
                wait(dve, "projqk", t)
                nc.vector.tensor_copy(Ks[:, :, :, 1, :], W[0][:].rearrange("p (c j m) -> p c j m", c=4, j=2))\
                  .then_inc(ta["k2"].sem, 1)

            def masked_scores(t):
                wait(dve, "scores", t)
                nc.vector.scalar_tensor_tensor(
                    A[:].rearrange("p g c a m -> p (g c a) m"),
                    S[:].rearrange("p g (k m) -> p (g k) m", m=64), SD ** -0.5,
                    mask[:].unsqueeze(1).to_broadcast([128, 32, 64]), ALU.mult, ALU.add).then_inc(ta["masked"].sem, 1)
                wait(dve, "masked", t)
                if not first(t):
                    wait(dve, "shifted", t.plus(-1))
                nc.vector.tensor_reduce(amx[:].rearrange("p g c a -> p (g c a)"),
                                        A[:].rearrange("p g c a m -> p (g c a) m"), AX.X, ALU.max)\
                  .then_inc(ta["max"].sem, 1)

            def attention(t):
                wait(dve, "exp", t)
                nc.vector.tensor_reduce(asum[:].rearrange("p g c a -> p (g c a)"),
                                        E[:].rearrange("p g c a m -> p (g c a) m"), AX.X, ALU.add)\
                  .then_inc(ta["sums"].sem, 1)
                wait(dve, "sums", t)
                if not first(t):
                    wait(dve, "t2", t.plus(-1))
                nc.vector.reciprocal(arc[:], asum[:]).then_inc(ta["r"].sem, 1)
                wait(dve, "r", t)
                nc.vector.tensor_tensor(arc[:, :, :, 1], arc[:, :, :, 1], nlam[:].rearrange("p (c g) -> p g c", c=4),
                                        ALU.mult).then_inc(ta["r2"].sem, 1)
                nc.vector.tensor_tensor(t1[:], E[:, :, :, 0, :], bc(arc[:, :, :, 0], 64), ALU.mult)\
                  .then_inc(ta["t1"].sem, 1)
                wait(dve, "t1", t)
                wait(dve, "t2", t)
                if not first(t):
                    wait(dve, "at_t", t.plus(-1))
                nc.vector.tensor_tensor(At[:].rearrange("p (c g) m -> p g c m", c=4), t1[:], t2[:], ALU.add)\
                  .then_inc(ta["attn"].sem, 1)

            def group_norm(t):
                wait(dve, "ob", t)
                nc.vector.tensor_tensor(Osq[:], Ob[:], Ob[:], ALU.mult).then_inc(ta["sq"].sem, 1)
                wait(dve, "sq", t)
                nc.vector.tensor_reduce(oms[:, 0, :], Osq[:].rearrange("p (h d) -> p h d", h=SH), AX.X, ALU.add)\
                  .then_inc(ta["ms"].sem, 1)
                wait(dve, "ms", t)
                nc.vector.tensor_scalar(oms[:, 1, :], oms[:, 0, :], 1.0 / (2 * SD), EPS, ALU.mult, ALU.add)\
                  .then_inc(ta["ms2"].sem, 1)
                wait(dve, "ms3", t)
                if not first(t):
                    wait(dve, "oct_t", t.plus(-1))
                nc.vector.tensor_tensor(Oc[:].rearrange("p (h d) -> p h d", h=SH),
                                        Ob[:].rearrange("p (h d) -> p h d", h=SH), bc(oms[:, 2, :], 2 * SD),
                                        ALU.mult).then_inc(ta["oc"].sem, 1)

            def residual(t):
                wait(dve, "proj_o", t)
                nc.vector.tensor_tensor(tile_of(xres, t), W[0][:, 0:128], tile_of(xres, t), ALU.add)\
                  .then_inc(ta["x2"].sem, 1)

            keys2(Turn(0))
            masked_scores(Turn(0))
            def middle(t):
                keys2(t.plus(1))
                attention(t)
                masked_scores(t.plus(1))
                group_norm(t)
                residual(t)
            middle(Turn(0))
            with dve.Fori(0, TB - 2) as i:
                middle(Turn(1, i, 1))
            t = Turn(TB - 1)
            attention(t)
            group_norm(t)
            residual(t)
            wait(dve, "x2", t)
            layer_norm(dve, link, TB, 4).then_inc(ta["h2"].sem, 1)

            L = lambda k: lg[:, k, :, :]
            rk = rank[:].unsqueeze(1).to_broadcast([128, TB, NE])
            wait(dve, "logits", Turn(0))
            link(nc.vector.tensor_tensor(L(0), W[0][:, 0:64].rearrange("p (t e) -> p t e", t=TB),
                                         gbias[:].unsqueeze(1).to_broadcast([128, TB, NE]), ALU.add))

            def largest(src, dst, tmp, mxi, m2i):
                link(nc.vector.tensor_reduce(g1[:, mxi, :], src, AX.X, ALU.max))
                link(nc.vector.tensor_tensor(tmp, src, bc(g1[:, mxi, :], NE), ALU.is_equal))
                link(nc.vector.tensor_tensor(tmp, tmp, rk, ALU.mult))
                link(nc.vector.tensor_reduce(g1[:, m2i, :], tmp, AX.X, ALU.max))
                link(nc.vector.tensor_tensor(dst, tmp, bc(g1[:, m2i, :], NE), ALU.is_equal))

            largest(L(0), L(1), L(2), 0, 1)
            nc.vector.tensor_tensor(L(8), L(0), bc(g1[:, 0, :], NE), ALU.subtract).then_inc(ta["gexp_in"].sem, 1)
            link(nc.vector.scalar_tensor_tensor(L(3), L(1), -3e38, L(0), ALU.mult, ALU.add))
            largest(L(3), L(4), L(2), 2, 1)
            link(nc.vector.tensor_tensor(L(5), L(1), L(4), ALU.add))
            wait(dve, "gexp", Turn(0))
            link(nc.vector.tensor_tensor(L(6), L(9), L(5), ALU.mult))
            link(nc.vector.tensor_reduce(g1[:, 3, :], L(6), AX.X, ALU.add))
            link(nc.vector.reciprocal(g1[:, 2, :], g1[:, 3, :]))
            link(nc.vector.tensor_tensor(L(7), L(6), bc(g1[:, 2, :], NE), ALU.mult))
            nc.vector.tensor_copy(L(8), L(7)).then_inc(ta["gates"].sem, 1)
            for t in range(TB):
                dve.wait_ge(ex_mm.sem, t + 1)
                if t >= 2:
                    dve.wait_ge(ex_add.sem, t - 1)
                nc.vector.tensor_tensor(prod[t % 2][:], S[:, 2 * (t % 2):2 * (t % 2) + 2, :].rearrange(
                    "p a (e o) -> p (a e) o", o=D), bc(lg[:, 7, t, :], D), ALU.mult).then_inc(ex_prod.sem, 1)
                nc.vector.tensor_tensor(xb[:, t, :], W[t % 2][:, 0:128], xres[:, t, :], ALU.add).then_inc(ex_b.sem, 1)

        def tail_gpsimd(pool):
            def columns(t):
                wait(pool, "hcopy", Turn(0))
                if not first(t):
                    wait(pool, "projv", t.plus(-1))
                src = tile_cols(hT, t).rearrange("p (j n) -> p j n", j=2)
                carry(pool, t, 0 + 0)
                nc.gpsimd.tensor_copy(hTd[:, :, 0, :], src)
                nc.gpsimd.tensor_copy(hTd[:, :, 1, :], src).then_inc(ta["hd"].sem, 1)

            def shift(t):
                wait(pool, "max", t)
                nc.gpsimd.tensor_tensor(A[:], A[:], bc(amx[:], 64), ALU.subtract).then_inc(ta["shifted"].sem, 1)

            def second_map(t):
                wait(pool, "r2", t)
                nc.gpsimd.tensor_tensor(t2[:], E[:, :, :, 1, :], bc(arc[:, :, :, 1], 64), ALU.mult)\
                  .then_inc(ta["t2"].sem, 1)

            def inverse_rms(t):
                wait(pool, "ms2", t)
                nc.gpsimd.tensor_tensor(oms[:, 2, :], oms[:, 1, :], mhalf[:], ALU.pow).then_inc(ta["ms3"].sem, 1)

            inverse_deviation(pool, 2)
            columns(Turn(0))
            shift(Turn(0))
            def middle(t):
                columns(t.plus(1))
                second_map(t)
                shift(t.plus(1))
                inverse_rms(t)
            middle(Turn(0))
            with pool.Fori(0, TB - 2) as i:
                middle(Turn(1, i, 1))
            second_map(Turn(TB - 1))
            inverse_rms(Turn(TB - 1))
            inverse_deviation(pool, 3)
            n = 0
            for t in range(TB):
                pool.wait_ge(ex_prod.sem, t + 1)
                pr = prod[t % 2]
                for m in (4, 2, 1):
                    nc.gpsimd.tensor_tensor(pr[:, 0:m, :], pr[:, 0:m, :], pr[:, m:2 * m, :], ALU.add)\
                      .then_inc(tail_pool.sem, 1)
                    n += 1
                    pool.wait_ge(tail_pool.sem, n)
                pool.wait_ge(ex_b.sem, t + 1)
                nc.gpsimd.tensor_tensor(xb[:, t, :], xb[:, t, :], pr[:, 0, :], ALU.add).then_inc(ex_add.sem, 1)

        def tail_scalar(act):
            act.wait_ge(ta["ht"].sem, 1)
            nc.scalar.copy(hT[:], S[:, 2:4, :].rearrange("p a n -> p (a n)")).then_inc(ta["hcopy"].sem, 1)

            def queries_keys(t):
                wait(act, "projqk", t)
                nc.scalar.copy(Qs[:].rearrange("p c n -> p (c n)"), OA[:, 0, :])
                nc.scalar.copy(Ks[:, :, :, 0, :], OA[:, 1, :].rearrange("p (c j m) -> p c j m", c=4, j=2))\
                  .then_inc(ta["qk1"].sem, 1)

            def values(t):
                wait(act, "projv", t)
                if first(t):
                    act.wait_ge(ld_a.sem, LD_A)
                v = W[1][:].rearrange("p (j h d) -> p j h d", j=2, h=8)
                nc.scalar.copy(Vb[0:64, :, :, 0:16], v[0:64, :, :, 0:16])
                nc.scalar.copy(Vb[64:128, :, :, 16:32], v[64:128, :, :, 16:32]).then_inc(ta["vb"].sem, 1)

            def exp(t):
                wait(act, "shifted", t)
                if not first(t):
                    wait(act, "attn", t.plus(-1))
                nc.scalar.activation(E[:].rearrange("p g c a m -> p (g c a m)"),
                                     A[:].rearrange("p g c a m -> p (g c a m)"), ACT.Exp).then_inc(ta["exp"].sem, 1)

            def weights(t):
                wait(act, "at_t", t)
                nc.scalar.copy(AT[:].rearrange("p h n -> p (h n)"), OA[:].rearrange("p a n -> p (a n)"))\
                  .then_inc(ta["at"].sem, 1)
                wait(act, "pv", t)
                nc.scalar.copy(Ob[:], W[0][:, 0:256]).then_inc(ta["ob"].sem, 1)

            def columns_out(t):
                wait(act, "oct_t", t)
                nc.scalar.copy(OcT[:].rearrange("p c n -> p (c n)"), W[1][:, 0:256]).then_inc(ta["oct"].sem, 1)

            queries_keys(Turn(0))
            values(Turn(0))
            exp(Turn(0))
            def middle(t):
                queries_keys(t.plus(1))
                weights(t)
                values(t.plus(1))
                columns_out(t)
                exp(t.plus(1))
            middle(Turn(0))
            with act.Fori(0, TB - 2) as i:
                middle(Turn(1, i, 1))
            weights(Turn(TB - 1))
            columns_out(Turn(TB - 1))
            wait(act, "h2t", Turn(0))
            nc.scalar.copy(hT[:], S[:, 0:2, :].rearrange("p a n -> p (a n)")).then_inc(ta["h2copy"].sem, 1)
            wait(act, "gexp_in", Turn(0))
            nc.scalar.activation(lg[:, 9, :, :], lg[:, 8, :, :], ACT.Exp).then_inc(ta["gexp"].sem, 1)
            wait(act, "gates_t", Turn(0))
            nc.scalar.copy(gT[:], OA[0:NE, :, :].rearrange("p a n -> p (a n)")).then_inc(ta["gt"].sem, 1)

        def tail_tensor(pe):
            mm = nc.tensor.matmul
            pe.wait_ge(free["pj"].sem, free["pj"].upto(LAST))
            pe.wait_ge(lo_done.sem, lo_done.upto(LAST, LAT))
            for t in range(TB):
                ins = nc.tensor.transpose(S[:, t // 4, 128 * (t % 4):128 * (t % 4) + 128],
                                          attnT[:, 128 * t:128 * t + 128], ident[:])
            ins.then_inc(ta["x1t"].sem, 1)
            wait(pe, "h", Turn(0))
            for t in range(TB):
                ins = nc.tensor.transpose(S[:, 2 + t // 4, 128 * (t % 4):128 * (t % 4) + 128], hn[:, t, :], ident[:])
            ins.then_inc(ta["ht"].sem, 1)

            def project(t):
                wait(pe, "hd", t)
                if t.i is not None or t.off >= 2:
                    wait(pe, "at", t.plus(-2))
                    wait(pe, "x2", t.plus(-2))
                if first(t):
                    pe.wait_ge(free["bc"].sem, free["bc"].upto(LAST, 1))
                for kind, dst in enumerate((OA[:, 0, :], OA[:, 1, :], W[0][:])):
                    for c in range(4):
                        ins = mm(dst[:, 128 * c:128 * c + 128], wpadT[:, kind, c, :], hTd[:, :, 0, :],
                                 start=True, stop=True)
                ins.then_inc(ta["projqk"].sem, 1)

            def project_values(t):
                if t.i is not None or t.off >= 2:
                    wait(pe, "oct", t.plus(-2))
                for j in range(2):
                    ins = mm(W[1][:, 256 * j:256 * j + 256], hTd[:, j, :, :].rearrange("p a n -> p (a n)"), wvaT[:],
                             start=True, stop=True)
                ins.then_inc(ta["projv"].sem, 1)

            def self_scores(t):
                wait(pe, "qk1", t)
                wait(pe, "k2", t)
                if not first(t):
                    wait(pe, "masked", t.plus(-1))
                else:
                    wait(pe, "hcopy", t)
                for c in range(4):
                    for j in range(2):
                        for g in range(4):
                            r = slice(32 * g, 32 * g + 32)
                            ins = mm(S[64 * j:64 * j + 64, g, 128 * c:128 * c + 128], Qs[r, c, 64 * j:64 * j + 64],
                                     Ks[r, c, j, :, :].rearrange("p a m -> p (a m)"), start=True, stop=True,
                                     tile_position=(32 * g, 64 * j))
                ins.then_inc(ta["scores"].sem, 1)

            def transpose_attention(t):
                wait(pe, "attn", t)
                if more(t):
                    wait(pe, "qk1", t.plus(1))
                for h in range(8):
                    ins = nc.tensor.transpose(OA[:, h // 4, 128 * (h % 4):128 * (h % 4) + 128],
                                              At[:, 2 * h:2 * h + 2, :].rearrange("p a m -> p (a m)"), ident[:])
                ins.then_inc(ta["at_t"].sem, 1)

            def weigh_values(t):
                wait(pe, "at", t)
                wait(pe, "vb", t)
                if more(t):
                    wait(pe, "k2", t.plus(1))
                else:
                    wait(pe, "x2", t.plus(-1))
                for j in range(2):
                    for h in range(8):
                        ins = mm(W[0][64 * j:64 * j + 64, 32 * h:32 * h + 32], AT[:, h, 64 * j:64 * j + 64],
                                 Vb[:, j, h, :], start=True, stop=True)
                ins.then_inc(ta["pv"].sem, 1)

            def project_out(t):
                wait(pe, "oc", t)
                if more(t):
                    wait(pe, "vb", t.plus(1))
                for c in range(2):
                    ins = nc.tensor.transpose(W[1][:, 128 * c:128 * c + 128], Oc[:, 128 * c:128 * c + 128], ident[:])
                ins.then_inc(ta["oct_t"].sem, 1)
                wait(pe, "oct", t)
                wait(pe, "ob", t)
                for c in range(2):
                    ins = mm(W[0][:, 0:128], OcT[:, c, :], woaT[:, c, :], start=(c == 0), stop=(c == 1))
                ins.then_inc(ta["proj_o"].sem, 1)

            project(Turn(0))
            self_scores(Turn(0))
            project_values(Turn(0))
            def middle(t):
                project(t.plus(1))
                self_scores(t.plus(1))
                transpose_attention(t)
                weigh_values(t)
                project_values(t.plus(1))
                project_out(t)
            middle(Turn(0))
            with pe.Fori(0, TB - 2) as i:
                middle(Turn(1, i, 1))
            t = Turn(TB - 1)
            transpose_attention(t)
            weigh_values(t)
            project_out(t)

            wait(pe, "h2", Turn(0))
            wait(pe, "masked", Turn(TB - 1))
            for t in range(TB):
                ins = nc.tensor.transpose(S[:, t // 4, 128 * (t % 4):128 * (t % 4) + 128], hn[:, t, :], ident[:])
            ins.then_inc(ta["h2t"].sem, 1)
            wait(pe, "h2copy", Turn(0))
            wait(pe, "x2", Turn(TB - 1))
            for t in range(TB):
                ins = mm(W[0][:, NE * t:NE * t + NE], hT[:, 128 * t:128 * t + 128], gwT[:], start=True, stop=True)
            ins.then_inc(ta["logits"].sem, 1)

            def experts(t):
                if t >= 2:
                    pe.wait_ge(ex_prod.sem, t - 1)
                for c in range(2):
                    mm(S[:, 2 * (t % 2) + c, :], hT[:, 128 * t:128 * t + 128],
                       ew[:, 4 * c:4 * c + 4, :].rearrange("p e o -> p (e o)"), start=True, stop=True)

            def expert_bias(t):
                if t >= 2:
                    pe.wait_ge(ex_b.sem, t - 1)
                mm(W[t % 2][:, 0:128], gT[:, 128 * t:128 * t + 128], eb[:], start=True, stop=True)\
                    .then_inc(ex_mm.sem, 1)

            pe.wait_ge(ld_ew.sem, 16)
            experts(0)
            experts(1)
            wait(pe, "gates", Turn(0))
            for t in range(TB):
                ins = nc.tensor.transpose(OA[0:NE, t // 4, 128 * (t % 4):128 * (t % 4) + 128], lg[:, 8, t, :], ident[:])
            ins.then_inc(ta["gates_t"].sem, 1)
            wait(pe, "gt", Turn(0))
            expert_bias(0)
            expert_bias(1)
            for t in range(2, TB):
                experts(t)
                expert_bias(t)


        block = es.enter_context(nc.Block())

        @block.sync
        def _(sp):
            with nc.allow_non_contiguous_dma(reason="columns of gains and biases"):
                for k, v in enumerate((ln1_g, ln1_b, ln2_g, ln2_b)):
                    sp.dma_start(gb[:, k:k + 1], v.rearrange("(p o) -> p o", o=1)).then_inc(ld_gb.sem, 16)
                for k, v in enumerate((ln1_g, ln2_g)):
                    sp.dma_start(g0row[0:1, k, :], v[0:1].rearrange("(o n) -> o n", o=1)).then_inc(ld_gb.sem, 16)
            sp.dma_start(lx[:], x.rearrange("b q d -> q b d")).then_inc(ld_x.sem, 16)
            sp.dma_start(wq_sb[:], Wq).then_inc(ld_w.sem, 16)
            sp.dma_start(wkv_sb[:], Wkv).then_inc(ld_w.sem, 16)
            sp.dma_start(wo_sb[:], Wo.rearrange("(n p) d -> p n d", p=128)).then_inc(ld_w.sem, 16)
            load_raw(sp, Turn(0))
            load_raw(sp, Turn(1))
            sp.wait_ge(padded.sem, 1)
            for j in range(4):
                for kind, wt, r0, r1 in ((0, aWq, 0, 16), (1, aWk, 0, 8), (2, aWk, 8, 16)):
                    src = wt.rearrange("(c j k) d -> j k c d", c=4, j=4)[j, r0:r1]
                    sp.dma_start(wpad[32 * j + r0:32 * j + r1, kind, :, :], src).then_inc(ld_a.sem, 16)
            sp.dma_start(wv_sb[:], aWv.rearrange("(c p) d -> p c d", p=128)).then_inc(ld_a.sem, 16)
            sp.dma_start(woa_sb[:], aWo).then_inc(ld_a.sem, 16)
            for k, v in enumerate((lq1, lk1, lq2, lk2)):
                sp.dma_start(lv[:, k, :], v.rearrange("h (o d) -> o (h d)", o=1).to_broadcast([128, 128]))\
                  .then_inc(ld_a.sem, 16)
            with nc.allow_non_contiguous_dma(reason="one scale per row"):
                for h in range(8):
                    sp.dma_start(rmsc[16 * h:16 * h + 16, :], rms_scale.rearrange("(p o) -> p o", o=1))\
                      .then_inc(ld_a.sem, 16)
            sp.dma_start(gw_sb[:], gate_w).then_inc(ld_a.sem, 16)
            sp.dma_start(gbias[:], gate_b.rearrange("(o e) -> o e", o=1).to_broadcast([128, NE])).then_inc(ld_a.sem, 16)
            sp.dma_start(eb[:], expert_b).then_inc(ld_a.sem, 16)

            with sp.Fori(0, B // 2 - 1) as i:
                for off in (2, 3):
                    n = Turn(off, i)
                    sp.wait_ge(split.sem, split.upto(n.plus(-2), GROUPS - 1))
                    load_raw(sp, n)

            sp.wait_ge(pe_item["bc"].sem, pe_item["bc"].upto(LAST, 1))
            sp.dma_start(xres[:], x.rearrange("(t j) q d -> (j q) t d", j=2)).then_inc(ld_res.sem, 16)
            sp.wait_ge(free["pj"].sem, free["pj"].upto(LAST))
            sp.dma_start(ew[:], expert_w.rearrange("e d o -> d e o")).then_inc(ld_ew.sem, 16)
            for t in range(TB):
                sp.wait_ge(ex_add.sem, t + 1)
                sp.dma_start(out[2 * t:2 * t + 2].rearrange("j q d -> (j q) d"), xb[:, t, :]).then_inc(ex_out.sem, 16)
            sp.wait_ge(ex_out.sem, 16 * TB)
        @block.vector
        def _(dve):
            chain = [0]

            def link(ins):
                chain[0] += 1
                ins.then_inc(dve_link.sem, 1)
                dve.wait_ge(dve_link.sem, chain[0])

            def statistics(turn, u):
                if u == 0:
                    dve.wait_ge(ld_raw[turn.off % 2].sem, raw_loaded(turn))
                    if not (turn.i is None and turn.off == 0):
                        dve.wait_ge(normed.sem, normed.upto(turn.plus(-1)))
                for t in STATS_AT.get(u, ()):
                    ins = bn(turn, t)
                if u == 3:
                    k = [0]

                    def step(ins):
                        ins.then_inc(dve_step.sem, 1)
                        dve.wait_ge(dve_step.sem, dve_step.upto(turn, k[0]))
                        k[0] += 1
                    step(ins)
                    last = stats_combine(128, TILES, step, half=-0.5, st=stc, sm=smc)
                    last.then_inc(stats_ok.sem, 1)

            def split_high(turn, g):
                if g == 0:
                    dve.wait_ge(normed.sem, normed.upto(turn))
                    if not (turn.i is None and turn.off < 2):
                        dve.wait_ge(pv_done.sem, pv_done.upto(turn.plus(-2), TILES - 1))
                nc.vector.tensor_copy(token_group(xk_hi, turn, g), token_group(raw, turn, g)).then_inc(split_hi.sem, 1)

            nc.vector.memset(st[:], 0.0)
            nc.vector.memset(stc[:], 0.0)
            nc.vector.memset(ones[:], 1.0)
            nc.vector.memset(oscale[:], 1.0 / OSCALE)
            link(nc.vector.memset(ones16[:], 1.0))
            dve.wait_ge(consts.sem, 1)
            dve.wait_ge(ld_gb.sem, 96)
            dve.wait_ge(consts.sem, 2)
            for k in range(2):
                ins = nc.vector.tensor_scalar(fold[:, k, :], ident[:], gb[:, 2 * k:2 * k + 1], None, ALU.mult)
            link(ins)
            for k in range(2):
                ins = nc.vector.tensor_scalar(fold[0:1, k, :], ones[0:1, :], g0row[0:1, k, :], -1.0, ALU.mult, ALU.mult)
            link(ins)
            for k in range(2):
                ins = nc.vector.tensor_copy(fold[:, k, 0:1], gb[:, 2 * k + 1:2 * k + 2])
            ins.then_inc(folded.sem, 1)
            dve.wait_ge(ld_x.sem, 16)
            for rnd in range(2):
                for b in range(B):
                    ins = nc.vector.bn_stats(st[0:NQ, b, :], lx[:, b, :])
                link(ins)
                stats_combine(NQ, B, link).then_inc(var_rdy.sem, 1)
                if rnd == 0:
                    for u in range(4):
                        statistics(Turn(0), u)
                if rnd == 1:
                    dve.wait_ge(ev_w.sem, FOLDS)
                    nc.vector.tensor_reduce(amax[:, 0:1], wvT[:].rearrange("p n c -> p (n c)"), AX.X, ALU.max,
                                            apply_absolute_value=True)
                    nc.vector.tensor_reduce(amax[:, 1:2], wo_sb[:].rearrange("p n c -> p (n c)"), AX.X, ALU.max,
                                            apply_absolute_value=True).then_inc(amax_rdy.sem, 1)
                dve.wait_ge(rstd_rdy.sem, rnd + 1)
                for b in range(B):
                    ins = nc.vector.tensor_scalar(lx[:, b, :], lx[:, b, :], sm[0:NQ, 0, b:b + 1],
                                                  sm[0:NQ, 1, b:b + 1], ALU.subtract, ALU.mult)
                link(ins)
            nc.vector.memset(lx[:, :, 0:1], 1.0).then_inc(lat_rdy.sem, 1)
            dve.wait_ge(amax_all.sem, 1)
            link(nc.vector.tensor_tensor(wscale[:, 1:2], amax[:, 3:4], amax[:, 4:5], ALU.mult))
            link(nc.vector.tensor_scalar(wscale[:, 1:2], wscale[:, 1:2], 1e-30, DH / WMAX, ALU.max, ALU.mult))
            link(nc.vector.reciprocal(wscale[:, 0:1], wscale[:, 1:2]))
            nc.vector.tensor_scalar(wscale[:, 1:2], wscale[:, 1:2], 1.0 / OSCALE, None, ALU.mult)\
              .then_inc(wscale_rdy.sem, 1)
            dve.wait_ge(ev_w.sem, FOLDS + H)
            link(nc.vector.tensor_tensor(G[:, :, 128:129], G[:, :, 128:129], G[:, :, 0:1], ALU.subtract))
            link(nc.vector.memset(G[:, :, 0:1], 0.0))
            nc.vector.tensor_reduce(amax[:, 2:3], G[:].rearrange("p h c -> p (h c)"), AX.X, ALU.max,
                                    apply_absolute_value=True).then_inc(amax_rdy.sem, 1)
            dve.wait_ge(lat_t.sem, 1)
            nc.vector.tensor_copy(lT[:], S[:, 0:2, :].rearrange("p a n -> p (a n)")).then_inc(lat_cp.sem, 1)
            dve.wait_ge(amax_all.sem, 2)
            link(nc.vector.tensor_scalar(sigma[:, 0:1], amax[:, 5:6], 1e-30, 129.0 / QMAX, ALU.max, ALU.mult))
            nc.vector.reciprocal(sigma[:, 1:2], sigma[:, 0:1]).then_inc(sigma_rdy.sem, 1)
            dve.wait_ge(lat_hi.sem, 1)
            dve.wait_ge(lat_cp.sem, 1)
            nc.vector.tensor_tensor(lT_lo[:], lT[:], lT_hi[:], ALU.subtract).then_inc(lat_lo.sem, 1)
            for g in range(GROUPS):
                split_high(Turn(0), g)
            dve.wait_ge(sigma_rdy.sem, 1)
            for k in range(2):
                dve.wait_ge(g_hi_rdy.sem, k + 1)
                h = slice(8 * k, 8 * k + 8)
                nc.vector.scalar_tensor_tensor(G_lo[:, h].rearrange("p h c -> p (h c)"),
                                               G[:, h].rearrange("p h c -> p (h c)"), sigma[:, 1:2],
                                               G_hi[:, h].rearrange("p h c -> p (h c)"), ALU.mult, ALU.subtract)\
                  .then_inc(g_rdy.sem, 1)
            dve.wait_ge(lat_rdy.sem, 1)
            link(nc.vector.tensor_copy(lk_hi[:], lx[:]))
            nc.vector.tensor_tensor(lk_lo[:], lx[:], lk_hi[:], ALU.subtract).then_inc(lat_lo.sem, 1)

            def queries_low(turn, c):
                dve.wait_ge(q_hi_done.sem, q_hi_done.upto(turn, c))
                cols = slice(c * HALF, (c + 1) * HALF)
                p = turn.off % 2
                nc.vector.tensor_tensor(q_lo[p][:, cols], W[BANK[("q", c)]][:], q_hi[p][:, cols], ALU.subtract)\
                  .then_inc(free["q"].sem, 1)

            def maxima(turn, n):
                dve.wait_ge(pe_item["m"].sem, pe_item["m"].upto(turn, n))
                r, c = M_ORDER[n]
                if n == 0 and not (turn.i is None and turn.off == 0):
                    dve.wait_ge(m16_done.sem, m16_done.upto(turn.plus(-1)))
                width = 512 if c < 3 else REST + NQ
                nc.vector.tensor_reduce(mx[:, r, c:c + 1], W[BANK[("m", n)]][:, 0:width], AX.X, ALU.max)\
                  .then_inc(free["m"].sem, 1)
                if n == MAXIMA - 1:
                    dve.wait_ge(free["m"].sem, free["m"].upto(turn, n))
                    if not (turn.i is None and turn.off == 0):
                        dve.wait_ge(pe_item["mt"].sem, pe_item["mt"].upto(turn.plus(-1), 1))
                    nc.vector.tensor_reduce(m16[:], mx[:], AX.X, ALU.max, negate=True).then_inc(m16_done.sem, 1)

            def low_part(turn, u):
                r, k = rows_of(u), pbuf(turn, u)
                dve.wait_ge(e_done.sem, e_done.upto(turn, u))
                src = S[0:r, 2 * (u % 2):2 * (u % 2) + 2, :].rearrange("p a n -> p (a n)")
                nc.vector.tensor_tensor(p_lo[k][0:r, :], src, p_hi[k][0:r, :], ALU.subtract)\
                  .then_inc(lo_done.sem, 1)

            def reciprocals(turn):
                dve.wait_ge(pe_item["sr"].sem, pe_item["sr"].upto(turn))
                nc.vector.reciprocal(rcol[:], W[BANK[("sr", 0)]][:, 0:8]).then_inc(free["sr"].sem, 1)

            def slot(b, prep=True, post=True, stats=True):
                nxt = b.plus(1)
                for u in range(UNITS):
                    if stats:
                        statistics(b.plus(2), u)
                    for kind, k in PLAN[u][0] + PLAN[u][1]:
                        if kind == "q" and prep:
                            queries_low(nxt, k)
                        if kind == "m" and prep:
                            maxima(nxt, k)
                        if kind == "sr" and post:
                            reciprocals(b.plus(-1))
                    low_part(b, u)
                    if prep and u < 2:
                        split_high(nxt, 2 * u)
                        split_high(nxt, 2 * u + 1)

            for early, late in PLAN:
                for kind, k in early + late:
                    if kind == "q":
                        queries_low(Turn(0), k)
                    if (kind, k) == ("t", 3):
                        for u in range(4):
                            statistics(Turn(1), u)
                        small_weights_vector(dve, link)
                    if kind == "m":
                        maxima(Turn(0), k)
                        if k in WO_AFTER:
                            h = WO_AFTER[k]
                            dve.wait_ge(ev_w.sem, FOLDS + H + h + 1)
                            nc.vector.scalar_tensor_tensor(WO_lo[:, h, :], wo_banks[h % 4], wscale[:, 0:1],
                                                           WO_hi[:, h, :], ALU.mult, ALU.subtract)\
                              .then_inc(wo_lo_done.sem, 1)
            lambdas_vector(dve, link)
            slot(Turn(0), post=False)
            with dve.Fori(0, B // 2 - 2) as i:
                slot(Turn(1, i))
                slot(Turn(2, i))
            slot(Turn(B - 3))
            slot(Turn(B - 2), stats=False)
            slot(Turn(B - 1), prep=False, stats=False)
            reciprocals(LAST)
            tail_vector(dve)

        @block.gpsimd
        def _(pool):
            nc.gpsimd.memset(wpad[:].rearrange("p a b c -> p (a b c)"), 0.0).then_inc(padded.sem, 1)
            nc.gpsimd.memset(sm[:].rearrange("p a b -> p (a b)"), 1.0)
            nc.gpsimd.memset(mhalf[:], -0.5)
            nc.gpsimd.memset(carrier[:], 0.0)
            nc.gpsimd.memset(mask[:], 0.0).then_inc(pool_link.sem, 1)
            nc.gpsimd.memset(ident[:], 0.0).then_inc(pool_link.sem, 1)
            pool.wait_ge(pool_link.sem, 2)
            nc.gpsimd.affine_select(out=ident[:], in_=ident[:], compare_op=ALU.not_equal, fill=1.0, base=0,
                                    pattern=[[-1, 128]], channel_multiplier=1).then_inc(consts.sem, 1)
            pool.wait_ge(consts.sem, 1)
            nc.gpsimd.tensor_copy(ident16[:], ident[:]).then_inc(consts.sem, 1)
            for j in range(2):
                pool.wait_ge(consts.sem, 2 + j)
                nc.gpsimd.affine_select(out=mask[64 * j:64 * j + 64, :], in_=mask[64 * j:64 * j + 64, :],
                                        compare_op=ALU.is_ge, fill=-3e38, base=0,
                                        pattern=[[-1, NQ]], channel_multiplier=1).then_inc(consts.sem, 1)
            pool.wait_ge(consts.sem, 4)
            for p in range(2):
                nc.gpsimd.memset(xk_hi[p][:, :, 0:1], 1.0)
                ins = nc.gpsimd.memset(xk_lo[p][:, :, 0:1], 0.0)
            ins.then_inc(pool_link.sem, 1)
            pool.wait_ge(pool_link.sem, 3)

            def inverse_deviation_ctx(turn):
                pool.wait_ge(stats_ok.sem, stats_ok.upto(turn))
                nc.gpsimd.tensor_tensor(smc[:, 1, :], smc[:, 7, :], mhalf[:, 0:TILES], ALU.pow)\
                  .then_inc(rstd_step.sem, 1)
                pool.wait_ge(rstd_step.sem, rstd_step.upto(turn))
                nc.gpsimd.tensor_tensor(smc[:, 2, :], smc[:, 0, :], smc[:, 1, :], ALU.mult)\
                  .then_inc(rstd_ctx.sem, 1)

            def split_tokens(turn):
                for g in range(GROUPS):
                    lo, hi, f = token_group(xk_lo, turn, g), token_group(xk_hi, turn, g), token_group(raw, turn, g)
                    pool.wait_ge(split_hi.sem, split_hi.upto(turn, g))
                    nc.gpsimd.tensor_tensor(lo, f, hi, ALU.subtract).then_inc(split.sem, 1)

            def at64(t, turn):
                if turn.i is None:
                    return t[:, 64 * turn.off:64 * turn.off + 64]
                return t[:, bass.ds(turn.times(64), 64)]

            def at_batch(t, turn):
                if turn.i is None:
                    return t[:, turn.off, :]
                return t[:, bass.ds(turn.times(1), 1), :].rearrange("p o d -> p (o d)")

            def current_T(turn):
                p = turn.off % 2
                if not (turn.i is None and turn.off < 2):
                    pool.wait_ge(s_done.sem, s_done.upto(turn.plus(-2), LAT))
                carry(pool, turn, 6 + turn.off % 2)
                nc.gpsimd.tensor_copy(cT_hi[p][:], at64(lT_hi, turn))
                nc.gpsimd.tensor_copy(cT_lo[p][:], at64(lT_lo, turn)).then_inc(curT.sem, 1)

            def current_k(turn):
                p = turn.off % 2
                if not (turn.i is None and turn.off < 2):
                    pool.wait_ge(pv_done.sem, pv_done.upto(turn.plus(-2), LAT))
                carry(pool, turn, 8 + turn.off % 2)
                nc.gpsimd.tensor_copy(ck_hi[p][:], at_batch(lk_hi, turn))
                nc.gpsimd.tensor_copy(ck_lo[p][:], at_batch(lk_lo, turn)).then_inc(curk.sem, 1)

            def denominators(turn):
                pool.wait_ge(oa_free.sem, oa_free.upto(turn))
                pool.wait_ge(free["ol"].sem, free["ol"].upto(turn, 1))
                nc.gpsimd.tensor_tensor(srow[:], o_sb[0:1, 0, :], o_sb[0:1, 1, :], ALU.add).then_inc(srow_done.sem, 1)

            def diagonals(turn):
                pool.wait_ge(free["sr"].sem, free["sr"].upto(turn))
                for k in range(2):
                    nc.gpsimd.tensor_tensor(diag[:, k], ident[:].unsqueeze(1).to_broadcast([128, 4, 128]),
                                            rcol[:, 4 * k:4 * k + 4].unsqueeze(2).to_broadcast([128, 4, 128]),
                                            ALU.mult).then_inc(diag_done.sem, 1)

            def normalise_outputs(turn):
                for k in range(2):
                    cols = slice(k * HALF, (k + 1) * HALF)
                    pool.wait_ge(free["bc"].sem, free["bc"].upto(turn, k))
                    nc.gpsimd.tensor_tensor(o_sb[:, 0, cols], o_sb[:, 0, cols], rb[:, cols], ALU.mult)
                    nc.gpsimd.tensor_tensor(o_sb[:, 1, cols], o_sb[:, 1, cols], rb[:, cols], ALU.mult)\
                      .then_inc(o_normed.sem, 1)

            def outputs_low(turn):
                for k in range(2):
                    cols = slice(k * HALF, (k + 1) * HALF)
                    pool.wait_ge(o_hi_done.sem, o_hi_done.upto(turn, k))
                    nc.gpsimd.tensor_tensor(o_lo[:, :, cols], o_sb[:, :, cols], o_hi[:, :, cols], ALU.subtract)\
                      .then_inc(o_split.sem, 1)

            def slot(b, prep=True, post=True, stats=True):
                if prep:
                    current_T(b.plus(1))
                    split_tokens(b.plus(1))
                    current_k(b.plus(1))
                if post:
                    denominators(b.plus(-1))
                if stats:
                    inverse_deviation_ctx(b.plus(2))
                if post:
                    diagonals(b.plus(-1))
                    normalise_outputs(b.plus(-1))
                    outputs_low(b.plus(-1))

            inverse_deviation(pool, 0)
            inverse_deviation_ctx(Turn(0))
            inverse_deviation(pool, 1)
            for k, (c0, c1) in enumerate(((0, 2), (2, 3))):
                pool.wait_ge(amax_rdy.sem, k + 1)
                nc.gpsimd.partition_all_reduce(amax[:, 3 + c0:3 + c1], amax[:, c0:c1], 128, bass.bass_isa.ReduceOp.max)\
                  .then_inc(amax_all.sem, 1)
            pool.wait_ge(lat_lo.sem, 1)
            current_T(Turn(0))
            split_tokens(Turn(0))
            pool.wait_ge(lat_lo.sem, 2)
            current_k(Turn(0))
            inverse_deviation_ctx(Turn(1))
            slot(Turn(0), post=False)
            with pool.Fori(0, B // 2 - 2) as i:
                slot(Turn(1, i))
                slot(Turn(2, i))
            slot(Turn(B - 3))
            slot(Turn(B - 2), stats=False)
            slot(Turn(B - 1), prep=False, stats=False)
            denominators(LAST)
            diagonals(LAST)
            normalise_outputs(LAST)
            outputs_low(LAST)
            tail_gpsimd(pool)

        @block.scalar
        def _(act):
            for n in range(FOLDS + H):
                act.wait_ge(pe_w.sem, n + 1)
                if n < FOLDS:
                    hp, kind = n // 3, n % 3
                    dst = (wqT[:, hp, :], wkT[:, hp, :], wvT[:, hp, :])[kind]
                    ins = nc.scalar.copy(dst, fold_bank(n)[:, 128:256] if kind == 0 else fold_bank(n))
                else:
                    ins = nc.scalar.activation(G[:, n - FOLDS, :], fold_bank(n), ACT.Copy, scale=DH ** -0.5)
                ins.then_inc(ev_w.sem, 1)
            def normalise(turn, tiles):
                if tiles[0] == 0:
                    act.wait_ge(rstd_ctx.sem, rstd_ctx.upto(turn))
                x_ = raw[turn.off % 2]
                for t in tiles:
                    r = rows_of(t)
                    ins = nc.scalar.activation(x_[0:r, t, :], x_[0:r, t, :], ACT.Identity, bias=smc[0:r, 2, t:t + 1],
                                               scale=smc[0:r, 1, t:t + 1])
                if tiles[-1] == TILES - 1:
                    ins.then_inc(normed.sem, 1)

            normalise(Turn(0), range(TILES))
            act.wait_ge(lat_cp.sem, 1)
            nc.scalar.copy(lT_hi[:], lT[:]).then_inc(lat_hi.sem, 1)
            act.wait_ge(sigma_rdy.sem, 1)
            for k in range(2):
                h = slice(8 * k, 8 * k + 8)
                nc.scalar.activation(G_hi[:, h].rearrange("p h c -> p (h c)"), G[:, h].rearrange("p h c -> p (h c)"),
                                     ACT.Copy, scale=sigma[:, 1:2]).then_inc(g_hi_rdy.sem, 1)

            def reciprocals_out(turn, k):
                act.wait_ge(pe_item["bc"].sem, pe_item["bc"].upto(turn, k))
                nc.scalar.copy(rb[:, k * HALF:(k + 1) * HALF], W[BANK[("bc", k)]][:]).then_inc(free["bc"].sem, 1)

            def outputs_high(turn, k):
                act.wait_ge(o_normed.sem, o_normed.upto(turn, k))
                cols = slice(k * HALF, (k + 1) * HALF)
                nc.scalar.copy(o_hi[:, :, cols], o_sb[:, :, cols]).then_inc(o_hi_done.sem, 1)

            def queries_high(turn, c):
                act.wait_ge(pe_item["q"].sem, pe_item["q"].upto(turn, c))
                p = turn.off % 2
                nc.scalar.copy(q_hi[p][:, c * HALF:(c + 1) * HALF], W[BANK[("q", c)]][:]).then_inc(q_hi_done.sem, 1)

            def transposed(turn, g):
                act.wait_ge(pe_item["t"].sem, pe_item["t"].upto(turn, g))
                p, w = turn.off % 2, (512 if g < 3 else REST)
                src = W[BANK[("t", g)]][:].bitcast(F16)
                nc.scalar.copy(xT_hi[p][:, 512 * g:512 * g + w], src[:, 0:w])
                nc.scalar.copy(xT_lo[p][:, 512 * g:512 * g + w], src[:, 512:512 + w]).then_inc(free["t"].sem, 1)

            def shift_row(turn, k):
                act.wait_ge(pe_item["mt"].sem, pe_item["mt"].upto(turn, k))
                nc.scalar.copy(q_hi[turn.off % 2][0:1, k * HALF:(k + 1) * HALF], W[BANK[("mt", k)]][0:1, :])\
                  .then_inc(free["mt"].sem, 1)

            def exponentials(turn, u):
                r, k = rows_of(u), pbuf(turn, u)
                act.wait_ge(s_done.sem, s_done.upto(turn, u))
                if not (turn.i is None and turn.off == 0 and u < NPB):
                    act.wait_ge(pv_done.sem, pv_done.upto(turn, u - NPB))
                src = S[0:r, 2 * (u % 2):2 * (u % 2) + 2, :].rearrange("p a n -> p (a n)")
                nc.scalar.activation(p_hi[k][0:r, :], src, ACT.Exp, scale=sigma[0:r, 0:1])
                nc.scalar.activation(src, src, ACT.Exp, scale=sigma[0:r, 0:1]).then_inc(e_done.sem, 1)

            def outputs(turn):
                act.wait_ge(pv_done.sem, pv_done.upto(turn, TILES - 1))
                nc.scalar.copy(o_sb[:, 0, :], OA[:].rearrange("p a n -> p (a n)")).then_inc(oa_free.sem, 1)

            def latent_outputs(turn):
                act.wait_ge(pv_done.sem, pv_done.upto(turn, LAT))
                for k in range(2):
                    nc.scalar.copy(o_sb[:, 1, k * HALF:(k + 1) * HALF], W[BANK[("ol", k)]][:])\
                      .then_inc(free["ol"].sem, 1)

            def projected(turn):
                act.wait_ge(pe_item["pj"].sem, pe_item["pj"].upto(turn))
                dst = attnT[:, 64 * turn.off:64 * turn.off + 64] if turn.i is None \
                    else attnT[:, bass.ds(turn.times(64), 64)]
                nc.scalar.activation(dst, W[BANK[("pj", 0)]][:, 0:NQ], ACT.Copy, scale=wscale[:, 1:2])\
                  .then_inc(free["pj"].sem, 1)

            def side_item(item, nxt, old, prep, post):
                kind, k = item
                if kind == "q" and prep:
                    queries_high(nxt, k)
                if kind == "t" and prep:
                    transposed(nxt, k)
                if kind == "mt" and prep:
                    shift_row(nxt, k)
                if kind == "bc" and post:
                    reciprocals_out(old, k)
                if kind == "pj" and post:
                    projected(old)

            def slot(b, prep=True, post=True, stats=True):
                nxt, old = b.plus(1), b.plus(-1)
                for u in range(UNITS):
                    early, late = PLAN[u]
                    exponentials(b, u)
                    if u == 0 and post:
                        outputs(old)
                    if u == LATENTS_AT and post:
                        latent_outputs(old)
                    if u in OUTPUTS_HIGH_AT and post:
                        outputs_high(old, OUTPUTS_HIGH_AT[u])
                    for item in early + late:
                        side_item(item, nxt, old, prep, post)
                    if stats and u in NORMALISE_AT:
                        normalise(b.plus(2), NORMALISE_AT[u])

            for early, late in PLAN:
                for item in early + late:
                    side_item(item, Turn(0), None, True, False)
                    if item[0] == "m" and item[1] in WO_AFTER:
                        h = WO_AFTER[item[1]]
                        if h == 0:
                            act.wait_ge(wscale_rdy.sem, 1)
                        act.wait_ge(pe_w.sem, FOLDS + H + h + 1)
                        nc.scalar.activation(WO_hi[:, h, :], wo_banks[h % 4], ACT.Copy, scale=wscale[:, 0:1])\
                          .then_inc(ev_w.sem, 1)
                    if item[0] == "m" and item[1] in SMALL_AFTER:
                        small_weights_scalar(act, SMALL_AFTER[item[1]])
                    if item == ("m", MAXIMA // 2):
                        normalise(Turn(1), range(TILES))
            slot(Turn(0), post=False)
            with act.Fori(0, B // 2 - 2) as i:
                slot(Turn(1, i))
                slot(Turn(2, i))
            slot(Turn(B - 3))
            slot(Turn(B - 2), stats=False)
            slot(Turn(B - 1), prep=False, stats=False)
            outputs(Turn(B - 1))
            latent_outputs(Turn(B - 1))
            for k in range(2):
                reciprocals_out(LAST, k)
            for k in range(2):
                outputs_high(LAST, k)
            projected(Turn(B - 1))
            tail_scalar(act)

        @block.tensor
        def _(pe):
            mm = nc.tensor.matmul
            pe.wait_ge(folded.sem, 1)
            pe.wait_ge(ld_w.sem, 48)
            for n in range(FOLDS):
                hp, kind = n // 3, n % 3
                if n >= 4:
                    pe.wait_ge(ev_w.sem, n - 3)
                w = (wq_sb[:, 128 * hp:128 * hp + 128], wkv_sb[:, 128 * hp:128 * hp + 128],
                     wkv_sb[:, H * DH + 128 * hp:H * DH + 128 * hp + 128])[kind]
                mm(fold_bank(n), w, fold[:].rearrange("p k d -> p (k d)"), start=True, stop=True)\
                    .then_inc(pe_w.sem, 1)
            for n in range(FOLDS, FOLDS + H):
                h = n - FOLDS
                pe.wait_ge(ev_w.sem, max(n - 3, FOLDS))
                r = slice(64 * (h % 2), 64 * (h % 2) + 64)
                mm(fold_bank(n), wqT[r, h // 2, :], wkT[r, h // 2, :], start=True, stop=True).then_inc(pe_w.sem, 1)
            pe.wait_ge(lat_rdy.sem, 1)
            for b in range(B):
                ins = nc.tensor.transpose(S[:, b // 8, 64 * (b % 8):64 * (b % 8) + 64], lx[:, b, :], ident[0:NQ, 0:NQ])
            ins.then_inc(lat_t.sem, 1)
            pe.wait_ge(ev_w.sem, FOLDS + H)
            pe.wait_ge(g_rdy.sem, 2)
            pe.wait_ge(consts.sem, 2)

            def output_map(h):
                if h >= 4:
                    pe.wait_ge(wo_lo_done.sem, h - 3)
                r = slice(64 * (h % 2), 64 * (h % 2) + 64)
                for c in (0, 128):
                    ins = mm(wo_banks[h % 4][:, c:c + 128], wvT[r, h // 2, c:c + 128], wo_sb[r, h // 2, :],
                             start=True, stop=True)
                ins.then_inc(pe_w.sem, 1)

            last_user = {}

            def bank_free(item, turn):
                bank = BANK[item]
                if bank in last_user:
                    (kind, k), t = last_user[bank]
                    pe.wait_ge(free[kind].sem, free[kind].upto(t, k))
                last_user[bank] = (item, turn)

            def side_item(item, turn):
                kind, k = item
                w, p = W[BANK[item]], turn.off % 2
                bank_free(item, turn)
                if kind == "q":
                    if k == 0:
                        pe.wait_ge(curT.sem, curT.upto(turn))
                    for j in range(8):
                        h, c, dst = 8 * (k % 2) + j, 128 * (k // 2), w[:, 64 * j:64 * j + 64]
                        mm(dst, G_hi[:, h, c:c + 128], cT_hi[p][:], start=True, stop=False)
                        mm(dst, G_hi[:, h, c:c + 128], cT_lo[p][:], start=False, stop=False)
                        ins = mm(dst, G_lo[:, h, c:c + 128], cT_hi[p][:], start=False, stop=True)
                if kind == "t":
                    pe.wait_ge(split.sem, split.upto(turn, k))
                    w16 = w[:].bitcast(F16)
                    for t in (range(4 * k, 4 * k + 4) if k < 3 else [FULL]):
                        r = rows_of(t)
                        for x_, o in ((xk_hi, 0), (xk_lo, 512)):
                            c = o + 128 * (t - 4 * k)
                            ins = nc.tensor.transpose(w16[:, c:c + r], x_[p][0:r, t, :], ident16[0:r, 0:r])
                if kind == "m":
                    r, c = M_ORDER[k]
                    if k == 0:
                        pe.wait_ge(q_hi_done.sem, q_hi_done.upto(turn, 3))
                    if M_ORDER[k] in ((0, 0), (0, 1), (0, 2), (0, 3)):
                        pe.wait_ge(free["t"].sem, free["t"].upto(turn, c))
                    rows = q_hi[p][:, 128 * r:128 * r + 128]
                    if c < 3:
                        ins = mm(w[:], rows, xT_hi[p][:, 512 * c:512 * c + 512], start=True, stop=True)
                    else:
                        mm(w[:, 0:REST], rows, xT_hi[p][:, 1536:1536 + REST], start=True, stop=True)
                        ins = mm(w[:, REST:REST + NQ], q_hi[p][:, COLS + 128 * r:COLS + 128 * r + 128], cT_hi[p][:],
                                 start=True, stop=True)
                if kind == "mt":
                    pe.wait_ge(m16_done.sem, m16_done.upto(turn))
                    for j in range(4):
                        ins = mm(w[0:1, 128 * j:128 * j + 128], m16[:, 4 * k + j:4 * k + j + 1], ident16[:],
                                 start=True, stop=True)
                if kind == "sr":
                    pe.wait_ge(srow_done.sem, srow_done.upto(turn))
                    for j in range(8):
                        ins = mm(w[:, j:j + 1], srow[:, 128 * j:128 * j + 128], oscale[:], start=True, stop=True)
                if kind == "bc":
                    pe.wait_ge(diag_done.sem, diag_done.upto(turn, k))
                    ins = mm(w[:], ones[:], diag[:, k].rearrange("p j n -> p (j n)"), start=True, stop=True)
                if kind == "pj":
                    pe.wait_ge(o_split.sem, o_split.upto(turn, 1))
                    for n in range(2 * H):
                        h, c = n // 2, n % 2
                        whi, wlo = (t_[:, h, 128 * c:128 * c + 128] for t_ in (WO_hi, WO_lo))
                        ohi, olo = (t_[:, c, 64 * h:64 * h + 64] for t_ in (o_hi, o_lo))
                        mm(w[:, 0:NQ], whi, ohi, start=n == 0, stop=False)
                        mm(w[:, 0:NQ], whi, olo, start=False, stop=False)
                        ins = mm(w[:, 0:NQ], wlo, ohi, start=False, stop=n == 2 * H - 1)
                ins.then_inc(pe_item[kind].sem, 1)

            def scores(turn, u):
                p, r = turn.off % 2, rows_of(u)
                if not (turn.i is None and turn.off == 0 and u < 2):
                    pe.wait_ge(lo_done.sem, lo_done.upto(turn, u - 2))
                if u == 0:
                    pe.wait_ge(free["mt"].sem, free["mt"].upto(turn, 1))
                    pe.wait_ge(free["q"].sem, free["q"].upto(turn, 3))
                if u < LAT:
                    hi, lo, qc = xT_hi[p][:, 128 * u:128 * u + r], xT_lo[p][:, 128 * u:128 * u + r], 0
                else:
                    hi, lo, qc = cT_hi[p][:], cT_lo[p][:], COLS
                cols = [slice(qc + HALF * k, qc + HALF * k + HALF) for k in range(2)]
                for k in range(2):
                    mm(score_bank(u, k)[0:r], hi, q_hi[p][:, cols[k]], start=True, stop=False)
                for k in range(2):
                    mm(score_bank(u, k)[0:r], hi, q_lo[p][:, cols[k]], start=False, stop=False)
                if u == LAT:
                    for k in range(2):
                        mm(score_bank(u, k)[0:r], ones16[:], q_hi[p][0:1, HALF * k:HALF * k + HALF],
                           start=False, stop=False)
                for k in range(2):
                    ins = mm(score_bank(u, k)[0:r], lo, q_hi[p][:, cols[k]], start=False, stop=True)
                ins.then_inc(s_done.sem, 1)

            def weigh(turn, u):
                p, r, kb = turn.off % 2, rows_of(u), pbuf(turn, u)
                pe.wait_ge(lo_done.sem, lo_done.upto(turn, u))
                if u == 0 and not (turn.i is None and turn.off == 0):
                    pe.wait_ge(oa_free.sem, oa_free.upto(turn.plus(-1)))
                if u < LAT:
                    hi, lo, first, last = xk_hi[p][0:r, u, :], xk_lo[p][0:r, u, :], u == 0, u == TILES - 1
                    dst = [OA[:, k, :] for k in range(2)]
                else:
                    pe.wait_ge(curk.sem, curk.upto(turn))
                    hi, lo, first, last = ck_hi[p][:], ck_lo[p][:], True, True
                    for k in range(2):
                        bank_free(("ol", k), turn)
                    dst = [W[BANK[("ol", k)]][:] for k in range(2)]
                ph, pl = p_hi[kb], p_lo[kb]
                cols = [slice(HALF * k, HALF * k + HALF) for k in range(2)]
                for k in range(2):
                    mm(dst[k], hi, ph[0:r, cols[k]], start=first, stop=False)
                for k in range(2):
                    mm(dst[k], hi, pl[0:r, cols[k]], start=False, stop=False)
                for k in range(2):
                    ins = mm(dst[k], lo, ph[0:r, cols[k]], start=False, stop=last)
                ins.then_inc(pv_done.sem, 1)

            def slot(b, prep=True, post=True):
                nxt, old = b.plus(1), b.plus(-1)
                last_user.clear()
                for k in range(2):
                    last_user[BANK[("mt", k)]] = (("mt", k), b)
                def side_items(items):
                    for item in items:
                        if item[0] in PREP and prep:
                            side_item(item, nxt)
                        if item[0] not in PREP and post:
                            side_item(item, old)

                for u in range(UNITS):
                    scores(b, u)
                    side_items(PLAN[u][0])
                    if u >= 2:
                        weigh(b, u - 2)
                    elif post and u == 0:
                        weigh(old, TILES - 1)
                    elif post and u == LATENTS_AT:
                        weigh(old, LAT)
                    side_items(PLAN[u][1])

            for early, late in PLAN:
                for item in early + late:
                    if item[0] in PREP:
                        side_item(item, Turn(0))
                    if item[0] == "m" and item[1] in WO_AFTER:
                        output_map(WO_AFTER[item[1]])
                    if item[0] == "m" and item[1] in SMALL_AFTER:
                        small_weights_tensor(pe, SMALL_AFTER[item[1]])
            pe.wait_ge(wo_lo_done.sem, H)
            pe.wait_ge(wt_c.sem, 5)
            slot(Turn(0), post=False)
            with pe.Fori(0, B // 2 - 2) as i:
                slot(Turn(1, i))
                slot(Turn(2, i))
            slot(Turn(B - 3))
            slot(Turn(B - 2))
            slot(Turn(B - 1), prep=False)
            weigh(Turn(B - 1), TILES - 1)
            weigh(Turn(B - 1), LAT)
            side_item(("sr", 0), Turn(B - 1))
            for k in range(2):
                side_item(("bc", k), Turn(B - 1))
            side_item(("pj", 0), Turn(B - 1))
            tail_tensor(pe)


_INS = ['x', 'ctx_1024', 'L0_xattn_ln1_g', 'L0_xattn_ln1_b', 'L0_xattn_ln2_g', 'L0_xattn_ln2_b', 'L0_xattn_Wq',
        'L0_xattn_Wkv', 'L0_xattn_Wo', 'L0_attn_Wq', 'L0_attn_Wk', 'L0_attn_Wv', 'L0_attn_Wo', 'L0_attn_lq1',
        'L0_attn_lk1', 'L0_attn_lq2', 'L0_attn_lk2', 'L0_attn_rms_scale', 'L0_ffn_gate_w', 'L0_ffn_gate_b',
        'L0_ffn_expert_w', 'L0_ffn_expert_b']


def kernel(**inputs):
    import numpy as np
    import concourse.bacc as bacc
    from concourse.bass_utils import run_bass_kernel_spmd

    nc = bacc.Bacc("TRN2", target_bir_lowering=False, num_devices=1)
    arrays, args = {}, []
    for name in _INS:
        a = np.ascontiguousarray(inputs[name])
        arrays[name] = a
        args.append(nc.dram_tensor(name, a.shape, mybir.dt.from_np(a.dtype), kind="ExternalInput").ap())
    args.append(nc.dram_tensor("out", (B, NQ, D), F32, kind="ExternalOutput").ap())
    perceiver(nc, *args)
    return run_bass_kernel_spmd(nc, [arrays], core_ids=[0]).results[0]["out"]
```

```python
import concourse.bass as bass
from concourse import mybir
from contextlib import ExitStack

F32 = mybir.dt.float32
F16 = mybir.dt.float16
BF16 = mybir.dt.bfloat16
ALU = mybir.AluOpType
ACT = mybir.ActivationFunctionType
AX = mybir.AxisListType

B, NQ, D = 16, 64, 128
NCTX = 1601
H, DH = 16, 64
COLS = H * NQ
FULL = NCTX // 128
REST = NCTX - FULL * 128
TILES = FULL + 1
UNITS = TILES + 1
LAT = TILES
HALF = COLS // 2
GROUPS = 4
EPS = 1e-5
OSCALE = 1024.0
WMAX = 32768.0
QMAX = 64.0
NPB = 4
TB = 8
SH, SD = 16, 8
NE = 8


class Turn:

    def __init__(self, off, i=None, step=2):
        self.off, self.i, self.step = off, i, step

    def plus(self, d):
        return Turn(self.off + d, self.i, self.step)

    def times(self, per, add=0):
        if self.i is None:
            return per * self.off + add
        return self.i * (self.step * per) + (per * self.off + add)


class Signal:

    def __init__(self, sem, per=1):
        self.sem, self.per = sem, per

    def upto(self, turn, k=0):
        return turn.times(self.per, k + 1)


MAXIMA = 32


LONG = [(r, c) for c in range(3) for r in range(8)]
SHORT = [(r, 3) for r in range(8)]
M_ORDER = LONG[0:3] + SHORT[0:1]
for _k in range(7):
    M_ORDER += LONG[3 * _k + 3:3 * _k + 5] + SHORT[_k + 1:_k + 2] + LONG[3 * _k + 5:3 * _k + 6]
assert sorted(M_ORDER) == sorted(LONG + SHORT)


def two(k):
    return [("m", 2 * k), ("m", 2 * k + 1)]


PLAN = [([], []),
        ([], []),
        ([], [("q", 0), ("q", 1)]),
        ([("t", 0)], [("q", 2), ("t", 1)]),
        ([("q", 3), ("sr", 0)], [("t", 2)]),
        ([("t", 3), ("bc", 0)], [("bc", 1)] + two(0))]
PLAN += [(two(2 * u - 11), two(2 * u - 10)) for u in range(6, 13)]
PLAN += [(two(15) + [("pj", 0), ("mt", 0)], [("mt", 1)])]
LATENTS_AT = 1


def bank_of_items():
    order = []
    for u, (early, late) in enumerate(PLAN):
        order += early + ([("ol", 0), ("ol", 1)] if u == LATENTS_AT else []) + late
    return {item: n % 2 for n, item in enumerate(order)}


BANK = bank_of_items()
assert BANK[("ol", 0)] != BANK[("ol", 1)]
STATS_AT = {0: range(0, 3), 1: range(3, 6), 2: range(6, 11), 3: range(11, 13)}
NORMALISE_AT = {6: range(0, 2), 7: range(2, 4), 8: range(4, 6), 9: range(6, 8), 10: range(8, 10), 11: range(10, 12),
                12: range(12, 13)}
OUTPUTS_HIGH_AT = {8: 0, 9: 1}
PREP = ("q", "t", "m", "mt")


def rows_of(u):
    return 128 if u < FULL else (REST if u == FULL else NQ)


def perceiver(nc, x, ctx_in, ln1_g, ln1_b, ln2_g, ln2_b, Wq, Wkv, Wo, aWq, aWk, aWv, aWo,
              lq1, lk1, lq2, lk2, rms_scale, gate_w, gate_b, expert_w, expert_b, out):
    es = ExitStack()
    with es:
        def sb(name, shape, dt=F32):
            return es.enter_context(nc.sbuf_tensor(name, shape, dt))

        def sem(name, per=1):
            return Signal(es.enter_context(nc.semaphore(name)), per)

        ident = sb("ident", [128, 128])
        ident16 = sb("ident16", [128, 128], F16)
        ones = sb("ones", [128, 128])
        ones16 = sb("ones16", [1, 64], F16)
        oscale = sb("oscale", [1, 1])
        rcol = sb("rcol", [128, 8])
        diag = sb("diag", [128, 2, 4, 128])
        rb = sb("rb", [128, COLS])
        region = sb("region", [128, 10 * 1024])

        def part(start, size, dt=F32):
            v = region[:, start:start + size]
            return v if dt == F32 else v.bitcast(dt)

        wq_sb = part(0, 1024)
        wkv_sb = part(1024, 2048)
        wo_sb = part(9216, 1024).rearrange("p (n d) -> p n d", d=128)
        G = part(0, 4096).rearrange("p (h c) -> p h c", h=H)
        wqT = part(4096, 1024).rearrange("p (n d) -> p n d", d=128)
        wkT = part(5120, 2048).rearrange("p (n d) -> p n d", d=256)
        wvT = part(7168, 2048).rearrange("p (n d) -> p n d", d=256)
        q_hi = [part(2048 * p, 1024, F16) for p in range(2)]
        q_lo = [part(2048 * p + 1024, 1024, F16) for p in range(2)]
        p_hi = [part(4096 + 1024 * k, 512, F16) for k in range(NPB)]
        p_lo = [part(4608 + 1024 * k, 512, F16) for k in range(NPB)]
        o_sb = part(8192, 2048).rearrange("p (k n) -> p k n", k=2)
        A = part(0, 2048).rearrange("p (g c a m) -> p g c a m", g=4, c=4, a=2)
        E = part(2048, 2048).rearrange("p (g c a m) -> p g c a m", g=4, c=4, a=2)
        t1 = part(4096, 1024).rearrange("p (g c m) -> p g c m", g=4, c=4)
        t2 = part(5120, 1024).rearrange("p (g c m) -> p g c m", g=4, c=4)
        At = part(6144, 1024).rearrange("p (h m) -> p h m", m=64)
        AT = part(7168, 1024).rearrange("p (h n) -> p h n", n=128)
        prod = [part(8192 + 1024 * p, 1024).rearrange("p (e o) -> p e o", o=D) for p in range(2)]
        gb = sb("gb", [128, 4])
        g0row = sb("g0row", [1, 2, 1])
        fold = sb("fold", [128, 2, 128])
        G_hi = sb("G_hi", [128, H, 256], F16)
        G_lo = sb("G_lo", [128, H, 256], F16)
        WO_hi = sb("WO_hi", [128, H, 256], F16)
        WO_lo = sb("WO_lo", [128, H, 256], F16)
        amax = sb("amax", [128, 6])
        sigma = sb("sigma", [128, 2])
        wscale = sb("wscale", [128, 2])
        lx = sb("lx", [NQ, B, D])
        lk_hi = sb("lk_hi", [NQ, B, D], F16)
        lk_lo = sb("lk_lo", [NQ, B, D], F16)
        lT = sb("lT", [128, B * NQ])
        lT_hi = sb("lT_hi", [128, B * NQ], F16)
        lT_lo = sb("lT_lo", [128, B * NQ], F16)
        cT_hi = [sb(f"cT_hi{p}", [128, NQ], F16) for p in range(2)]
        cT_lo = [sb(f"cT_lo{p}", [128, NQ], F16) for p in range(2)]
        ck_hi = [sb(f"ck_hi{p}", [NQ, D], F16) for p in range(2)]
        ck_lo = [sb(f"ck_lo{p}", [NQ, D], F16) for p in range(2)]
        raw = [sb(f"raw{p}", [128, TILES, D]) for p in range(2)]
        xk = [sb(f"xk{p}", [128, 2, TILES, D], F16) for p in range(2)]
        xk_hi, xk_lo = ([xk[p][:, k] for p in range(2)] for k in range(2))
        xT_hi = [sb(f"xT_hi{p}", [128, TILES * 128], F16) for p in range(2)]
        xT_lo = [sb(f"xT_lo{p}", [128, TILES * 128], F16) for p in range(2)]
        srow = sb("srow", [1, COLS])
        attnT = sb("attnT", [128, B * NQ])
        st = sb("st", [128, 16, 6])
        sm = sb("sm", [128, 8, 16])
        stc = sb("stc", [128, TILES, 6])
        smc = sb("smc", [128, 8, TILES])
        carrier = sb("carrier", [1, 16])
        mhalf = sb("mhalf", [128, 16])
        mx = sb("mx", [128, 8, 4])
        m16 = sb("m16", [128, 8], F16)
        xres = raw[0][:, 0:TB, :]
        hn = raw[1][:, 0:TB, :]
        hT = xk[0][:].rearrange("p k t d -> p (k t d)")[:, 0:2 * B * NQ].bitcast(F32)
        wpad = sb("wpad", [128, 3, 4, 128])
        wpadT = sb("wpadT", [128, 3, 4, 128])
        wv_sb = sb("wv_sb", [128, 2, 128])
        wvaT = sb("wvaT", [128, 256])
        woa_sb = sb("woa_sb", [128, 256])
        woaT = sb("woaT", [128, 2, 128])
        rmsc = sb("rmsc", [128, 1])
        lv = sb("lv", [128, 4, 128])
        lp = sb("lp", [128, 2, 128])
        lsum = sb("lsum", [128, 2, SH])
        lexp = sb("lexp", [128, 2, SH])
        nlam = sb("nlam", [128, SH])
        mask = sb("mask", [128, NQ], BF16)
        identb = sb("identb", [128, 128], BF16)
        gw_sb = sb("gw_sb", [NE, 128])
        gwT = sb("gwT", [128, NE])
        gbias = sb("gbias", [128, NE])
        ew = sb("ew", [128, NE, 128])
        o_hi = lT[:].bitcast(F16).rearrange("p (c n) -> p c n", c=2)
        o_lo = ew[:].rearrange("p e o -> p (e o)").bitcast(F16).rearrange("p (c n) -> p c n", c=2)
        eb = sb("eb", [NE, 128])

        S = es.enter_context(nc.psum_tensor("S", [128, 4, 512], F32))
        OA = es.enter_context(nc.psum_tensor("OA", [128, 2, 512], F32))
        W = [es.enter_context(nc.psum_tensor(f"W{k}", [128, 512], F32)) for k in range(2)]

        ld_w = sem("ld_w")
        ld_gb = sem("ld_gb")
        ld_x = sem("ld_x")
        ld_res = sem("ld_res")
        ld_raw = [sem(f"ld_raw{p}") for p in range(2)]
        ld_a = sem("ld_a")
        ld_ew = sem("ld_ew")
        consts = sem("consts")
        padded = sem("padded")
        pool_link = sem("pool_link")
        dve_link = sem("dve_link")
        folded = sem("folded")
        pe_w = sem("pe_w")
        ev_w = sem("ev_w")
        amax_rdy = sem("amax_rdy")
        wscale_rdy = sem("wscale_rdy")
        wo_lo_done = sem("wo_lo_done")
        g_hi_rdy = sem("g_hi_rdy")
        sigma_rdy = sem("sigma_rdy")
        amax_all = sem("amax_all")
        g_rdy = sem("g_rdy")
        var_rdy = sem("var_rdy")
        rstd_rdy = sem("rstd_rdy")
        rstd_ctx = sem("rstd_ctx")
        lat_rdy = sem("lat_rdy")
        lat_t = sem("lat_t")
        lat_cp = sem("lat_cp")
        lat_hi = sem("lat_hi")
        lat_lo = sem("lat_lo")
        rstd_step = sem("rstd_step")
        s_done = sem("s_done", UNITS)
        e_done = sem("e_done", UNITS)
        lo_done = sem("lo_done", UNITS)
        pv_done = sem("pv_done", UNITS)
        oa_free = sem("oa_free")
        pe_item = {k: sem("pe_" + k, n) for k, n in
                   (("q", 4), ("t", 4), ("m", MAXIMA), ("mt", 2), ("sr", 1), ("bc", 2), ("pj", 1))}
        q_hi_done = sem("q_hi_done", 4)
        free = {"q": sem("q_lo_done", 4), "t": sem("t_copied", 4), "m": sem("m_reduced", MAXIMA),
                "mt": sem("m_row", 2), "ol": sem("ol_copied", 2), "sr": sem("recip_done"),
                "bc": sem("rb_copied", 2), "pj": sem("pj_copied", 1)}
        diag_done = sem("diag_done", 2)
        o_normed = sem("o_normed", 2)
        o_hi_done = sem("o_hi_done", 2)
        o_split = sem("o_split", 2)
        stats_ok = sem("stats_ok")
        normed = sem("normed")
        split_hi = sem("split_hi", GROUPS)
        split = sem("split", GROUPS)
        curT = sem("curT")
        curk = sem("curk")
        m16_done = sem("m16_done")
        srow_done = sem("srow_done")
        dve_step = sem("dve_step", 4)

        def pbuf(turn, u):
            return (2 * (turn.off % 2) + u) % NPB

        def score_bank(u, half):
            return S[:, 2 * (u % 2) + half, :]

        def load_raw(sp, turn):
            p = turn.off % 2
            b = turn.times(1)
            first = ctx_in[bass.ds(b, 1), 0:FULL * 128, :] if turn.i is not None else ctx_in[b:b + 1, 0:FULL * 128, :]
            last = ctx_in[bass.ds(b, 1), FULL * 128:NCTX, :] if turn.i is not None else ctx_in[b:b + 1, FULL * 128:NCTX, :]
            sp.dma_start(raw[p][:, 0:FULL, :],
                         first.rearrange("o (p t) d -> p (o t) d", t=FULL)).then_inc(ld_raw[p].sem, 16)
            sp.dma_start(raw[p][0:REST, FULL, :],
                         last.rearrange("o p d -> p (o d)")).then_inc(ld_raw[p].sem, 16)

        FOLDS = 3 * H // 2
        fold_banks = [W[0][:, 0:256], W[1][:, 0:256], OA[:, 0, 0:256], OA[:, 1, 0:256]]

        def fold_bank(n):
            return fold_banks[n % 4]

        wo_banks = [OA[:, 0, 0:256], OA[:, 1, 0:256], S[:, 2, 0:256], S[:, 3, 0:256]]
        WO_AFTER = {2 * h + 1: h for h in range(H)}
        SMALL_AFTER = {7 + 6 * g: g for g in range(5)}

        LD_A = 16 * (12 + 2 + 4 + 8 + 3)

        def stats_combine(P, n, link, half=0.5, st=st, sm=sm):
            mean_e, var_e, mean_o, var_o = (st[0:P, 0:n, k] for k in (1, 2, 4, 5))
            c = lambda k: sm[0:P, k, 0:n]
            nc.vector.tensor_tensor(c(2), mean_e, mean_o, ALU.subtract)
            nc.vector.tensor_tensor(c(3), var_e, var_o, ALU.add)
            link(nc.vector.tensor_tensor(c(4), mean_e, mean_o, ALU.add))
            nc.vector.tensor_scalar(c(0), c(4), half, None, ALU.mult)
            link(nc.vector.tensor_tensor(c(5), c(2), c(2), ALU.mult))
            link(nc.vector.scalar_tensor_tensor(c(6), c(5), 32.0, c(3), ALU.mult, ALU.add))
            return nc.vector.tensor_scalar(c(7), c(6), 1.0 / D, EPS, ALU.mult, ALU.add)

        def bn(turn, t):
            r = rows_of(t)
            return nc.vector.bn_stats(stc[0:r, t, :], raw[turn.off % 2][0:r, t, :])

        def token_group(t, turn, g):
            if g < 3:
                return t[turn.off % 2][:, 4 * g:4 * g + 4, 1:D]
            return t[turn.off % 2][0:REST, FULL:TILES, 1:D]

        def raw_loaded(turn):
            return (turn.i * 32 if turn.i is not None else 0) + 32 * (turn.off // 2) + 32

        def denominators(eng, vec, turn):
            eng.wait_ge(oa_free.sem, oa_free.upto(turn))
            eng.wait_ge(free["ol"].sem, free["ol"].upto(turn, 1))
            vec.tensor_tensor(srow[:], o_sb[0:1, 0, :], o_sb[0:1, 1, :], ALU.add).then_inc(srow_done.sem, 1)

        def diagonals(eng, vec, turn):
            eng.wait_ge(free["sr"].sem, free["sr"].upto(turn))
            for k in range(2):
                vec.tensor_tensor(diag[:, k], ident[:].unsqueeze(1).to_broadcast([128, 4, 128]),
                                        rcol[:, 4 * k:4 * k + 4].unsqueeze(2).to_broadcast([128, 4, 128]),
                                        ALU.mult).then_inc(diag_done.sem, 1)

        def normalise_outputs(eng, vec, turn):
            for k in range(2):
                cols = slice(k * HALF, (k + 1) * HALF)
                eng.wait_ge(free["bc"].sem, free["bc"].upto(turn, k))
                vec.tensor_tensor(o_sb[:, 0, cols], o_sb[:, 0, cols], rb[:, cols], ALU.mult)
                vec.tensor_tensor(o_sb[:, 1, cols], o_sb[:, 1, cols], rb[:, cols], ALU.mult)\
                  .then_inc(o_normed.sem, 1)

        def outputs_low(eng, vec, turn):
            for k in range(2):
                cols = slice(k * HALF, (k + 1) * HALF)
                eng.wait_ge(o_hi_done.sem, o_hi_done.upto(turn, k))
                vec.tensor_tensor(o_lo[:, :, cols], o_sb[:, :, cols], o_hi[:, :, cols], ALU.subtract)\
                  .then_inc(o_split.sem, 1)

        hTd = sb("hTd", [128, 2, 2, 64])
        Qs = sb("Qs", [128, 4, 128])
        Ks = sb("Ks", [128, 4, 2, 2, 64])
        Vb = sb("Vb", [128, 2, 8, 32])
        amx = sb("amx", [128, 4, 4, 2])
        asum = sb("asum", [128, 4, 4, 2])
        arc = sb("arc", [128, 4, 4, 2])
        Ob = sb("Ob", [128, 256])
        Osq = sb("Osq", [128, 256])
        Oc = sb("Oc", [128, 256])
        oms = sb("oms", [128, 3, SH])
        OcT = sb("OcT", [128, 2, 128])
        lg = sb("lg", [128, 10, TB, NE])
        g1 = sb("g1", [128, 4, TB])
        rank = sb("rank", [128, NE])
        esum = At[:].rearrange("p h m -> p (h m)")[:, 0:D]
        gT = AT[:].rearrange("p h n -> p (h n)")[0:NE, :]
        xb = attnT[:].rearrange("p (t d) -> p t d", d=D)
        ta = {n: sem("ta_" + n) for n in (
            "x1t", "x1", "h", "ht", "hcopy",
            "hd", "projqk", "projv", "q", "qk", "vb", "scores", "max", "shifted", "exp", "r", "r2",
            "t1", "t2", "sums", "attn", "at_t", "at", "pv", "ob", "sq", "ms", "ms2", "ms3", "oc", "oct_t", "oct", "proj_o",
            "x2", "h2", "h2t", "h2copy", "logits", "gexp_in", "gexp", "gates", "gates_t", "gt")}
        ex_mm, ex_prod, ex_b, ex_sum, ex_add, ex_odd, ex_out = (
            sem("ex_" + n) for n in ("mm", "prod", "xb", "sum", "add", "odd", "out"))
        tail_pool = sem("tail_pool")
        wt_t, wt_c = sem("wt_t"), sem("wt_c")
        lam_in, lam_exp = sem("lam_in"), sem("lam_exp")
        rms_rdy = sem("rms_rdy")
        LAST = Turn(B - 1)
        EARLY = TB - 1
        X1_AT, H_AT = 7, 12

        def early_bank(k):
            return W[k][:, 0:128 * (4 if k == 0 else EARLY - 4)]

        def early_x1(pe):
            for k in range(2):
                for t in range(4 * k, min(4 * k + 4, EARLY)):
                    ins = nc.tensor.transpose(W[k][:, 128 * (t % 4):128 * (t % 4) + 128],
                                              attnT[:, 128 * t:128 * t + 128], ident[:])
            ins.then_inc(ta["x1t"].sem, 1)

        def early_variances(dve, link):
            wait(dve, "x1t", Turn(0))
            dve.wait_ge(ld_res.sem, 16)
            dve.wait_ge(split.sem, split.upto(LAST, GROUPS - 1))
            for k in range(2):
                tiles = xres[:, 4 * k:min(4 * k + 4, EARLY), :].rearrange("p t d -> p (t d)")
                ins = nc.vector.tensor_tensor(tiles, early_bank(k), tiles, ALU.add)
            link(ins)
            variances(link, range(EARLY))

        def early_columns(pe):
            wait(pe, "h", Turn(0))
            for k in range(2):
                for t in range(4 * k, min(4 * k + 4, EARLY)):
                    ins = nc.tensor.transpose(W[k][:, 128 * (t % 4):128 * (t % 4) + 128], hn[:, t, :], ident[:])
            ins.then_inc(ta["ht"].sem, 1)

        def early_columns_out(act):
            wait(act, "ht", Turn(0))
            act.wait_ge(pv_done.sem, pv_done.upto(LAST.plus(-1), TILES - 1))
            for k in range(2):
                w = 128 * (4 if k == 0 else EARLY - 4)
                ins = nc.scalar.copy(hT[:, 512 * k:512 * k + w], early_bank(k))
            ins.then_inc(ta["hcopy"].sem, 1)

        def carry(pool, turn, site):
            if turn.i is not None:
                nc.gpsimd.tensor_tensor(carrier[:, site:site + 1], carrier[:, 14:15], carrier[:, 15:16], ALU.mult)

        def inverse_deviation(pool, n):
            pool.wait_ge(var_rdy.sem, n + 1)
            w = B if n < 2 else (EARLY if n == 2 else TB)
            nc.gpsimd.tensor_tensor(sm[:, 1, 0:w], sm[:, 7, 0:w], mhalf[:, 0:w], ALU.pow).then_inc(rstd_rdy.sem, 1)

        def variances(link, tiles):
            n = tiles[-1] + 1
            for t in tiles:
                ins = nc.vector.bn_stats(st[:, t, :], xres[:, t, :])
            link(ins)
            stats_combine(128, n, link).then_inc(var_rdy.sem, 1)

        def normalise_tiles(dve, tiles, turn_no):
            dve.wait_ge(rstd_rdy.sem, turn_no)
            for t in tiles:
                ins = nc.vector.tensor_scalar(hn[:, t, :], xres[:, t, :], sm[:, 0, t:t + 1], sm[:, 1, t:t + 1],
                                              ALU.subtract, ALU.mult)
            return ins

        def layer_norm(dve, link, tiles, turn_no):
            variances(link, tiles)
            return normalise_tiles(dve, tiles, turn_no)

        def small_weights_vector(dve, link):
            dve.wait_ge(ld_a.sem, LD_A)
            for k in range(2):
                ins = nc.vector.tensor_tensor(lp[:, k, :], lv[:, 2 * k, :], lv[:, 2 * k + 1, :], ALU.mult)
            link(ins)
            nc.vector.tensor_reduce(lsum[:], lp[:].rearrange("p k (h d) -> p k h d", d=SD), AX.X, ALU.add)\
              .then_inc(lam_in.sem, 1)
            nc.vector.tensor_scalar(rmsc[:], rmsc[:], 1.0 - 0.8, None, ALU.mult).then_inc(rms_rdy.sem, 1)
            nc.vector.memset(Vb[:].rearrange("p a b c -> p (a b c)"), 0.0)
            for e in range(NE):
                ins = nc.vector.memset(rank[:, e:e + 1], float(NE - e))
            link(ins)

        def lambdas_vector(dve, link):
            dve.wait_ge(lam_exp.sem, 1)
            link(nc.vector.tensor_tensor(nlam[:], lexp[:, 1, :], lexp[:, 0, :], ALU.subtract))
            link(nc.vector.tensor_scalar(nlam[:], nlam[:], -0.8, None, ALU.add))

        def small_weights_tensor(pe, g):
            if g == 0:
                pe.wait_ge(ld_a.sem, LD_A)
            if g >= 2:
                pe.wait_ge(wt_c.sem, g - 1)
            w = S[:, g % 2, :]
            if g < 3:
                for c in range(4):
                    ins = nc.tensor.transpose(w[:, 128 * c:128 * c + 128], wpad[:, g, c, :], ident[:])
            if g == 3:
                for c in range(2):
                    nc.tensor.transpose(w[:, 128 * c:128 * c + 128], wv_sb[:, c, :], ident[:])
                    ins = nc.tensor.transpose(w[:, 256 + 128 * c:384 + 128 * c], woa_sb[:, 128 * c:128 * c + 128],
                                              ident[:])
            if g == 4:
                ins = nc.tensor.transpose(w[:, 0:NE], gw_sb[:], ident[0:NE, 0:NE])
            ins.then_inc(wt_t.sem, 1)

        def small_weights_scalar(act, g):
            if g == 0:
                act.wait_ge(lam_in.sem, 1)
                nc.scalar.activation(lexp[:], lsum[:], ACT.Exp).then_inc(lam_exp.sem, 1)
            act.wait_ge(wt_t.sem, g + 1)
            w = S[:, g % 2, :]
            if g < 3:
                ins = nc.scalar.copy(wpadT[:, g, :, :].rearrange("p c n -> p (c n)"), w)
            if g == 3:
                act.wait_ge(rms_rdy.sem, 1)
                nc.scalar.copy(wvaT[:], w[:, 0:256])
                ins = nc.scalar.activation(woaT[:].rearrange("p c n -> p (c n)"), w[:, 256:512], ACT.Copy,
                                           scale=rmsc[:])
            if g == 4:
                ins = nc.scalar.copy(gwT[:], w[:, 0:NE])
            ins.then_inc(wt_c.sem, 1)

        def tile_cols(t, turn):
            if turn.i is None:
                return t[:, 128 * turn.off:128 * turn.off + 128]
            return t[:, bass.ds(turn.times(128), 128)]

        def tile_of(t, turn):
            if turn.i is None:
                return t[:, turn.off, :]
            return t[:, bass.ds(turn.times(1), 1), :].rearrange("p o d -> p (o d)")

        def wait(eng, name, turn):
            eng.wait_ge(ta[name].sem, ta[name].upto(turn))

        def first(turn):
            return turn.i is None and turn.off == 0

        def more(turn):
            return turn.i is not None or turn.off < TB - 1

        def bc(ap, n):
            return ap.unsqueeze(len(ap.shape)).to_broadcast(list(ap.shape) + [n])

        def side_bank(item, turn):
            return 1 if turn is LAST and item[0] in ("sr", "bc", "pj") else BANK[item]

        def reciprocals(dve, turn):
            dve.wait_ge(pe_item["sr"].sem, pe_item["sr"].upto(turn))
            nc.vector.reciprocal(rcol[:], W[side_bank(("sr", 0), turn)][:, 0:8]).then_inc(free["sr"].sem, 1)

        def tail_vector(dve, link):
            def last_norm():
                wait(dve, "x1t", Turn(1))
                x_ = xres[:, EARLY, :]
                link(nc.vector.tensor_tensor(x_, W[1][:, 0:128], x_, ALU.add))
                layer_norm(dve, link, range(EARLY, TB), 4).then_inc(ta["h"].sem, 1)

            def maxima(t):
                wait(dve, "scores", t)
                nc.vector.tensor_reduce(amx[:].rearrange("p g c a -> p (g c a)"),
                                        S[:].rearrange("p g (k m) -> p (g k) m", m=64), AX.X, ALU.max)\
                  .then_inc(ta["max"].sem, 1)

            def shift(t):
                wait(dve, "max", t)
                nc.vector.tensor_tensor(A[:].rearrange("p g c a m -> p (g c a) m"),
                                        S[:].rearrange("p g (k m) -> p (g k) m", m=64),
                                        bc(amx[:].rearrange("p g c a -> p (g c a)"), 64), ALU.subtract)\
                  .then_inc(ta["shifted"].sem, 1)

            def attention(t):
                wait(dve, "exp", t)
                nc.vector.tensor_reduce(asum[:].rearrange("p g c a -> p (g c a)"),
                                        E[:].rearrange("p g c a m -> p (g c a) m"), AX.X, ALU.add)\
                  .then_inc(ta["sums"].sem, 1)
                wait(dve, "sums", t)
                if not first(t):
                    wait(dve, "t2", t.plus(-1))
                nc.vector.reciprocal(arc[:], asum[:]).then_inc(ta["r"].sem, 1)
                wait(dve, "r", t)
                nc.vector.tensor_tensor(arc[:, :, :, 1], arc[:, :, :, 1], nlam[:].rearrange("p (c g) -> p g c", c=4),
                                        ALU.mult).then_inc(ta["r2"].sem, 1)
                nc.vector.tensor_tensor(t1[:], E[:, :, :, 0, :], bc(arc[:, :, :, 0], 64), ALU.mult)\
                  .then_inc(ta["t1"].sem, 1)
                wait(dve, "t1", t)
                wait(dve, "t2", t)
                if not first(t):
                    wait(dve, "at_t", t.plus(-1))
                nc.vector.tensor_tensor(At[:].rearrange("p (c g) m -> p g c m", c=4), t1[:], t2[:], ALU.add)\
                  .then_inc(ta["attn"].sem, 1)

            def mean_squares(t):
                wait(dve, "ob", t)
                nc.vector.tensor_tensor(Osq[:], Ob[:], Ob[:], ALU.mult).then_inc(ta["sq"].sem, 1)
                wait(dve, "sq", t)
                nc.vector.tensor_reduce(oms[:, 0, :], Osq[:].rearrange("p (h d) -> p h d", h=SH), AX.X, ALU.add)\
                  .then_inc(ta["ms"].sem, 1)
                wait(dve, "ms", t)
                nc.vector.tensor_scalar(oms[:, 1, :], oms[:, 0, :], 1.0 / (2 * SD), EPS, ALU.mult, ALU.add)\
                  .then_inc(ta["ms2"].sem, 1)

            def group_norm(t):
                wait(dve, "ms3", t)
                if not first(t):
                    wait(dve, "oct_t", t.plus(-1))
                nc.vector.tensor_tensor(Oc[:].rearrange("p (h d) -> p h d", h=SH),
                                        Ob[:].rearrange("p (h d) -> p h d", h=SH), bc(oms[:, 2, :], 2 * SD),
                                        ALU.mult).then_inc(ta["oc"].sem, 1)

            def residual(t):
                wait(dve, "proj_o", t)
                nc.vector.tensor_tensor(tile_of(xres, t), W[1][:, 256:384], tile_of(xres, t), ALU.add)\
                  .then_inc(ta["x2"].sem, 1)

            denominators(dve, nc.vector, LAST)
            reciprocals(dve, LAST)
            diagonals(dve, nc.vector, LAST)
            normalise_outputs(dve, nc.vector, LAST)
            outputs_low(dve, nc.vector, LAST)
            maxima(Turn(0))
            shift(Turn(0))
            def middle(t, last_but_one=True, last=True, following=True):
                if last:
                    mean_squares(t.plus(-1))
                attention(t)
                if last_but_one:
                    residual(t.plus(-2))
                if last:
                    group_norm(t.plus(-1))
                if following:
                    maxima(t.plus(1))
                    shift(t.plus(1))
            middle(Turn(0), last_but_one=False, last=False)
            last_norm()
            middle(Turn(1), last_but_one=False)
            with dve.Fori(0, TB - 3) as i:
                middle(Turn(2, i, 1))
            t = Turn(TB - 1)
            middle(t, following=False)
            residual(t.plus(-1))
            mean_squares(t)
            group_norm(t)
            residual(t)
            wait(dve, "x2", t)
            layer_norm(dve, link, range(TB), 5).then_inc(ta["h2"].sem, 1)

            L = lambda k: lg[:, k, :, :]
            rk = rank[:].unsqueeze(1).to_broadcast([128, TB, NE])
            wait(dve, "logits", Turn(0))
            link(nc.vector.tensor_tensor(L(0), W[0][:, 0:64].rearrange("p (t e) -> p t e", t=TB),
                                         gbias[:].unsqueeze(1).to_broadcast([128, TB, NE]), ALU.add))

            def largest(src, dst, tmp, mxi, m2i):
                link(nc.vector.tensor_reduce(g1[:, mxi, :], src, AX.X, ALU.max))
                link(nc.vector.tensor_tensor(tmp, src, bc(g1[:, mxi, :], NE), ALU.is_equal))
                link(nc.vector.tensor_tensor(tmp, tmp, rk, ALU.mult))
                link(nc.vector.tensor_reduce(g1[:, m2i, :], tmp, AX.X, ALU.max))
                link(nc.vector.tensor_tensor(dst, tmp, bc(g1[:, m2i, :], NE), ALU.is_equal))

            largest(L(0), L(1), L(2), 0, 1)
            nc.vector.tensor_tensor(L(8), L(0), bc(g1[:, 0, :], NE), ALU.subtract).then_inc(ta["gexp_in"].sem, 1)
            link(nc.vector.scalar_tensor_tensor(L(3), L(1), -3e38, L(0), ALU.mult, ALU.add))
            largest(L(3), L(4), L(2), 2, 1)
            link(nc.vector.tensor_tensor(L(5), L(1), L(4), ALU.add))
            wait(dve, "gexp", Turn(0))
            link(nc.vector.tensor_tensor(L(6), L(9), L(5), ALU.mult))
            link(nc.vector.tensor_reduce(g1[:, 3, :], L(6), AX.X, ALU.add))
            link(nc.vector.reciprocal(g1[:, 2, :], g1[:, 3, :]))
            link(nc.vector.tensor_tensor(L(7), L(6), bc(g1[:, 2, :], NE), ALU.mult))
            nc.vector.tensor_copy(L(8), L(7)).then_inc(ta["gates"].sem, 1)
            for t in range(TB):
                dve.wait_ge(ex_mm.sem, t + 1)
                if t >= 2 and t % 2 == 0:
                    dve.wait_ge(ex_add.sem, t // 2)
                nc.vector.tensor_tensor(prod[t % 2][:], S[:, 2 * (t % 2):2 * (t % 2) + 2, :].rearrange(
                    "p a (e o) -> p (a e) o", o=D), bc(lg[:, 7, t, :], D), ALU.mult).then_inc(ex_prod.sem, 1)
                nc.vector.tensor_tensor(xb[:, t, :], W[t % 2][:, 0:128], xres[:, t, :], ALU.add).then_inc(ex_b.sem, 1)
                if t % 2 == 1:
                    dve.wait_ge(ex_prod.sem, t + 1)
                    nc.vector.tensor_reduce(esum[:], prod[1][:].rearrange("p e o -> p o e"), AX.X, ALU.add)\
                      .then_inc(ex_sum.sem, 1)
                    dve.wait_ge(ex_sum.sem, t // 2 + 1)
                    nc.vector.tensor_tensor(xb[:, t, :], xb[:, t, :], esum[:], ALU.add).then_inc(ex_odd.sem, 1)

        def tail_gpsimd(pool):
            def columns(t):
                wait(pool, "hcopy", Turn(1) if t.i is not None or t.off > 1 else Turn(0))
                if not first(t):
                    wait(pool, "projv", t.plus(-1))
                src = tile_cols(hT, t).rearrange("p (j n) -> p j n", j=2)
                carry(pool, t, 0 + 0)
                nc.gpsimd.tensor_copy(hTd[:, :, 0, :], src)
                nc.gpsimd.tensor_copy(hTd[:, :, 1, :], src).then_inc(ta["hd"].sem, 1)

            def second_map(t):
                wait(pool, "r2", t)
                nc.gpsimd.tensor_tensor(t2[:], E[:, :, :, 1, :], bc(arc[:, :, :, 1], 64), ALU.mult)\
                  .then_inc(ta["t2"].sem, 1)

            def inverse_rms(t):
                wait(pool, "ms2", t)
                nc.gpsimd.tensor_tensor(oms[:, 2, :], oms[:, 1, :], mhalf[:], ALU.pow).then_inc(ta["ms3"].sem, 1)

            inverse_deviation(pool, 2)
            columns(Turn(0))
            columns(Turn(1))
            second_map(Turn(0))
            def middle(t):
                columns(t.plus(1))
                second_map(t)
                inverse_rms(t.plus(-1))
            inverse_deviation(pool, 3)
            middle(Turn(1))
            with pool.Fori(0, TB - 3) as i:
                middle(Turn(2, i, 1))
            t = Turn(TB - 1)
            second_map(t)
            inverse_rms(t.plus(-1))
            inverse_rms(t)
            inverse_deviation(pool, 4)
            n = 0
            for t in range(0, TB, 2):
                pool.wait_ge(ex_prod.sem, t + 1)
                pr = prod[0]
                for m in (4, 2, 1):
                    nc.gpsimd.tensor_tensor(pr[:, 0:m, :], pr[:, 0:m, :], pr[:, m:2 * m, :], ALU.add)\
                      .then_inc(tail_pool.sem, 1)
                    n += 1
                    pool.wait_ge(tail_pool.sem, n)
                pool.wait_ge(ex_b.sem, t + 1)
                nc.gpsimd.tensor_tensor(xb[:, t, :], xb[:, t, :], pr[:, 0, :], ALU.add).then_inc(ex_add.sem, 1)

        def tail_scalar(act, reciprocals_out, outputs_high, projected):
            def queries_keys(t):
                wait(act, "projqk", t)
                nc.scalar.copy(Ks[:, :, :, 0, :], OA[:, 1, :].rearrange("p (c j m) -> p c j m", c=4, j=2))
                nc.scalar.copy(Ks[:, :, :, 1, :], W[0][:].rearrange("p (c j m) -> p c j m", c=4, j=2))
                nc.scalar.copy(Qs[:].rearrange("p c n -> p (c n)"), OA[:, 0, :]).then_inc(ta["qk"].sem, 1)

            def values(t):
                wait(act, "projv", t)
                if first(t):
                    act.wait_ge(ld_a.sem, LD_A)
                v = OA[:, 0, :].rearrange("p (j h d) -> p j h d", j=2, h=8)
                nc.scalar.copy(Vb[0:64, :, :, 0:16], v[0:64, :, :, 0:16])
                nc.scalar.copy(Vb[64:128, :, :, 16:32], v[64:128, :, :, 16:32]).then_inc(ta["vb"].sem, 1)

            def exp(t):
                wait(act, "shifted", t)
                if not first(t):
                    wait(act, "attn", t.plus(-1))
                nc.scalar.activation(E[:].rearrange("p g c a m -> p (g c a m)"),
                                     A[:].rearrange("p g c a m -> p (g c a m)"), ACT.Exp, scale=SD ** -0.5)\
                  .then_inc(ta["exp"].sem, 1)

            def weights(t):
                wait(act, "at_t", t)
                nc.scalar.copy(AT[:].rearrange("p h n -> p (h n)"), OA[:].rearrange("p a n -> p (a n)"))\
                  .then_inc(ta["at"].sem, 1)

            def outputs(t):
                wait(act, "pv", t)
                if not first(t):
                    wait(act, "oc", t.plus(-1))
                nc.scalar.copy(Ob[:], W[0][:, 0:256]).then_inc(ta["ob"].sem, 1)

            def columns_out(t):
                wait(act, "oct_t", t)
                nc.scalar.copy(OcT[:].rearrange("p c n -> p (c n)"), W[1][:, 0:256]).then_inc(ta["oct"].sem, 1)

            queries_keys(Turn(0))
            for k in range(2):
                reciprocals_out(LAST, k)
            values(Turn(0))
            for k in range(2):
                outputs_high(LAST, k)
            queries_keys(Turn(1))
            exp(Turn(0))
            def middle(t, last=True, following=True, next_but_one=True):
                weights(t)
                if last:
                    columns_out(t.plus(-1))
                if following:
                    exp(t.plus(1))
                outputs(t)
                if following:
                    values(t.plus(1))
                if next_but_one:
                    queries_keys(t.plus(2))
            projected(LAST)
            middle(Turn(0), last=False)
            wait(act, "ht", Turn(1))
            nc.scalar.copy(hT[:, 128 * EARLY:128 * TB], W[1][:, 0:128]).then_inc(ta["hcopy"].sem, 1)
            with act.Fori(0, TB - 3) as i:
                middle(Turn(1, i, 1))
            middle(Turn(TB - 2), next_but_one=False)
            middle(Turn(TB - 1), following=False, next_but_one=False)
            columns_out(Turn(TB - 1))
            wait(act, "h2t", Turn(0))
            nc.scalar.copy(hT[:], S[:, 0:2, :].rearrange("p a n -> p (a n)")).then_inc(ta["h2copy"].sem, 1)
            wait(act, "gexp_in", Turn(0))
            nc.scalar.activation(lg[:, 9, :, :], lg[:, 8, :, :], ACT.Exp).then_inc(ta["gexp"].sem, 1)
            wait(act, "gates_t", Turn(0))
            nc.scalar.copy(gT[:], OA[0:NE, :, :].rearrange("p a n -> p (a n)")).then_inc(ta["gt"].sem, 1)

        def tail_tensor(pe, side_item):
            mm = nc.tensor.matmul

            def project(t):
                if first(t):
                    pe.wait_ge(oa_free.sem, oa_free.upto(LAST))
                    pe.wait_ge(free["ol"].sem, free["ol"].upto(LAST, 1))
                    wait(pe, "hcopy", t)
                else:
                    wait(pe, "qk", t.plus(-1))
                    if t.i is not None or t.off >= 2:
                        wait(pe, "ob", t.plus(-2))
                for kind, dst in ((1, OA[:, 1, :]), (2, W[0][:]), (0, OA[:, 0, :])):
                    if kind == 0 and not first(t):
                        wait(pe, "vb", t.plus(-1))
                    for c in range(4):
                        ins = mm(dst[:, 128 * c:128 * c + 128], wpadT[:, kind, c, :], tile_cols(hT, t),
                                 start=True, stop=True)
                ins.then_inc(ta["projqk"].sem, 1)

            def project_values(t):
                wait(pe, "hd", t)
                if first(t):
                    wait(pe, "qk", t)
                for j in range(2):
                    ins = mm(OA[:, 0, 256 * j:256 * j + 256], hTd[:, j, :, :].rearrange("p a n -> p (a n)"), wvaT[:],
                             start=True, stop=True)
                ins.then_inc(ta["projv"].sem, 1)

            def self_scores(t):
                if not first(t):
                    wait(pe, "shifted", t.plus(-1))
                else:
                    pe.wait_ge(lo_done.sem, lo_done.upto(LAST, LAT))
                wait(pe, "qk", t)
                for c in range(4):
                    for j in range(2):
                        for g in range(4):
                            r = slice(32 * g, 32 * g + 32)
                            mm(S[64 * j:64 * j + 64, g, 128 * c:128 * c + 128], identb[:, 64 * j:64 * j + 64],
                               mask[:].unsqueeze(1).to_broadcast([128, 2, NQ]), start=True, stop=False)
                            ins = mm(S[64 * j:64 * j + 64, g, 128 * c:128 * c + 128], Qs[r, c, 64 * j:64 * j + 64],
                                     Ks[r, c, j, :, :].rearrange("p a m -> p (a m)"), start=False, stop=True,
                                     tile_position=(32 * g, 64 * j))
                ins.then_inc(ta["scores"].sem, 1)

            def transpose_attention(t):
                wait(pe, "attn", t)
                wait(pe, "vb", t)
                for h in range(8):
                    ins = nc.tensor.transpose(OA[:, h // 4, 128 * (h % 4):128 * (h % 4) + 128],
                                              At[:, 2 * h:2 * h + 2, :].rearrange("p a m -> p (a m)"), ident[:])
                ins.then_inc(ta["at_t"].sem, 1)

            def weigh_values(t):
                wait(pe, "at", t)
                for j in range(2):
                    for h in range(8):
                        ins = mm(W[0][64 * j:64 * j + 64, 32 * h:32 * h + 32], AT[:, h, 64 * j:64 * j + 64],
                                 Vb[:, j, h, :], start=True, stop=True)
                ins.then_inc(ta["pv"].sem, 1)

            def transpose_outputs(t):
                wait(pe, "oc", t)
                for c in range(2):
                    ins = nc.tensor.transpose(W[1][:, 128 * c:128 * c + 128], Oc[:, 128 * c:128 * c + 128], ident[:])
                ins.then_inc(ta["oct_t"].sem, 1)

            def project_out(t):
                wait(pe, "oct", t)
                if not first(t):
                    wait(pe, "x2", t.plus(-1))
                for c in range(2):
                    ins = mm(W[1][:, 256:384], OcT[:, c, :], woaT[:, c, :], start=(c == 0), stop=(c == 1))
                ins.then_inc(ta["proj_o"].sem, 1)

            side_item(("sr", 0), LAST)
            project(Turn(0))
            side_item(("bc", 0), LAST)
            self_scores(Turn(0))
            side_item(("bc", 1), LAST)
            project_values(Turn(0))
            project(Turn(1))
            side_item(("pj", 0), LAST)
            def middle(t, last=True, following=True, next_but_one=True):
                if following:
                    self_scores(t.plus(1))
                transpose_attention(t)
                if last:
                    transpose_outputs(t.plus(-1))
                weigh_values(t)
                if following:
                    project_values(t.plus(1))
                if next_but_one:
                    project(t.plus(2))
                if last:
                    project_out(t.plus(-1))
            middle(Turn(0), last=False)
            pe.wait_ge(free["pj"].sem, free["pj"].upto(LAST))
            nc.tensor.transpose(W[1][:, 0:128], attnT[:, 128 * EARLY:128 * TB], ident[:]).then_inc(ta["x1t"].sem, 1)
            wait(pe, "h", Turn(1))
            nc.tensor.transpose(W[1][:, 0:128], hn[:, EARLY, :], ident[:]).then_inc(ta["ht"].sem, 1)
            wait(pe, "hcopy", Turn(1))
            with pe.Fori(0, TB - 3) as i:
                middle(Turn(1, i, 1))
            middle(Turn(TB - 2), next_but_one=False)
            t = Turn(TB - 1)
            middle(t, following=False, next_but_one=False)
            transpose_outputs(t)
            project_out(t)

            wait(pe, "h2", Turn(0))
            for t in range(TB):
                ins = nc.tensor.transpose(S[:, t // 4, 128 * (t % 4):128 * (t % 4) + 128], hn[:, t, :], ident[:])
            ins.then_inc(ta["h2t"].sem, 1)
            wait(pe, "h2copy", Turn(0))
            wait(pe, "x2", Turn(TB - 1))
            for t in range(TB):
                ins = mm(W[0][:, NE * t:NE * t + NE], hT[:, 128 * t:128 * t + 128], gwT[:], start=True, stop=True)
            ins.then_inc(ta["logits"].sem, 1)

            def experts(t):
                if t >= 2:
                    pe.wait_ge(ex_prod.sem, t - 1)
                for c in range(2):
                    mm(S[:, 2 * (t % 2) + c, :], hT[:, 128 * t:128 * t + 128],
                       ew[:, 4 * c:4 * c + 4, :].rearrange("p e o -> p (e o)"), start=True, stop=True)

            def expert_bias(t):
                if t >= 2:
                    pe.wait_ge(ex_b.sem, t - 1)
                mm(W[t % 2][:, 0:128], gT[:, 128 * t:128 * t + 128], eb[:], start=True, stop=True)\
                    .then_inc(ex_mm.sem, 1)

            pe.wait_ge(ld_ew.sem, 16)
            experts(0)
            experts(1)
            wait(pe, "gates", Turn(0))
            for t in range(TB):
                ins = nc.tensor.transpose(OA[0:NE, t // 4, 128 * (t % 4):128 * (t % 4) + 128], lg[:, 8, t, :], ident[:])
            ins.then_inc(ta["gates_t"].sem, 1)
            wait(pe, "gt", Turn(0))
            expert_bias(0)
            expert_bias(1)
            for t in range(2, TB):
                experts(t)
                expert_bias(t)


        block = es.enter_context(nc.Block())

        @block.sync
        def _(sp):
            with nc.allow_non_contiguous_dma(reason="columns of gains and biases"):
                for k, v in enumerate((ln1_g, ln1_b, ln2_g, ln2_b)):
                    sp.dma_start(gb[:, k:k + 1], v.rearrange("(p o) -> p o", o=1)).then_inc(ld_gb.sem, 16)
                for k, v in enumerate((ln1_g, ln2_g)):
                    sp.dma_start(g0row[0:1, k, :], v[0:1].rearrange("(o n) -> o n", o=1)).then_inc(ld_gb.sem, 16)
            sp.dma_start(lx[:], x.rearrange("b q d -> q b d")).then_inc(ld_x.sem, 16)
            sp.dma_start(wq_sb[:], Wq).then_inc(ld_w.sem, 16)
            sp.dma_start(wkv_sb[:], Wkv).then_inc(ld_w.sem, 16)
            sp.dma_start(wo_sb[:], Wo.rearrange("(n p) d -> p n d", p=128)).then_inc(ld_w.sem, 16)
            load_raw(sp, Turn(0))
            load_raw(sp, Turn(1))
            sp.wait_ge(padded.sem, 1)
            for j in range(4):
                for kind, wt, r0, r1 in ((0, aWq, 0, 16), (1, aWk, 0, 8), (2, aWk, 8, 16)):
                    src = wt.rearrange("(c j k) d -> j k c d", c=4, j=4)[j, r0:r1]
                    sp.dma_start(wpad[32 * j + r0:32 * j + r1, kind, :, :], src).then_inc(ld_a.sem, 16)
            sp.dma_start(wv_sb[:], aWv.rearrange("(c p) d -> p c d", p=128)).then_inc(ld_a.sem, 16)
            sp.dma_start(woa_sb[:], aWo).then_inc(ld_a.sem, 16)
            for k, v in enumerate((lq1, lk1, lq2, lk2)):
                sp.dma_start(lv[:, k, :], v.rearrange("h (o d) -> o (h d)", o=1).to_broadcast([128, 128]))\
                  .then_inc(ld_a.sem, 16)
            with nc.allow_non_contiguous_dma(reason="one scale per row"):
                for h in range(8):
                    sp.dma_start(rmsc[16 * h:16 * h + 16, :], rms_scale.rearrange("(p o) -> p o", o=1))\
                      .then_inc(ld_a.sem, 16)
            sp.dma_start(gw_sb[:], gate_w).then_inc(ld_a.sem, 16)
            sp.dma_start(gbias[:], gate_b.rearrange("(o e) -> o e", o=1).to_broadcast([128, NE])).then_inc(ld_a.sem, 16)
            sp.dma_start(eb[:], expert_b).then_inc(ld_a.sem, 16)

            with sp.Fori(0, B // 2 - 1) as i:
                for off in (2, 3):
                    n = Turn(off, i)
                    sp.wait_ge(split.sem, split.upto(n.plus(-2), GROUPS - 1))
                    load_raw(sp, n)

            sp.wait_ge(split.sem, split.upto(LAST.plus(-1), GROUPS - 1))
            sp.dma_start(xres[:], x.rearrange("(t j) q d -> (j q) t d", j=2)).then_inc(ld_res.sem, 16)
            sp.wait_ge(free["pj"].sem, free["pj"].upto(LAST))
            sp.dma_start(ew[:], expert_w.rearrange("e d o -> d e o")).then_inc(ld_ew.sem, 16)
            for t in range(TB):
                done = ex_odd if t % 2 else ex_add
                sp.wait_ge(done.sem, t // 2 + 1)
                sp.dma_start(out[2 * t:2 * t + 2].rearrange("j q d -> (j q) d"), xb[:, t, :]).then_inc(ex_out.sem, 16)
            sp.wait_ge(ex_out.sem, 16 * TB)
        @block.vector
        def _(dve):
            chain = [0]

            def link(ins):
                chain[0] += 1
                ins.then_inc(dve_link.sem, 1)
                dve.wait_ge(dve_link.sem, chain[0])

            def statistics(turn, u):
                if u == 0:
                    dve.wait_ge(ld_raw[turn.off % 2].sem, raw_loaded(turn))
                    if not (turn.i is None and turn.off == 0):
                        dve.wait_ge(normed.sem, normed.upto(turn.plus(-1)))
                for t in STATS_AT.get(u, ()):
                    ins = bn(turn, t)
                if u == 3:
                    k = [0]

                    def step(ins):
                        ins.then_inc(dve_step.sem, 1)
                        dve.wait_ge(dve_step.sem, dve_step.upto(turn, k[0]))
                        k[0] += 1
                    step(ins)
                    last = stats_combine(128, TILES, step, half=-0.5, st=stc, sm=smc)
                    last.then_inc(stats_ok.sem, 1)

            def split_high(turn, g):
                if g == 0:
                    dve.wait_ge(normed.sem, normed.upto(turn))
                    if not (turn.i is None and turn.off < 2):
                        dve.wait_ge(pv_done.sem, pv_done.upto(turn.plus(-2), TILES - 1))
                nc.vector.tensor_copy(token_group(xk_hi, turn, g), token_group(raw, turn, g)).then_inc(split_hi.sem, 1)

            nc.vector.memset(st[:], 0.0)
            nc.vector.memset(stc[:], 0.0)
            nc.vector.memset(ones[:], 1.0)
            nc.vector.memset(oscale[:], 1.0 / OSCALE)
            link(nc.vector.memset(ones16[:], 1.0))
            dve.wait_ge(consts.sem, 1)
            dve.wait_ge(ld_gb.sem, 96)
            dve.wait_ge(consts.sem, 2)
            for k in range(2):
                ins = nc.vector.tensor_scalar(fold[:, k, :], ident[:], gb[:, 2 * k:2 * k + 1], None, ALU.mult)
            link(ins)
            for k in range(2):
                ins = nc.vector.tensor_scalar(fold[0:1, k, :], ones[0:1, :], g0row[0:1, k, :], -1.0, ALU.mult, ALU.mult)
            link(ins)
            for k in range(2):
                ins = nc.vector.tensor_copy(fold[:, k, 0:1], gb[:, 2 * k + 1:2 * k + 2])
            ins.then_inc(folded.sem, 1)
            dve.wait_ge(ld_x.sem, 16)
            for rnd in range(2):
                for b in range(B):
                    ins = nc.vector.bn_stats(st[0:NQ, b, :], lx[:, b, :])
                link(ins)
                stats_combine(NQ, B, link).then_inc(var_rdy.sem, 1)
                if rnd == 0:
                    for u in range(4):
                        statistics(Turn(0), u)
                if rnd == 1:
                    dve.wait_ge(ev_w.sem, FOLDS)
                    nc.vector.tensor_reduce(amax[:, 0:1], wvT[:].rearrange("p n c -> p (n c)"), AX.X, ALU.max,
                                            apply_absolute_value=True)
                    nc.vector.tensor_reduce(amax[:, 1:2], wo_sb[:].rearrange("p n c -> p (n c)"), AX.X, ALU.max,
                                            apply_absolute_value=True).then_inc(amax_rdy.sem, 1)
                dve.wait_ge(rstd_rdy.sem, rnd + 1)
                for b in range(B):
                    ins = nc.vector.tensor_scalar(lx[:, b, :], lx[:, b, :], sm[0:NQ, 0, b:b + 1],
                                                  sm[0:NQ, 1, b:b + 1], ALU.subtract, ALU.mult)
                link(ins)
            nc.vector.memset(lx[:, :, 0:1], 1.0).then_inc(lat_rdy.sem, 1)
            dve.wait_ge(amax_all.sem, 1)
            link(nc.vector.tensor_tensor(wscale[:, 1:2], amax[:, 3:4], amax[:, 4:5], ALU.mult))
            link(nc.vector.tensor_scalar(wscale[:, 1:2], wscale[:, 1:2], 1e-30, DH / WMAX, ALU.max, ALU.mult))
            link(nc.vector.reciprocal(wscale[:, 0:1], wscale[:, 1:2]))
            nc.vector.tensor_scalar(wscale[:, 1:2], wscale[:, 1:2], 1.0 / OSCALE, None, ALU.mult)\
              .then_inc(wscale_rdy.sem, 1)
            dve.wait_ge(ev_w.sem, FOLDS + H)
            link(nc.vector.tensor_tensor(G[:, :, 128:129], G[:, :, 128:129], G[:, :, 0:1], ALU.subtract))
            link(nc.vector.memset(G[:, :, 0:1], 0.0))
            nc.vector.tensor_reduce(amax[:, 2:3], G[:].rearrange("p h c -> p (h c)"), AX.X, ALU.max,
                                    apply_absolute_value=True).then_inc(amax_rdy.sem, 1)
            dve.wait_ge(lat_t.sem, 1)
            nc.vector.tensor_copy(lT[:], S[:, 0:2, :].rearrange("p a n -> p (a n)")).then_inc(lat_cp.sem, 1)
            dve.wait_ge(amax_all.sem, 2)
            link(nc.vector.tensor_scalar(sigma[:, 0:1], amax[:, 5:6], 1e-30, 129.0 / QMAX, ALU.max, ALU.mult))
            nc.vector.reciprocal(sigma[:, 1:2], sigma[:, 0:1]).then_inc(sigma_rdy.sem, 1)
            dve.wait_ge(lat_hi.sem, 1)
            dve.wait_ge(lat_cp.sem, 1)
            nc.vector.tensor_tensor(lT_lo[:], lT[:], lT_hi[:], ALU.subtract).then_inc(lat_lo.sem, 1)
            for g in range(GROUPS):
                split_high(Turn(0), g)
            dve.wait_ge(sigma_rdy.sem, 1)
            for k in range(2):
                dve.wait_ge(g_hi_rdy.sem, k + 1)
                h = slice(8 * k, 8 * k + 8)
                nc.vector.scalar_tensor_tensor(G_lo[:, h].rearrange("p h c -> p (h c)"),
                                               G[:, h].rearrange("p h c -> p (h c)"), sigma[:, 1:2],
                                               G_hi[:, h].rearrange("p h c -> p (h c)"), ALU.mult, ALU.subtract)\
                  .then_inc(g_rdy.sem, 1)
            dve.wait_ge(lat_rdy.sem, 1)
            link(nc.vector.tensor_copy(lk_hi[:], lx[:]))
            nc.vector.tensor_tensor(lk_lo[:], lx[:], lk_hi[:], ALU.subtract).then_inc(lat_lo.sem, 1)

            def queries_low(turn, c):
                dve.wait_ge(q_hi_done.sem, q_hi_done.upto(turn, c))
                cols = slice(c * HALF, (c + 1) * HALF)
                p = turn.off % 2
                nc.vector.tensor_tensor(q_lo[p][:, cols], W[BANK[("q", c)]][:], q_hi[p][:, cols], ALU.subtract)\
                  .then_inc(free["q"].sem, 1)

            def maxima(turn, n):
                dve.wait_ge(pe_item["m"].sem, pe_item["m"].upto(turn, n))
                r, c = M_ORDER[n]
                if n == 0 and not (turn.i is None and turn.off == 0):
                    dve.wait_ge(m16_done.sem, m16_done.upto(turn.plus(-1)))
                width = 512 if c < 3 else REST + NQ
                nc.vector.tensor_reduce(mx[:, r, c:c + 1], W[BANK[("m", n)]][:, 0:width], AX.X, ALU.max)\
                  .then_inc(free["m"].sem, 1)
                if n == MAXIMA - 1:
                    dve.wait_ge(free["m"].sem, free["m"].upto(turn, n))
                    if not (turn.i is None and turn.off == 0):
                        dve.wait_ge(pe_item["mt"].sem, pe_item["mt"].upto(turn.plus(-1), 1))
                    nc.vector.tensor_reduce(m16[:], mx[:], AX.X, ALU.max, negate=True).then_inc(m16_done.sem, 1)

            def low_part(turn, u):
                r, k = rows_of(u), pbuf(turn, u)
                dve.wait_ge(e_done.sem, e_done.upto(turn, u))
                src = S[0:r, 2 * (u % 2):2 * (u % 2) + 2, :].rearrange("p a n -> p (a n)")
                nc.vector.tensor_tensor(p_lo[k][0:r, :], src, p_hi[k][0:r, :], ALU.subtract)\
                  .then_inc(lo_done.sem, 1)

            def slot(b, prep=True, post=True, stats=True):
                nxt = b.plus(1)
                for u in range(UNITS):
                    if stats:
                        statistics(b.plus(2), u)
                    for kind, k in PLAN[u][0] + PLAN[u][1]:
                        if kind == "q" and prep:
                            queries_low(nxt, k)
                        if kind == "m" and prep:
                            maxima(nxt, k)
                        if kind == "sr" and post:
                            reciprocals(dve, b.plus(-1))
                    if b is LAST and u == X1_AT + 1:
                        early_variances(dve, link)
                    if b is LAST and u == H_AT - 1:
                        normalise_tiles(dve, range(EARLY), 3).then_inc(ta["h"].sem, 1)
                    low_part(b, u)
                    if prep and u < 2:
                        split_high(nxt, 2 * u)
                        split_high(nxt, 2 * u + 1)

            for early, late in PLAN:
                for kind, k in early + late:
                    if kind == "q":
                        queries_low(Turn(0), k)
                    if (kind, k) == ("t", 3):
                        for u in range(4):
                            statistics(Turn(1), u)
                        small_weights_vector(dve, link)
                    if kind == "m":
                        maxima(Turn(0), k)
                        if k in WO_AFTER:
                            h = WO_AFTER[k]
                            dve.wait_ge(ev_w.sem, FOLDS + H + h + 1)
                            nc.vector.scalar_tensor_tensor(WO_lo[:, h, :], wo_banks[h % 4], wscale[:, 0:1],
                                                           WO_hi[:, h, :], ALU.mult, ALU.subtract)\
                              .then_inc(wo_lo_done.sem, 1)
            lambdas_vector(dve, link)
            slot(Turn(0), post=False)
            with dve.Fori(0, B // 2 - 2) as i:
                slot(Turn(1, i))
                slot(Turn(2, i))
            slot(Turn(B - 3))
            slot(Turn(B - 2), stats=False)
            slot(LAST, prep=False, stats=False)
            tail_vector(dve, link)

        @block.gpsimd
        def _(pool):
            nc.gpsimd.memset(wpad[:].rearrange("p a b c -> p (a b c)"), 0.0).then_inc(padded.sem, 1)
            nc.gpsimd.memset(sm[:].rearrange("p a b -> p (a b)"), 1.0)
            nc.gpsimd.memset(mhalf[:], -0.5)
            nc.gpsimd.memset(carrier[:], 0.0)
            nc.gpsimd.memset(mask[:], 0.0).then_inc(pool_link.sem, 1)
            nc.gpsimd.memset(ident[:], 0.0).then_inc(pool_link.sem, 1)
            pool.wait_ge(pool_link.sem, 2)
            nc.gpsimd.affine_select(out=ident[:], in_=ident[:], compare_op=ALU.not_equal, fill=1.0, base=0,
                                    pattern=[[-1, 128]], channel_multiplier=1).then_inc(consts.sem, 1)
            pool.wait_ge(consts.sem, 1)
            nc.gpsimd.tensor_copy(identb[:], ident[:])
            nc.gpsimd.tensor_copy(ident16[:], ident[:]).then_inc(consts.sem, 1)
            for j in range(2):
                pool.wait_ge(consts.sem, 2 + j)
                nc.gpsimd.affine_select(out=mask[64 * j:64 * j + 64, :], in_=mask[64 * j:64 * j + 64, :],
                                        compare_op=ALU.is_ge, fill=-3e38, base=0,
                                        pattern=[[-1, NQ]], channel_multiplier=1).then_inc(consts.sem, 1)
            pool.wait_ge(consts.sem, 4)
            for p in range(2):
                nc.gpsimd.memset(xk_hi[p][:, :, 0:1], 1.0)
                ins = nc.gpsimd.memset(xk_lo[p][:, :, 0:1], 0.0)
            ins.then_inc(pool_link.sem, 1)
            pool.wait_ge(pool_link.sem, 3)

            def inverse_deviation_ctx(turn):
                pool.wait_ge(stats_ok.sem, stats_ok.upto(turn))
                nc.gpsimd.tensor_tensor(smc[:, 1, :], smc[:, 7, :], mhalf[:, 0:TILES], ALU.pow)\
                  .then_inc(rstd_step.sem, 1)
                pool.wait_ge(rstd_step.sem, rstd_step.upto(turn))
                nc.gpsimd.tensor_tensor(smc[:, 2, :], smc[:, 0, :], smc[:, 1, :], ALU.mult)\
                  .then_inc(rstd_ctx.sem, 1)

            def split_tokens(turn):
                for g in range(GROUPS):
                    lo, hi, f = token_group(xk_lo, turn, g), token_group(xk_hi, turn, g), token_group(raw, turn, g)
                    pool.wait_ge(split_hi.sem, split_hi.upto(turn, g))
                    nc.gpsimd.tensor_tensor(lo, f, hi, ALU.subtract).then_inc(split.sem, 1)

            def at64(t, turn):
                if turn.i is None:
                    return t[:, 64 * turn.off:64 * turn.off + 64]
                return t[:, bass.ds(turn.times(64), 64)]

            def at_batch(t, turn):
                if turn.i is None:
                    return t[:, turn.off, :]
                return t[:, bass.ds(turn.times(1), 1), :].rearrange("p o d -> p (o d)")

            def current_T(turn):
                p = turn.off % 2
                if not (turn.i is None and turn.off < 2):
                    pool.wait_ge(s_done.sem, s_done.upto(turn.plus(-2), LAT))
                carry(pool, turn, 6 + turn.off % 2)
                nc.gpsimd.tensor_copy(cT_hi[p][:], at64(lT_hi, turn))
                nc.gpsimd.tensor_copy(cT_lo[p][:], at64(lT_lo, turn)).then_inc(curT.sem, 1)

            def current_k(turn):
                p = turn.off % 2
                if not (turn.i is None and turn.off < 2):
                    pool.wait_ge(pv_done.sem, pv_done.upto(turn.plus(-2), LAT))
                carry(pool, turn, 8 + turn.off % 2)
                nc.gpsimd.tensor_copy(ck_hi[p][:], at_batch(lk_hi, turn))
                nc.gpsimd.tensor_copy(ck_lo[p][:], at_batch(lk_lo, turn)).then_inc(curk.sem, 1)

            def slot(b, prep=True, post=True, stats=True):
                if prep:
                    current_T(b.plus(1))
                    split_tokens(b.plus(1))
                    current_k(b.plus(1))
                if post:
                    denominators(pool, nc.gpsimd, b.plus(-1))
                if stats:
                    inverse_deviation_ctx(b.plus(2))
                if post:
                    diagonals(pool, nc.gpsimd, b.plus(-1))
                    normalise_outputs(pool, nc.gpsimd, b.plus(-1))
                    outputs_low(pool, nc.gpsimd, b.plus(-1))

            inverse_deviation(pool, 0)
            inverse_deviation_ctx(Turn(0))
            inverse_deviation(pool, 1)
            for k, (c0, c1) in enumerate(((0, 2), (2, 3))):
                pool.wait_ge(amax_rdy.sem, k + 1)
                nc.gpsimd.partition_all_reduce(amax[:, 3 + c0:3 + c1], amax[:, c0:c1], 128, bass.bass_isa.ReduceOp.max)\
                  .then_inc(amax_all.sem, 1)
            pool.wait_ge(lat_lo.sem, 1)
            current_T(Turn(0))
            split_tokens(Turn(0))
            pool.wait_ge(lat_lo.sem, 2)
            current_k(Turn(0))
            inverse_deviation_ctx(Turn(1))
            slot(Turn(0), post=False)
            with pool.Fori(0, B // 2 - 2) as i:
                slot(Turn(1, i))
                slot(Turn(2, i))
            slot(Turn(B - 3))
            slot(Turn(B - 2), stats=False)
            slot(LAST, prep=False, stats=False)
            tail_gpsimd(pool)

        @block.scalar
        def _(act):
            for n in range(FOLDS + H):
                act.wait_ge(pe_w.sem, n + 1)
                if n < FOLDS:
                    hp, kind = n // 3, n % 3
                    dst = (wqT[:, hp, :], wkT[:, hp, :], wvT[:, hp, :])[kind]
                    ins = nc.scalar.copy(dst, fold_bank(n)[:, 128:256] if kind == 0 else fold_bank(n))
                else:
                    ins = nc.scalar.activation(G[:, n - FOLDS, :], fold_bank(n), ACT.Copy, scale=DH ** -0.5)
                ins.then_inc(ev_w.sem, 1)
            def normalise(turn, tiles):
                if tiles[0] == 0:
                    act.wait_ge(rstd_ctx.sem, rstd_ctx.upto(turn))
                x_ = raw[turn.off % 2]
                for t in tiles:
                    r = rows_of(t)
                    ins = nc.scalar.activation(x_[0:r, t, :], x_[0:r, t, :], ACT.Identity, bias=smc[0:r, 2, t:t + 1],
                                               scale=smc[0:r, 1, t:t + 1])
                if tiles[-1] == TILES - 1:
                    ins.then_inc(normed.sem, 1)

            normalise(Turn(0), range(TILES))
            act.wait_ge(lat_cp.sem, 1)
            nc.scalar.copy(lT_hi[:], lT[:]).then_inc(lat_hi.sem, 1)
            act.wait_ge(sigma_rdy.sem, 1)
            for k in range(2):
                h = slice(8 * k, 8 * k + 8)
                nc.scalar.activation(G_hi[:, h].rearrange("p h c -> p (h c)"), G[:, h].rearrange("p h c -> p (h c)"),
                                     ACT.Copy, scale=sigma[:, 1:2]).then_inc(g_hi_rdy.sem, 1)

            def reciprocals_out(turn, k):
                act.wait_ge(pe_item["bc"].sem, pe_item["bc"].upto(turn, k))
                nc.scalar.copy(rb[:, k * HALF:(k + 1) * HALF], W[side_bank(("bc", k), turn)][:]).then_inc(free["bc"].sem, 1)

            def outputs_high(turn, k):
                act.wait_ge(o_normed.sem, o_normed.upto(turn, k))
                cols = slice(k * HALF, (k + 1) * HALF)
                nc.scalar.copy(o_hi[:, :, cols], o_sb[:, :, cols]).then_inc(o_hi_done.sem, 1)

            def queries_high(turn, c):
                act.wait_ge(pe_item["q"].sem, pe_item["q"].upto(turn, c))
                p = turn.off % 2
                nc.scalar.copy(q_hi[p][:, c * HALF:(c + 1) * HALF], W[BANK[("q", c)]][:]).then_inc(q_hi_done.sem, 1)

            def transposed(turn, g):
                act.wait_ge(pe_item["t"].sem, pe_item["t"].upto(turn, g))
                p, w = turn.off % 2, (512 if g < 3 else REST)
                src = W[BANK[("t", g)]][:].bitcast(F16)
                nc.scalar.copy(xT_hi[p][:, 512 * g:512 * g + w], src[:, 0:w])
                nc.scalar.copy(xT_lo[p][:, 512 * g:512 * g + w], src[:, 512:512 + w]).then_inc(free["t"].sem, 1)

            def shift_row(turn, k):
                act.wait_ge(pe_item["mt"].sem, pe_item["mt"].upto(turn, k))
                nc.scalar.copy(q_hi[turn.off % 2][0:1, k * HALF:(k + 1) * HALF], W[BANK[("mt", k)]][0:1, :])\
                  .then_inc(free["mt"].sem, 1)

            def exponentials_high(turn, u):
                r, k = rows_of(u), pbuf(turn, u)
                act.wait_ge(s_done.sem, s_done.upto(turn, u))
                if not (turn.i is None and turn.off == 0 and u < NPB):
                    act.wait_ge(pv_done.sem, pv_done.upto(turn, u - NPB))
                src = S[0:r, 2 * (u % 2):2 * (u % 2) + 2, :].rearrange("p a n -> p (a n)")
                nc.scalar.activation(p_hi[k][0:r, :], src, ACT.Exp, scale=sigma[0:r, 0:1])

            def exponentials_full(turn, u):
                r = rows_of(u)
                src = S[0:r, 2 * (u % 2):2 * (u % 2) + 2, :].rearrange("p a n -> p (a n)")
                nc.scalar.activation(src, src, ACT.Exp, scale=sigma[0:r, 0:1]).then_inc(e_done.sem, 1)

            def outputs(turn):
                act.wait_ge(pv_done.sem, pv_done.upto(turn, TILES - 1))
                nc.scalar.copy(o_sb[:, 0, :], OA[:].rearrange("p a n -> p (a n)")).then_inc(oa_free.sem, 1)

            def latent_outputs(turn):
                act.wait_ge(pv_done.sem, pv_done.upto(turn, LAT))
                for k in range(2):
                    nc.scalar.copy(o_sb[:, 1, k * HALF:(k + 1) * HALF], W[BANK[("ol", k)]][:])\
                      .then_inc(free["ol"].sem, 1)

            def projected(turn):
                act.wait_ge(pe_item["pj"].sem, pe_item["pj"].upto(turn))
                dst = attnT[:, 64 * turn.off:64 * turn.off + 64] if turn.i is None \
                    else attnT[:, bass.ds(turn.times(64), 64)]
                nc.scalar.activation(dst, W[side_bank(("pj", 0), turn)][:, 0:NQ], ACT.Copy, scale=wscale[:, 1:2])\
                  .then_inc(free["pj"].sem, 1)

            def side_item(item, nxt, old, prep, post):
                kind, k = item
                if kind == "q" and prep:
                    queries_high(nxt, k)
                if kind == "t" and prep:
                    transposed(nxt, k)
                if kind == "mt" and prep:
                    shift_row(nxt, k)
                if kind == "bc" and post:
                    reciprocals_out(old, k)
                if kind == "pj" and post:
                    projected(old)

            def slot(b, prep=True, post=True, stats=True):
                nxt, old = b.plus(1), b.plus(-1)
                for u in range(UNITS):
                    early, late = PLAN[u]
                    exponentials_high(b, u)
                    if u < UNITS - 1:
                        for item in early:
                            side_item(item, nxt, old, prep, post)
                    exponentials_full(b, u)
                    if u == 0 and post:
                        outputs(old)
                    if u == LATENTS_AT and post:
                        latent_outputs(old)
                    if u in OUTPUTS_HIGH_AT and post:
                        outputs_high(old, OUTPUTS_HIGH_AT[u])
                    for item in (late if u < UNITS - 1 else early + late):
                        side_item(item, nxt, old, prep, post)
                    if b is LAST and u == H_AT:
                        early_columns_out(act)
                    if stats and u in NORMALISE_AT:
                        normalise(b.plus(2), NORMALISE_AT[u])

            for early, late in PLAN:
                for item in early + late:
                    side_item(item, Turn(0), None, True, False)
                    if item[0] == "m" and item[1] in WO_AFTER:
                        h = WO_AFTER[item[1]]
                        if h == 0:
                            act.wait_ge(wscale_rdy.sem, 1)
                        act.wait_ge(pe_w.sem, FOLDS + H + h + 1)
                        nc.scalar.activation(WO_hi[:, h, :], wo_banks[h % 4], ACT.Copy, scale=wscale[:, 0:1])\
                          .then_inc(ev_w.sem, 1)
                    if item[0] == "m" and item[1] in SMALL_AFTER:
                        small_weights_scalar(act, SMALL_AFTER[item[1]])
                    if item == ("m", MAXIMA // 2):
                        normalise(Turn(1), range(TILES))
            slot(Turn(0), post=False)
            with act.Fori(0, B // 2 - 2) as i:
                slot(Turn(1, i))
                slot(Turn(2, i))
            slot(Turn(B - 3))
            slot(Turn(B - 2), stats=False)
            slot(LAST, prep=False, stats=False)
            outputs(Turn(B - 1))
            latent_outputs(Turn(B - 1))
            tail_scalar(act, reciprocals_out, outputs_high, projected)

        @block.tensor
        def _(pe):
            mm = nc.tensor.matmul
            pe.wait_ge(folded.sem, 1)
            pe.wait_ge(ld_w.sem, 48)
            for n in range(FOLDS):
                hp, kind = n // 3, n % 3
                if n >= 4:
                    pe.wait_ge(ev_w.sem, n - 3)
                w = (wq_sb[:, 128 * hp:128 * hp + 128], wkv_sb[:, 128 * hp:128 * hp + 128],
                     wkv_sb[:, H * DH + 128 * hp:H * DH + 128 * hp + 128])[kind]
                mm(fold_bank(n), w, fold[:].rearrange("p k d -> p (k d)"), start=True, stop=True)\
                    .then_inc(pe_w.sem, 1)
            for n in range(FOLDS, FOLDS + H):
                h = n - FOLDS
                pe.wait_ge(ev_w.sem, max(n - 3, FOLDS))
                r = slice(64 * (h % 2), 64 * (h % 2) + 64)
                mm(fold_bank(n), wqT[r, h // 2, :], wkT[r, h // 2, :], start=True, stop=True).then_inc(pe_w.sem, 1)
            pe.wait_ge(lat_rdy.sem, 1)
            for b in range(B):
                ins = nc.tensor.transpose(S[:, b // 8, 64 * (b % 8):64 * (b % 8) + 64], lx[:, b, :], ident[0:NQ, 0:NQ])
            ins.then_inc(lat_t.sem, 1)
            pe.wait_ge(ev_w.sem, FOLDS + H)
            pe.wait_ge(g_rdy.sem, 2)
            pe.wait_ge(consts.sem, 2)

            def output_map(h):
                if h >= 4:
                    pe.wait_ge(wo_lo_done.sem, h - 3)
                r = slice(64 * (h % 2), 64 * (h % 2) + 64)
                for c in (0, 128):
                    ins = mm(wo_banks[h % 4][:, c:c + 128], wvT[r, h // 2, c:c + 128], wo_sb[r, h // 2, :],
                             start=True, stop=True)
                ins.then_inc(pe_w.sem, 1)

            last_user = {}

            def bank_free(item, turn):
                bank = side_bank(item, turn)
                if bank in last_user:
                    (kind, k), t = last_user[bank]
                    pe.wait_ge(free[kind].sem, free[kind].upto(t, k))
                last_user[bank] = (item, turn)

            def side_item(item, turn):
                kind, k = item
                w, p = W[side_bank(item, turn)], turn.off % 2
                bank_free(item, turn)
                if kind == "q":
                    if k == 0:
                        pe.wait_ge(curT.sem, curT.upto(turn))
                    for j in range(8):
                        h, c, dst = 8 * (k % 2) + j, 128 * (k // 2), w[:, 64 * j:64 * j + 64]
                        mm(dst, G_hi[:, h, c:c + 128], cT_hi[p][:], start=True, stop=False)
                        mm(dst, G_hi[:, h, c:c + 128], cT_lo[p][:], start=False, stop=False)
                        ins = mm(dst, G_lo[:, h, c:c + 128], cT_hi[p][:], start=False, stop=True)
                if kind == "t":
                    pe.wait_ge(split.sem, split.upto(turn, k))
                    w16 = w[:].bitcast(F16)
                    for t in (range(4 * k, 4 * k + 4) if k < 3 else [FULL]):
                        r = rows_of(t)
                        for x_, o in ((xk_hi, 0), (xk_lo, 512)):
                            c = o + 128 * (t - 4 * k)
                            ins = nc.tensor.transpose(w16[:, c:c + r], x_[p][0:r, t, :], ident16[0:r, 0:r])
                if kind == "m":
                    r, c = M_ORDER[k]
                    if k == 0:
                        pe.wait_ge(q_hi_done.sem, q_hi_done.upto(turn, 3))
                    if M_ORDER[k] in ((0, 0), (0, 1), (0, 2), (0, 3)):
                        pe.wait_ge(free["t"].sem, free["t"].upto(turn, c))
                    rows = q_hi[p][:, 128 * r:128 * r + 128]
                    if c < 3:
                        ins = mm(w[:], rows, xT_hi[p][:, 512 * c:512 * c + 512], start=True, stop=True)
                    else:
                        mm(w[:, 0:REST], rows, xT_hi[p][:, 1536:1536 + REST], start=True, stop=True)
                        ins = mm(w[:, REST:REST + NQ], q_hi[p][:, COLS + 128 * r:COLS + 128 * r + 128], cT_hi[p][:],
                                 start=True, stop=True)
                if kind == "mt":
                    pe.wait_ge(m16_done.sem, m16_done.upto(turn))
                    for j in range(4):
                        ins = mm(w[0:1, 128 * j:128 * j + 128], m16[:, 4 * k + j:4 * k + j + 1], ident16[:],
                                 start=True, stop=True)
                if kind == "sr":
                    pe.wait_ge(srow_done.sem, srow_done.upto(turn))
                    for j in range(8):
                        ins = mm(w[:, j:j + 1], srow[:, 128 * j:128 * j + 128], oscale[:], start=True, stop=True)
                if kind == "bc":
                    pe.wait_ge(diag_done.sem, diag_done.upto(turn, k))
                    ins = mm(w[:], ones[:], diag[:, k].rearrange("p j n -> p (j n)"), start=True, stop=True)
                if kind == "pj":
                    pe.wait_ge(o_split.sem, o_split.upto(turn, 1))
                    for n in range(2 * H):
                        h, c = n // 2, n % 2
                        whi, wlo = (t_[:, h, 128 * c:128 * c + 128] for t_ in (WO_hi, WO_lo))
                        ohi, olo = (t_[:, c, 64 * h:64 * h + 64] for t_ in (o_hi, o_lo))
                        mm(w[:, 0:NQ], whi, ohi, start=n == 0, stop=False)
                        mm(w[:, 0:NQ], whi, olo, start=False, stop=False)
                        ins = mm(w[:, 0:NQ], wlo, ohi, start=False, stop=n == 2 * H - 1)
                ins.then_inc(pe_item[kind].sem, 1)

            def scores(turn, u):
                p, r = turn.off % 2, rows_of(u)
                if not (turn.i is None and turn.off == 0 and u < 2):
                    pe.wait_ge(lo_done.sem, lo_done.upto(turn, u - 2))
                if u == 0:
                    pe.wait_ge(free["mt"].sem, free["mt"].upto(turn, 1))
                    pe.wait_ge(free["q"].sem, free["q"].upto(turn, 3))
                if u < LAT:
                    hi, lo, qc = xT_hi[p][:, 128 * u:128 * u + r], xT_lo[p][:, 128 * u:128 * u + r], 0
                else:
                    hi, lo, qc = cT_hi[p][:], cT_lo[p][:], COLS
                cols = [slice(qc + HALF * k, qc + HALF * k + HALF) for k in range(2)]
                for k in range(2):
                    mm(score_bank(u, k)[0:r], hi, q_hi[p][:, cols[k]], start=True, stop=False)
                for k in range(2):
                    mm(score_bank(u, k)[0:r], hi, q_lo[p][:, cols[k]], start=False, stop=False)
                if u == LAT:
                    for k in range(2):
                        mm(score_bank(u, k)[0:r], ones16[:], q_hi[p][0:1, HALF * k:HALF * k + HALF],
                           start=False, stop=False)
                for k in range(2):
                    ins = mm(score_bank(u, k)[0:r], lo, q_hi[p][:, cols[k]], start=False, stop=True)
                ins.then_inc(s_done.sem, 1)

            def weigh(turn, u):
                p, r, kb = turn.off % 2, rows_of(u), pbuf(turn, u)
                pe.wait_ge(lo_done.sem, lo_done.upto(turn, u))
                if u == 0 and not (turn.i is None and turn.off == 0):
                    pe.wait_ge(oa_free.sem, oa_free.upto(turn.plus(-1)))
                if u < LAT:
                    hi, lo, first, last = xk_hi[p][0:r, u, :], xk_lo[p][0:r, u, :], u == 0, u == TILES - 1
                    dst = [OA[:, k, :] for k in range(2)]
                else:
                    pe.wait_ge(curk.sem, curk.upto(turn))
                    hi, lo, first, last = ck_hi[p][:], ck_lo[p][:], True, True
                    for k in range(2):
                        bank_free(("ol", k), turn)
                    dst = [W[BANK[("ol", k)]][:] for k in range(2)]
                ph, pl = p_hi[kb], p_lo[kb]
                cols = [slice(HALF * k, HALF * k + HALF) for k in range(2)]
                for k in range(2):
                    mm(dst[k], hi, ph[0:r, cols[k]], start=first, stop=False)
                for k in range(2):
                    mm(dst[k], hi, pl[0:r, cols[k]], start=False, stop=False)
                for k in range(2):
                    ins = mm(dst[k], lo, ph[0:r, cols[k]], start=False, stop=last)
                ins.then_inc(pv_done.sem, 1)

            def slot(b, prep=True, post=True):
                nxt, old = b.plus(1), b.plus(-1)
                last_user.clear()
                for k in range(2):
                    last_user[BANK[("mt", k)]] = (("mt", k), b)
                def side_items(items):
                    for item in items:
                        if item[0] in PREP and prep:
                            side_item(item, nxt)
                        if item[0] not in PREP and post:
                            side_item(item, old)

                for u in range(UNITS):
                    scores(b, u)
                    side_items(PLAN[u][0])
                    if u >= 2:
                        weigh(b, u - 2)
                    elif post and u == 0:
                        weigh(old, TILES - 1)
                    elif post and u == LATENTS_AT:
                        weigh(old, LAT)
                    side_items(PLAN[u][1])
                    if b is LAST and u == X1_AT:
                        pe.wait_ge(free["bc"].sem, free["bc"].upto(old, 1))
                        pe.wait_ge(free["pj"].sem, free["pj"].upto(Turn(2 * EARLY - 1)))
                        early_x1(pe)
                    if b is LAST and u == H_AT:
                        early_columns(pe)
                        pe.wait_ge(ta["hcopy"].sem, 1)

            for early, late in PLAN:
                for item in early + late:
                    if item[0] in PREP:
                        side_item(item, Turn(0))
                    if item[0] == "m" and item[1] in WO_AFTER:
                        output_map(WO_AFTER[item[1]])
                    if item[0] == "m" and item[1] in SMALL_AFTER:
                        small_weights_tensor(pe, SMALL_AFTER[item[1]])
            pe.wait_ge(wo_lo_done.sem, H)
            pe.wait_ge(wt_c.sem, 5)
            slot(Turn(0), post=False)
            with pe.Fori(0, B // 2 - 2) as i:
                slot(Turn(1, i))
                slot(Turn(2, i))
            slot(Turn(B - 3))
            slot(Turn(B - 2))
            slot(LAST, prep=False)
            weigh(Turn(B - 1), TILES - 1)
            weigh(Turn(B - 1), LAT)
            tail_tensor(pe, side_item)


_INS = ['x', 'ctx_1024', 'L0_xattn_ln1_g', 'L0_xattn_ln1_b', 'L0_xattn_ln2_g', 'L0_xattn_ln2_b', 'L0_xattn_Wq',
        'L0_xattn_Wkv', 'L0_xattn_Wo', 'L0_attn_Wq', 'L0_attn_Wk', 'L0_attn_Wv', 'L0_attn_Wo', 'L0_attn_lq1',
        'L0_attn_lk1', 'L0_attn_lq2', 'L0_attn_lk2', 'L0_attn_rms_scale', 'L0_ffn_gate_w', 'L0_ffn_gate_b',
        'L0_ffn_expert_w', 'L0_ffn_expert_b']


def kernel(**inputs):
    import numpy as np
    import concourse.bacc as bacc
    from concourse.bass_utils import run_bass_kernel_spmd

    nc = bacc.Bacc("TRN2", target_bir_lowering=False, num_devices=1)
    arrays, args = {}, []
    for name in _INS:
        a = np.ascontiguousarray(inputs[name])
        arrays[name] = a
        args.append(nc.dram_tensor(name, a.shape, mybir.dt.from_np(a.dtype), kind="ExternalInput").ap())
    args.append(nc.dram_tensor("out", (B, NQ, D), F32, kind="ExternalOutput").ap())
    perceiver(nc, *args)
    return run_bass_kernel_spmd(nc, [arrays], core_ids=[0]).results[0]["out"]
```
